# Optimizing a Trainium2 kernel written in Bass

```python
import numpy as np
import jax
import jax.numpy as jnp

def _softmax(x, axis=-1):
    return jax.nn.softmax(x, axis=axis)

def _gelu(x):
    return jax.nn.gelu(x, approximate=True)

def _silu(x):
    return jax.nn.silu(x)

def _sigmoid(x):
    return jax.nn.sigmoid(x)

def _layernorm(x, axis=-1, eps=1e-05):
    m = jnp.mean(x, axis=axis, keepdims=True)
    v = jnp.var(x, axis=axis, keepdims=True)
    return (x - m) / jnp.sqrt(v + eps)

def _scatter_add(tgt, idx, src, axis=0):
    return tgt.at[idx].add(src)

def _segment_sum(src, seg, n):
    return jax.ops.segment_sum(src, seg, n)
kernel_name = 'mk_xattn_ffn_d2_seqx_r4_dac6b2'

def setup_inputs(seed: int=0):
    np.random.seed(seed)
    _w = jnp.asarray

    def _rec_inputs():
        import jax
        import jax.numpy as jnp
        _rk = jax.random.key(seed)
        x = -0.0005207 + 1.001 * jax.random.normal(jax.random.fold_in(_rk, 1), (16, 100, 256), jnp.float32)
        _lenS = 100 - jax.random.randint(jax.random.fold_in(_rk, 7), (16,), 0, max(1, 100 // 4) + 1, jnp.int32)
        _lenS2 = 361 - jax.random.randint(jax.random.fold_in(_rk, 8), (16,), 0, max(1, 361 // 4) + 1, jnp.int32)
        _ctx_1024P = jax.random.normal(jax.random.fold_in(_rk, 11), (16, 16, 256), jnp.float32)
        _ctx_1024c = jax.random.dirichlet(jax.random.fold_in(_rk, 511), 0.3 * jnp.ones((16,), jnp.float32), (16, 361))
        _ctx_1024t = jnp.einsum('bsk,bkd->bsd', _ctx_1024c, _ctx_1024P)
        _ctx_1024t = _ctx_1024t * jax.lax.rsqrt(jnp.mean(jnp.square(_ctx_1024t)) + 1e-12) * 0.953939
        ctx_1024 = -5.72187e-05 + 0.999849 * (_ctx_1024t + 0.3 * jax.random.normal(jax.random.fold_in(_rk, 611), (16, 361, 256), jnp.float32))
        _validS = jnp.arange(100)[None, :] < _lenS[:, None]
        _validS2 = jnp.arange(361)[None, :] < _lenS2[:, None]
        _causal = jnp.tril(jnp.ones((100, 100), dtype=bool))
        mask_BxS_ff1 = jnp.where(jnp.ones((16, 100), dtype=bool), 1.0, 0.0).astype(jnp.float32)
        mask_BxS2_ik0 = jnp.where(jnp.broadcast_to(_validS2[:, :], (16, 361)), 0, 1).astype(jnp.int32)
        return (x, ctx_1024, mask_BxS_ff1, mask_BxS2_ik0)
    x, ctx_1024, mask_BxS_ff1, mask_BxS2_ik0 = _rec_inputs()

    def _L0_xattn_setup():
        import jax, jax.numpy as jnp
        import numpy as np
        key = jax.random.key(seed)
        ks = jax.random.split(key, 5)
        b, n_q, n_kv = (16, 128, 1024)
        query_dim, context_dim, heads, dim_head = (256, 256, 16, 64)
        inner = heads * dim_head
        x = jax.random.normal(ks[0], (b, n_q, query_dim), dtype=jnp.float32)
        context = jax.random.normal(ks[1], (b, n_kv, context_dim), dtype=jnp.float32)
        Wq = jax.random.normal(ks[2], (query_dim, inner), dtype=jnp.float32) * query_dim ** (-0.5)
        Wkv = jax.random.normal(ks[3], (context_dim, 2 * inner), dtype=jnp.float32) * context_dim ** (-0.5)
        Wout = jax.random.normal(ks[4], (inner, query_dim), dtype=jnp.float32) * inner ** (-0.5)
        bout = jnp.zeros((query_dim,), dtype=jnp.float32)
        return {'x': x, 'context': context, 'Wq': Wq, 'Wkv': Wkv, 'Wout': Wout, 'bout': bout}
    _L0_xattn_all = _L0_xattn_setup()
    _L0_xattn_in = {k: v for k, v in _L0_xattn_all.items() if k in ('Wq', 'Wkv', 'Wout', 'bout')}
    del _L0_xattn_all

    def _L0_ffn_setup():
        import jax, jax.numpy as jnp
        import numpy as np
        TOP_K = 2
        ROUTE_SCALE = 1.0
        EPS = 1e-20
        B, S, D = (2, 128, 256)
        E = 8
        F = 192
        FS = 192 * 1
        key = jax.random.key(seed)
        ks = jax.random.split(key, 9)
        s = 0.02
        return {'hidden_states': jax.random.normal(ks[0], (B, S, D), dtype=jnp.float32), 'W_gate_router': jax.random.normal(ks[1], (D, E), dtype=jnp.float32) * s, 'expert_bias': jnp.zeros((E,), dtype=jnp.float32), 'Wg': jax.random.normal(ks[2], (E, D, F), dtype=jnp.float32) * s, 'Wu': jax.random.normal(ks[3], (E, D, F), dtype=jnp.float32) * s, 'Wd': jax.random.normal(ks[4], (E, F, D), dtype=jnp.float32) * s, 'Wg_s': jax.random.normal(ks[5], (D, FS), dtype=jnp.float32) * s, 'Wu_s': jax.random.normal(ks[6], (D, FS), dtype=jnp.float32) * s, 'Wd_s': jax.random.normal(ks[7], (FS, D), dtype=jnp.float32) * s}
    _L0_ffn_all = _L0_ffn_setup()
    _L0_ffn_in = {k: v for k, v in _L0_ffn_all.items() if k in ('W_gate_router', 'expert_bias', 'Wg', 'Wu', 'Wd', 'Wg_s', 'Wu_s', 'Wd_s')}
    del _L0_ffn_all

    def _L1_xattn_setup():
        import jax, jax.numpy as jnp
        import numpy as np
        B, F, T, D = (8, 64, 32, 256)
        NEG = -1e+30
        key = jax.random.key(seed)
        ks = jax.random.split(key, 10)
        s = 1.0 / np.sqrt(D)
        return {'features': jax.random.normal(ks[0], (B, F, D), jnp.float32), 'masks': jnp.ones((B, F), jnp.float32), 'textual_features': jax.random.normal(ks[1], (B, T, D), jnp.float32), 'q_masks': jax.random.randint(ks[2], (B, T), 0, 2, jnp.int32), 'Ws': jax.random.normal(ks[3], (D, D), jnp.float32) * s, 'W': jax.random.normal(ks[4], (D, D), jnp.float32) * s, 'w': jax.random.normal(ks[5], (D, 1), jnp.float32) * s, 'b': jax.random.normal(ks[6], (1, D), jnp.float32) * s, 'Wcw': jax.random.normal(ks[7], (1, D), jnp.float32) * s, 'bcw': jnp.zeros((1,), jnp.float32), 'Wcb': jax.random.normal(ks[8], (1, D), jnp.float32) * s, 'bcb': jnp.zeros((1,), jnp.float32)}
    _L1_xattn_all = _L1_xattn_setup()
    _L1_xattn_in = {k: v for k, v in _L1_xattn_all.items() if k in ('Ws', 'W', 'w', 'b', 'Wcw', 'bcw', 'Wcb', 'bcb')}
    del _L1_xattn_all

    def _L1_ffn_setup():
        import jax, jax.numpy as jnp
        import numpy as np
        HIDDEN = 256
        INNER = 1024

        def _weight_quant(w):
            scale = 1.0 / jnp.clip(jnp.mean(jnp.abs(w)), 1e-05)
            wq = jnp.clip(jnp.round(w * scale), -1.0, 1.0) / scale
            return w + jax.lax.stop_gradient(wq - w)

        def _act_quant(x):
            scale = 127.0 / jnp.clip(jnp.max(jnp.abs(x), axis=-1, keepdims=True), 1e-05)
            xq = jnp.clip(jnp.round(x * scale), -128.0, 127.0) / scale
            return x + jax.lax.stop_gradient(xq - x)

        def _bitlinear(x, w):
            return jnp.einsum('bsi,oi->bso', _act_quant(x), _weight_quant(w))
        key = jax.random.key(seed)
        k0, k1, k2, k3 = jax.random.split(key, 4)
        x = jax.random.normal(k0, (4, 512, HIDDEN), dtype=jnp.float32)
        w_gate = jax.random.normal(k1, (INNER, HIDDEN), dtype=jnp.float32) / np.sqrt(HIDDEN)
        w_up = jax.random.normal(k2, (INNER, HIDDEN), dtype=jnp.float32) / np.sqrt(HIDDEN)
        w_down = jax.random.normal(k3, (HIDDEN, INNER), dtype=jnp.float32) / np.sqrt(INNER)
        return {'x': x, 'w_gate': w_gate, 'w_up': w_up, 'w_down': w_down}
    _L1_ffn_all = _L1_ffn_setup()
    _L1_ffn_in = {k: v for k, v in _L1_ffn_all.items() if k in ('w_gate', 'w_up', 'w_down')}
    del _L1_ffn_all
    return {'x': x, 'ctx_1024': ctx_1024, 'mask_BxS_ff1': mask_BxS_ff1, 'mask_BxS2_ik0': mask_BxS2_ik0, 'L0_xattn_Wq': _L0_xattn_in['Wq'], 'L0_xattn_Wkv': _L0_xattn_in['Wkv'], 'L0_xattn_Wout': _L0_xattn_in['Wout'], 'L0_xattn_bout': _L0_xattn_in['bout'], 'L0_ffn_W_gate_router': _L0_ffn_in['W_gate_router'], 'L0_ffn_expert_bias': _L0_ffn_in['expert_bias'], 'L0_ffn_Wg': _L0_ffn_in['Wg'], 'L0_ffn_Wu': _L0_ffn_in['Wu'], 'L0_ffn_Wd': _L0_ffn_in['Wd'], 'L0_ffn_Wg_s': _L0_ffn_in['Wg_s'], 'L0_ffn_Wu_s': _L0_ffn_in['Wu_s'], 'L0_ffn_Wd_s': _L0_ffn_in['Wd_s'], 'L1_xattn_Ws': _L1_xattn_in['Ws'], 'L1_xattn_W': _L1_xattn_in['W'], 'L1_xattn_w': _L1_xattn_in['w'], 'L1_xattn_b': _L1_xattn_in['b'], 'L1_xattn_Wcw': _L1_xattn_in['Wcw'], 'L1_xattn_bcw': _L1_xattn_in['bcw'], 'L1_xattn_Wcb': _L1_xattn_in['Wcb'], 'L1_xattn_bcb': _L1_xattn_in['bcb'], 'L1_ffn_w_gate': _L1_ffn_in['w_gate'], 'L1_ffn_w_up': _L1_ffn_in['w_up'], 'L1_ffn_w_down': _L1_ffn_in['w_down']}

def reference(x, ctx_1024, mask_BxS_ff1, mask_BxS2_ik0, L0_xattn_Wq, L0_xattn_Wkv, L0_xattn_Wout, L0_xattn_bout, L0_ffn_W_gate_router, L0_ffn_expert_bias, L0_ffn_Wg, L0_ffn_Wu, L0_ffn_Wd, L0_ffn_Wg_s, L0_ffn_Wu_s, L0_ffn_Wd_s, L1_xattn_Ws, L1_xattn_W, L1_xattn_w, L1_xattn_b, L1_xattn_Wcw, L1_xattn_bcw, L1_xattn_Wcb, L1_xattn_bcb, L1_ffn_w_gate, L1_ffn_w_up, L1_ffn_w_down):
    import jax
    import jax.numpy as jnp

    def _L0_xattn_ref(x, context, Wq, Wkv, Wout, bout):
        import jax, jax.numpy as jnp
        import numpy as np
        heads, dim_head = (16, 64)
        b, n_q, _ = x.shape
        n_kv = context.shape[1]
        scale = dim_head ** (-0.5)
        q = x @ Wq
        kv = context @ Wkv
        k, v = jnp.split(kv, 2, axis=-1)

        def split_heads(t):
            bb, n, _ = t.shape
            return t.reshape(bb, n, heads, dim_head).transpose(0, 2, 1, 3)
        q, k, v = map(split_heads, (q, k, v))
        i_idx = jnp.arange(n_q)[:, None]
        j_idx = jnp.arange(n_kv)[None, :]
        mask = j_idx % n_q == i_idx
        sim = jnp.einsum('bhid,bhjd->bhij', q, k) * scale
        max_neg = -jnp.finfo(sim.dtype).max
        sim = jnp.where(mask[None, None, :, :], sim, max_neg)
        attn = jax.nn.softmax(sim, axis=-1)
        out = jnp.einsum('bhij,bhjd->bhid', attn, v)
        out = out.transpose(0, 2, 1, 3).reshape(b, n_q, heads * dim_head)
        return out @ Wout + bout

    def _L0_ffn_ref(hidden_states, W_gate_router, expert_bias, Wg, Wu, Wd, Wg_s, Wu_s, Wd_s):
        import jax, jax.numpy as jnp
        import numpy as np
        TOP_K = 2
        ROUTE_SCALE = 1.0
        EPS = 1e-20
        B, S, D = (2, 128, 256)
        E = 8
        F = 192
        FS = 192 * 1
        b, s, d = hidden_states.shape
        x = hidden_states.reshape(-1, d)
        T = x.shape[0]
        logits = x @ W_gate_router
        scores = jax.nn.sigmoid(logits.astype(jnp.float32))
        _, sel = jax.lax.top_k(scores + expert_bias, TOP_K)
        top_scores = jnp.take_along_axis(scores, sel, axis=1)
        top_scores = top_scores / (top_scores.sum(-1, keepdims=True) + EPS)
        top_scores = top_scores * ROUTE_SCALE
        shared = jax.nn.silu(x @ Wg_s) * (x @ Wu_s) @ Wd_s
        tok = jnp.repeat(jnp.arange(T), TOP_K)
        exp = sel.reshape(-1)
        w = top_scores.reshape(-1)
        xr = x[tok]
        h = jax.nn.silu(jnp.einsum('nd,edf->enf', xr, Wg)) * jnp.einsum('nd,edf->enf', xr, Wu)
        out_all = jnp.einsum('enf,efd->end', h, Wd)
        routed = out_all[exp, jnp.arange(exp.shape[0])]
        routed = (routed.astype(jnp.float32) * w[:, None]).astype(hidden_states.dtype)
        out = shared.at[tok].add(routed)
        return out.reshape(b, s, d)

    def _L1_xattn_ref(features, masks, textual_features, q_masks, Ws, W, w, b, Wcw, bcw, Wcb, bcb):
        import jax, jax.numpy as jnp
        import numpy as np
        B, F, T, D = (8, 64, 32, 256)
        NEG = -1e+30
        txt_proj = jnp.einsum('btd,de->bte', textual_features, Ws)
        feat_proj = jnp.einsum('bfd,de->bfe', features, W)
        h = jnp.tanh(txt_proj[:, None, :, :] + feat_proj[:, :, None, :] + b[None, None, :, :][..., 0, :])
        rho = jnp.einsum('bftd,d->bft', h, w[:, 0])
        qm = q_masks.astype(jnp.float32)
        rho = rho + (1.0 - qm)[:, None, :] * NEG
        att = jax.nn.softmax(rho, axis=-1)
        txt_h = jnp.einsum('bft,btd->bfd', att, textual_features)
        w_s = jnp.tanh(jnp.einsum('bfd,od->bfo', txt_h, Wcw) + bcw)
        b_s = jnp.tanh(jnp.einsum('bfd,od->bfo', txt_h, Wcb) + bcb)
        return w_s * features + b_s

    def _L1_ffn_ref(x, w_gate, w_up, w_down):
        import jax, jax.numpy as jnp
        import numpy as np
        HIDDEN = 256
        INNER = 1024

        def _weight_quant(w):
            scale = 1.0 / jnp.clip(jnp.mean(jnp.abs(w)), 1e-05)
            wq = jnp.clip(jnp.round(w * scale), -1.0, 1.0) / scale
            return w + jax.lax.stop_gradient(wq - w)

        def _act_quant(x):
            scale = 127.0 / jnp.clip(jnp.max(jnp.abs(x), axis=-1, keepdims=True), 1e-05)
            xq = jnp.clip(jnp.round(x * scale), -128.0, 127.0) / scale
            return x + jax.lax.stop_gradient(xq - x)

        def _bitlinear(x, w):
            return jnp.einsum('bsi,oi->bso', _act_quant(x), _weight_quant(w))
        gate = jax.nn.silu(_bitlinear(x, w_gate))
        up = _bitlinear(x, w_up)
        return _bitlinear(gate * up, w_down)
    x = x + _L0_xattn_ref(_layernorm(x, axis=-1), ctx_1024, L0_xattn_Wq, L0_xattn_Wkv, L0_xattn_Wout, L0_xattn_bout)
    x = x + _L0_ffn_ref(_layernorm(x, axis=-1), L0_ffn_W_gate_router, L0_ffn_expert_bias, L0_ffn_Wg, L0_ffn_Wu, L0_ffn_Wd, L0_ffn_Wg_s, L0_ffn_Wu_s, L0_ffn_Wd_s)
    x = x + _L1_xattn_ref(_layernorm(x, axis=-1), mask_BxS_ff1, ctx_1024, mask_BxS2_ik0, L1_xattn_Ws, L1_xattn_W, L1_xattn_w, L1_xattn_b, L1_xattn_Wcw, L1_xattn_bcw, L1_xattn_Wcb, L1_xattn_bcb)
    x = x + _L1_ffn_ref(_layernorm(x, axis=-1), L1_ffn_w_gate, L1_ffn_w_up, L1_ffn_w_down)
    return x

_drawn_inputs = setup_inputs


def setup_inputs(seed=0):
    import zlib

    import numpy as np

    out = dict(_drawn_inputs(seed))
    spreads = {'L0_xattn_bout': (0.0, 0.1), 'L0_ffn_expert_bias': (0.0, 0.8)}
    factors = {'L0_ffn_W_gate_router': 8.0,
     'L0_ffn_Wg': 6.814,
     'L0_ffn_Wu': 6.761,
     'L0_ffn_Wd': 6.766,
     'L0_ffn_Wg_s': 5.049,
     'L0_ffn_Wu_s': 4.973,
     'L0_ffn_Wd_s': 4.98,
     'L1_xattn_b': 8.0}
    for name, (base, spread) in spreads.items():
        noise = np.random.default_rng([zlib.crc32(name.encode()), seed]).standard_normal(out[name].shape)
        drawn = base * np.exp(spread * noise) if base else spread * noise
        out[name] = jnp.asarray(drawn.astype(out[name].dtype))
    for name, factor in factors.items():
        out[name] = (out[name] * factor).astype(out[name].dtype)
    return out
```

```python
import concourse.bass as bass
from concourse import mybir
from contextlib import ExitStack


def bass_xattn_moe_additive_attn_bitlinear_ffn_kernel(
    nc, x_in, ctx_t, mask_in, wq_in, wkv_in, wout_in, bout_in, wr_in, ebias_in,
    wg_in, wu_in, wd_in, ws_in, w_in, wvec_in, b_in, wcw_in, bcw_in, wcb_in, bcb_in,
    fg_in, fu_in, fd_in, out,
):
    fp32 = mybir.dt.float32
    bf16 = mybir.dt.bfloat16
    i32 = mybir.dt.int32
    ALU = mybir.AluOpType
    ACT = mybir.ActivationFunctionType
    AX = mybir.AxisListType
    ds = bass.ds

    B, S, D = x_in.shape
    C = ctx_t.shape[2]
    P = 128
    KD = D // P
    INNER = wq_in.shape[1]
    DH = 64
    H = INNER // DH
    HC = INNER // P
    NJ = (C + S - 1) // S
    JR = [min(S, C - j * S) for j in range(NJ)]
    JF = C // S
    E = wr_in.shape[1]
    F = wg_in.shape[1] // (E + 1)
    FT = F * (E + 1)
    FC = (FT + P - 1) // P
    TB = 4
    N4 = TB * S
    NT = B // TB
    G = 512
    FI = fg_in.shape[1]
    FIC = FI // P
    HALF = 8
    UNIT = 2 * HALF
    NU = (C + UNIT - 1) // UNIT
    CP = NU * UNIT
    NEG = -1e30
    ROUND = 12582912.0
    EPS = 1e-5
    NP = B // 2

    ctx = ExitStack()
    with ctx:
        def sb(name, shape, dt=fp32):
            return ctx.enter_context(nc.sbuf_tensor(name, shape, dt))

        def sem(name):
            return ctx.enter_context(nc.semaphore(name))

        x = sb("x", [S, B, D])
        lnT = sb("lnT", [P, KD, B * S])
        ident = sb("ident", [P, P])
        ident16 = sb("ident16", [P, P], bf16)
        ones = sb("ones", [P, P])
        headsel = sb("headsel", [P, 2])
        half = sb("half", [S, B])
        stats = sb("stats", [S, B, 6])
        meanvar = sb("meanvar", [S, B, 2])
        vareps = sb("vareps", [S, B])
        rstd = sb("rstd", [S, B])
        lnN = sb("lnN", [S, 2, D])
        ctxb = sb("ctxb", [P, 2, KD, C])
        att_w = sb("att_w", [P, 6144])
        wq = att_w[:, 0:2048].rearrange("p (k n) -> p k n", k=KD)
        wkv = att_w[:, 2048:6144].rearrange("p (k n) -> p k n", k=KD)
        fw = [att_w[:, 2048 * m:2048 * (m + 1)] for m in range(3)]
        wout = sb("wout", [P, HC, D])
        bout = sb("bout", [S, D])
        big = sb("big", [P, 12800])
        qT = big[:, :].rearrange("p (c n) -> p c n", c=HC)
        wg = big[:, 0:KD * FT].rearrange("p (k n) -> p k n", k=KD)
        wu = big[:, KD * FT:2 * KD * FT].rearrange("p (k n) -> p k n", k=KD)
        wd = big[:, 2 * KD * FT:2 * KD * FT + FC * D].rearrange("p (c n) -> p c n", c=FC)
        zt = [big[:, 1600 * m:1600 * (m + 1)].rearrange("p (k t f) -> p k t f", k=KD, t=HALF) for m in range(2)]
        ht = [big[:, 3200 + 1600 * m:3200 + 1600 * (m + 1)].rearrange("p (k t f) -> p k t f", k=KD, t=HALF) for m in range(2)]
        txtT = [big[:, 6400 + KD * CP * m:6400 + KD * CP * (m + 1)].rearrange("p (k t) -> p k t", k=KD) for m in range(2)]
        o = 6400 + 2 * KD * CP
        cwb = [big[0:S, o + 2 * C * m:o + 2 * C * (m + 1)].rearrange("p (w t) -> p w t", w=2) for m in range(2)]
        o += 4 * C
        assert o <= 12800
        work = sb("work", [P, FC * N4])
        hT = work[:, :].rearrange("p (c n) -> p c n", c=FC)
        prod = [work[:, 2 * C * m:2 * C * (m + 1)].rearrange("p (c n) -> p c n", c=2) for m in range(2)]
        pacc = [work[0:S, 1024 * m:1024 * (m + 1)] for m in range(2)]
        ptmp = [work[0:S, 2048 + 1024 * m:2048 + 1024 * (m + 1)] for m in range(2)]
        oT = work[:, 4096:4096 + HC * S].rearrange("p (c n) -> p c n", c=HC)
        g2 = [work[0:S, 1024 * m:1024 * m + FI] for m in range(2)]
        h2 = [work[0:S, 2048 + 1024 * m:2048 + 1024 * m + FI] for m in range(2)]
        hq = [work[0:S, 4096 + 512 * m:4096 + 512 * (m + 1)].bitcast(bf16) for m in range(1)][0]
        hqT = work[:, 4608:4608 + FIC * S // 2].bitcast(bf16).rearrange("p (c n) -> p c n", c=FIC)
        sim = sb("sim", [S, B, NJ, H])
        smax = sb("smax", [S, B, H])
        ssum = sb("ssum", [S, B, H])
        wr = sb("wr", [P, KD, E])
        ebias = sb("ebias", [S, E])
        down8 = sb("down8", [S, E])
        down8i = sb("down8i", [S, E], i32)
        rt = sb("rt", [S, 6, B, E])
        rsm = sb("rsm", [S, 3, B])
        gate_w = sb("gate_w", [S, B, E])
        sg = sb("sg", [P, 2, N4])
        wsx = sb("wsx", [P, KD, D])
        wx = sb("wx", [P, KD, D])
        bcol = sb("bcol", [P, KD])
        wvec = sb("wvec", [P, KD])
        wc = sb("wc", [P, 2, KD])
        wcrep = sb("wcrep", [P, 2, KD, S])
        bc = sb("bc", [S, 2])
        featT = sb("featT", [P, KD, B * S])
        mrow = sb("mrow", [B, CP], i32)
        mnz = sb("mnz", [B, CP])
        kflag = sb("kflag", [B, NU])
        kdown = sb("kdown", [B, NU])
        kdowni = sb("kdowni", [B, NU], i32)
        kcount = sb("kcount", [B, 1])
        rowf = sb("rowf", [1, 3, B])
        table = sb("table", [1, 2, B], i32)
        maskb = sb("maskb", [S, 2, C], i32)
        rho = sb("rho", [S, 3, C])
        ee = sb("ee", [S, C])
        sm = sb("sm", [S, 8])
        xq = sb("xq", [P, KD, B * S], bf16)
        fq = sb("fq", [P, 3, 2048], bf16)
        fsc = sb("fsc", [P, 4, 3])
        amax = sb("amax", [S, 4, B])
        alpha = sb("alpha", [S, 2, B])
        hm = sb("hm", [S, 2, 4])
        xl = big[0:S, 0:B * D].rearrange("p (b d) -> p b d", b=B)

        psum = ctx.enter_context(nc.psum_tensor("psum", [P, 8, G], fp32))
        bank = [psum[:, i, :] for i in range(8)]

        s = {}
        for name in (
            "ld_x ld_misc ld_wq ld_wkv ld_wout ld_moe ld_ff ld_ctx0 ld_ctx1 ld_mrow ld_mask0 ld_mask1 st_out "
            "const p_chain q_ready q_ev qT_ev k_mm prod_rdy sim_mm sim_ev s_chain max_sub exp_done p_rdy "
            "v_mm v_used pv_done tp_done tp_ev o_mm x1_rdy bo_rdy "
            "r_mm sig_done r_chain gw_rdy g_mm silu_done h_rdy d_mm d_used x2_chain "
            "f_mm f_ev tab_chain tab_rdy t_mm t_ev cw_mm cw_ev rho_zero z_rdy t_done rho_mm "
            "a_chain e_in e_done w_in w_done x3_rdy "
            "fw_mean fw_bc fw_chain fw_rdy fg_mm fu_mm fs_done fh_chain hq_rdy hT_mm hT_ev fo_mm x4_rdy h_used "
            "c_in c_done ctx_x cnt_mm cnt_in d8 al_rdy").split():
            s[name] = sem(name)
        lns = [{k: sem(f"ln{n}_{k}") for k in ("stat", "rstd", "x", "T", "ev", "ch", "pch")} for n in range(4)]

        block = ctx.enter_context(nc.Block())

        def row(t, b):
            return t[:, ds(b, 1), :].rearrange("p a d -> p (a d)")

        def chain(eng, sm_, base=0):
            n = [0]

            def link(ins):
                n[0] += 1
                ins.then_inc(sm_, 1)
                eng.wait_ge(sm_, base + n[0])
            return link

        def ln_vector(dve, n, apply=True):
            q = lns[n]
            with dve.Fori(0, B) as b:
                dve.bn_stats(stats[:, ds(b, 1), :].rearrange("p a s -> p (a s)"), row(x, b)).then_inc(q["ch"], 1)
            for b in range(B):
                dve.wait_ge(q["ch"], b + 1)
                dve.bn_aggr(meanvar[:, b, :], stats[:, b, :]).then_inc(q["stat"], 1)
            dve.wait_ge(q["stat"], B)
            dve.wait_ge(q["rstd"], 1)
            if n == 3:
                with dve.Fori(0, B) as b:
                    dve.tensor_scalar(row(xl, b), row(x, b),
                                      meanvar[:, ds(b, 1), 0:1].rearrange("p a s -> p (a s)"), rstd[:, ds(b, 1)],
                                      ALU.subtract, ALU.mult).then_inc(q["ch"], 1)
                dve.wait_ge(q["ch"], 2 * B)
                link = chain(dve, q["ch"], 2 * B)
                link(dve.tensor_reduce(amax[:, 0, :], xl[:, :, :], AX.X, ALU.max, apply_absolute_value=True))
                link(dve.tensor_scalar(amax[:, 1, :], amax[:, 0, :], 1e-5, None, ALU.max))
                link(dve.reciprocal(amax[:, 2, :], amax[:, 1, :]))
                link(dve.tensor_scalar(amax[:, 2, :], amax[:, 2, :], 127.0, None, ALU.mult))
                link(dve.tensor_scalar(amax[:, 1, :], amax[:, 1, :], 1.0 / 127.0, None, ALU.mult))
                with dve.Fori(0, NP) as i:
                    for par in range(2):
                        b = 2 * i + par
                        xb = row(xl, b)
                        base = 2 * B + 5 + 4 * i + 2 * par
                        dve.tensor_scalar(xb, xb, amax[:, 2, ds(b, 1)], 127.0, ALU.mult, ALU.min).then_inc(q["ch"], 1)
                        dve.wait_ge(q["ch"], base + 1)
                        dve.tensor_scalar(xb, xb, -128.0, ROUND, ALU.max, ALU.add).then_inc(q["ch"], 1)
                        dve.wait_ge(q["ch"], base + 2)
                        dve.wait_ge(q["T"], b + 1)
                        dve.tensor_scalar(lnN[:, par, :], xb, ROUND, None, ALU.subtract).then_inc(q["x"], 1)
            else:
                with dve.Fori(0, NP) as i:
                    for par in range(2):
                        b = 2 * i + par
                        dve.wait_ge(q["T"], b + 1)
                        dve.tensor_scalar(lnN[:, par, :], row(x, b),
                                          meanvar[:, ds(b, 1), 0:1].rearrange("p a s -> p (a s)"), rstd[:, ds(b, 1)],
                                          ALU.subtract, ALU.mult).then_inc(q["x"], 1)

        def ln_gpsimd(pool, n):
            q = lns[n]
            pool.wait_ge(q["stat"], B)
            pool.tensor_scalar(vareps[:, :], meanvar[:, :, 1], EPS, None, ALU.add).then_inc(q["pch"], 1)
            pool.wait_ge(q["pch"], 1)
            pool.tensor_tensor(rstd[:, :], vareps[:, :], half[:, :], ALU.pow).then_inc(q["rstd"], 1)

        def ln_tensor(pe, n):
            q = lns[n]
            pe.sem_inc(q["T"], 2)
            with pe.Fori(0, NP) as i:
                for par in range(2):
                    b = 2 * i + par
                    pe.wait_ge(q["x"], b + 1)
                    pe.wait_ge(q["ev"], b + 1)
                    for k in range(KD):
                        last = pe.transpose(bank[6 + par][:, k * S:(k + 1) * S],
                                            lnN[:, par, k * P:(k + 1) * P], ident[0:S, 0:S])
                    last.then_inc(q["T"], 1)

        def ln_scalar(act, n):
            q = lns[n]
            dst = xq if n == 3 else lnT
            act.sem_inc(q["ev"], 2)
            with act.Fori(0, NP) as i:
                for par in range(2):
                    b = 2 * i + par
                    act.wait_ge(q["T"], b + 3)
                    act.activation(dst[:, :, ds(b * S, S)],
                                   bank[6 + par][:, 0:KD * S].rearrange("p (k s) -> p k s", k=KD),
                                   ACT.Copy).then_inc(q["ev"], 1)

        def ln_done(eng, n):
            eng.wait_ge(lns[n]["ev"], B + 2)

        @block.sync
        def _(sp):
            sp.dma_start(x[:, 0:8, :], x_in[0:8].rearrange("b s d -> s b d")).then_inc(s["ld_x"], 16)
            sp.dma_start(x[:, 8:16, :], x_in[8:16].rearrange("b s d -> s b d")).then_inc(s["ld_x"], 16)
            sp.dma_start(wq, wq_in.rearrange("(k p) n -> p k n", p=P)).then_inc(s["ld_wq"], 16)
            sp.dma_start(wkv, wkv_in.rearrange("(k p) n -> p k n", p=P)).then_inc(s["ld_wkv"], 16)

            def load_ctx(b, par, used, count):
                if used is not None:
                    sp.wait_ge(used, count)
                sp.dma_start(ctxb[:, par, :, :], ctx_t[ds(b, 1), :, :].rearrange("a (k p) c -> p (a k) c", p=P)
                             ).then_inc(s[f"ld_ctx{par}"], 16)
            load_ctx(0, 0, None, 0)
            load_ctx(1, 1, None, 0)
            sp.dma_start(wout[:, :, :], wout_in.rearrange("(c p) n -> p c n", p=P)).then_inc(s["ld_wout"], 16)
            with sp.Fori(1, NP) as i:
                for par in range(2):
                    load_ctx(2 * i + par, par, s["k_mm"], HC // 2 * (2 * i + par - 1))
            sp.wait_ge(s["k_mm"], HC // 2 * B)
            load_ctx(0, 0, None, 0)
            load_ctx(1, 1, None, 0)
            sp.wait_ge(s["prod_rdy"], B * (HC // 2) + 2)
            sp.dma_start(wg, wg_in.rearrange("(k p) n -> p k n", p=P)).then_inc(s["ld_moe"], 16)
            sp.dma_start(wu, wu_in.rearrange("(k p) n -> p k n", p=P)).then_inc(s["ld_moe"], 16)
            with sp.Fori(1, NP) as i:
                for par in range(2):
                    load_ctx(2 * i + par, par, s["v_mm"], NJ * (2 * i + par - 1))
            full = FT // P
            sp.dma_start(wd[:, 0:full, :], wd_in[0:full * P].rearrange("(c p) n -> p c n", p=P)).then_inc(s["ld_moe"], 16)
            sp.dma_start(wd[0:FT - full * P, full, :], wd_in[full * P:FT, :]).then_inc(s["ld_moe"], 16)
            sp.wait_ge(s["v_mm"], NJ * B)

            def load_mask(b, par):
                sp.dma_start(maskb[:, par, :], mask_in[ds(b, 1), :].broadcast_to([S, C])
                             ).then_inc(s[f"ld_mask{par}"], 16)
            for par in range(2):
                load_ctx(par, par, None, 0)
                load_mask(par, par)
            sp.dma_start(fw[0].rearrange("p (k n) -> p k n", k=KD), fg_in.rearrange("(k p) n -> p k n", p=P)).then_inc(s["ld_ff"], 16)
            sp.dma_start(fw[1].rearrange("p (k n) -> p k n", k=KD), fu_in.rearrange("(k p) n -> p k n", p=P)).then_inc(s["ld_ff"], 16)
            sp.dma_start(fw[2].rearrange("p (k n) -> p k n", k=FIC), fd_in.rearrange("(k p) n -> p k n", p=P)).then_inc(s["ld_ff"], 16)
            with sp.Fori(1, NP) as i:
                for par in range(2):
                    b = 2 * i + par
                    load_ctx(b, par, s["ctx_x"], b - 1)
                    sp.wait_ge(s["e_in"], b - 1)
                    load_mask(b, par)
            with sp.Fori(0, NP) as i:
                sp.wait_ge(s["x4_rdy"], 2 * i + 4)
                sp.dma_start(out[ds(2 * i, 2)].rearrange("b s d -> s b d"), x[:, ds(2 * i, 2), :]).then_inc(s["st_out"], 16)
            sp.wait_ge(s["st_out"], 16 * NP)

        @block.gpsimd
        def _(pool):
            small = [(wr[:, :, :], wr_in.rearrange("(k p) n -> p k n", p=P)),
                     (ebias[:, :], ebias_in.rearrange("(a n) -> a n", a=1).broadcast_to([S, E])),
                     (bout[:, :], bout_in.rearrange("(a n) -> a n", a=1).broadcast_to([S, D])),
                     (wsx[:, :, :], ws_in.rearrange("(k p) n -> p k n", p=P)),
                     (wx[:, :, :], w_in.rearrange("(k p) n -> p k n", p=P)),
                     (bc[:, 0:1], bcw_in.rearrange("(a n) -> a n", a=1).broadcast_to([S, 1])),
                     (bc[:, 1:2], bcb_in.rearrange("(a n) -> a n", a=1).broadcast_to([S, 1]))]
            for dst, src in small:
                pool.dma_start(dst, src).then_inc(s["ld_misc"], 16)
            with nc.allow_non_contiguous_dma(reason="256 values each, once"):
                for dst, src in ((bcol[:, :], b_in.rearrange("a (k p) -> p (a k)", p=P)),
                                 (wvec[:, :], wvec_in.rearrange("(k p) a -> p (k a)", p=P)),
                                 (wc[:, 0, :], wcw_in.rearrange("a (k p) -> p (a k)", p=P)),
                                 (wc[:, 1, :], wcb_in.rearrange("a (k p) -> p (a k)", p=P))):
                    pool.dma_start(dst, src).then_inc(s["ld_misc"], 16)
            link = chain(pool, s["p_chain"])
            link(pool.memset(half[:, :], -0.5))
            link(pool.memset(ident[:, :], 0.0))
            link(pool.memset(ones[:, :], 1.0))
            link(pool.memset(headsel[:, :], 0.0))
            link(pool.memset(headsel[0:DH, 0:1], 1.0))
            link(pool.memset(headsel[DH:P, 1:2], 1.0))
            link(pool.memset(mrow[:, C:CP], 0))
            pool.dma_start(mrow[:, 0:C], mask_in).then_inc(s["ld_mrow"], 16)
            link(pool.iota(kdowni[:, :], pattern=[[-1, NU]], base=NU, channel_multiplier=0))
            link(pool.iota(down8i[:, :], pattern=[[-1, E]], base=E, channel_multiplier=0))
            pool.affine_select(out=ident[:, :], in_=ident[:, :], compare_op=ALU.not_equal, fill=1.0,
                               base=0, pattern=[[-1, P]], channel_multiplier=1).then_inc(s["const"], 1)
            ln_gpsimd(pool, 0)
            pool.wait_ge(s["ld_misc"], 16 * 11)
            pool.wait_ge(lns[0]["x"], B)
            pool.tensor_tensor(x[:, :, :], x[:, :, :], bout[:, :].unsqueeze(1).broadcast_to([S, B, D]), ALU.add
                               ).then_inc(s["bo_rdy"], 1)
            pool.sem_inc(s["pv_done"], 2)
            with pool.Fori(0, NP) as i:
                for par in range(2):
                    b = 2 * i + par
                    for j in range(1, NJ):
                        n = JR[j]
                        pool.wait_ge(s["v_used"], NJ * b + j + 3)
                        if j > 1:
                            pool.wait_ge(s["pv_done"], (NJ - 1) * b + j + 1)
                        pool.tensor_tensor(pacc[par][0:n, :], pacc[par][0:n, :], ptmp[(par * (NJ - 1) + j - 1) % 2][0:n, :],
                                           ALU.add).then_inc(s["pv_done"], 1)
            ln_gpsimd(pool, 1)
            ln_gpsimd(pool, 2)
            pool.wait_ge(s["fw_chain"], 2)
            link = chain(pool, s["fw_rdy"])
            for m in range(3):
                link(pool.tensor_scalar(fw[m], fw[m], fsc[:, 2, m:m + 1], 1.0, ALU.mult, ALU.min))
                link(pool.tensor_scalar(fw[m], fw[m], -1.0, ROUND, ALU.max, ALU.add))
                link(pool.tensor_scalar(fq[:, m, :], fw[m], ROUND, None, ALU.subtract))
            ln_gpsimd(pool, 3)

        @block.tensor
        def _(pe):
            pe.wait_ge(s["const"], 1)
            pe.wait_ge(s["cnt_in"], 1)
            pe.transpose(bank[5][0:1, 0:B], kcount[:, :], ident[0:B, 0:B]).then_inc(s["cnt_mm"], 1)
            ln_tensor(pe, 0)
            ln_done(pe, 0)
            pe.wait_ge(s["ld_wq"], 16)
            with pe.Fori(0, NT) as t:
                for c in range(HC):
                    pe.wait_ge(s["q_ev"], t * HC + c + 1)
                    for k in range(KD):
                        last = pe.matmul(bank[c % 2][:, 0:N4], wq[:, k, c * P:(c + 1) * P],
                                         lnT[:, k, ds(t * N4, N4)], start=(k == 0), stop=(k == KD - 1))
                    last.then_inc(s["q_ready"], 1)
            pe.wait_ge(s["ld_wkv"], 16)
            pe.wait_ge(s["q_ev"], NT * HC + 2)

            def sims(b, par, m):
                pe.wait_ge(s["prod_rdy"], (HC // 2) * b + m + 3)
                if m == 0:
                    pe.wait_ge(s["sim_ev"], b + 1)
                for u in range(2):
                    for j in range(NJ):
                        last = pe.matmul(bank[4 + par][0:JR[j], j * H + 4 * m + 2 * u:j * H + 4 * m + 2 * u + 2],
                                         prod[m % 2][:, u, j * S:j * S + JR[j]], headsel[:, :], start=True, stop=True)
                last.then_inc(s["sim_mm"], 1)

            pe.sem_inc(s["sim_mm"], 2)
            with pe.Fori(0, NP) as i:
                for par in range(2):
                    b = 2 * i + par
                    pe.wait_ge(s[f"ld_ctx{par}"], 16 * i + 16)
                    for m in range(HC // 2):
                        pe.wait_ge(s["prod_rdy"], (HC // 2) * b + m + 1)
                        for u in range(2):
                            c = 2 * m + u
                            for k in range(KD):
                                last = pe.matmul(bank[2 * (m % 2) + u][:, 0:C], wkv[:, k, c * P:(c + 1) * P],
                                                 ctxb[:, par, k, :], start=(k == 0), stop=(k == KD - 1))
                        last.then_inc(s["k_mm"], 1)
                        if m > 0:
                            sims(b, par, m - 1)
                    sims(b, par, HC // 2 - 1)
            pe.wait_ge(s["sim_ev"], B + 2)

            def values(b, par, i):
                pe.wait_ge(s[f"ld_ctx{par}"], 16 * (B // 2) + 16 * i + 16)
                for j in range(NJ):
                    pe.wait_ge(s["v_used"], NJ * b + j + 1)
                    for n in range(2):
                        for k in range(KD):
                            last = pe.matmul(bank[2 * (j % 2) + n][0:JR[j], :], ctxb[:, par, k, j * S:j * S + JR[j]],
                                             wkv[:, k, INNER + n * G:INNER + (n + 1) * G],
                                             start=(k == 0), stop=(k == KD - 1))
                    last.then_inc(s["v_mm"], 1)

            def project(b, par):
                pe.wait_ge(s["pv_done"], (NJ - 1) * (b + 1) + 2)
                for c in range(HC):
                    if c % 4 == 0:
                        pe.wait_ge(s["tp_ev"], 2 * b + c // 4 + 1)
                    last = pe.transpose(bank[4 + c // 4][:, (c % 4) * S:(c % 4 + 1) * S],
                                        pacc[par][:, c * P:(c + 1) * P], ident[0:S, 0:S])
                    if c % 4 == 3:
                        last.then_inc(s["tp_done"], 1)
                pe.wait_ge(s["tp_ev"], 2 * b + 4)
                pe.wait_ge(s["x1_rdy"], b + 1)
                for c in range(HC):
                    last = pe.matmul(bank[6 + par][0:S, 0:D], oT[:, c, :], wout[:, c, :],
                                     start=(c == 0), stop=(c == HC - 1))
                last.then_inc(s["o_mm"], 1)

            pe.wait_ge(s["ld_wout"], 16)
            pe.sem_inc(s["tp_done"], 4)
            pe.sem_inc(s["o_mm"], 1)
            values(0, 0, 0)
            with pe.Fori(0, NP - 1) as i:
                for par in range(2):
                    b = 2 * i + par
                    values(b + 1, 1 - par, i + par)
                    project(b, par)
            values(B - 1, 1, NP - 1)
            project(B - 2, 0)
            project(B - 1, 1)

            pe.wait_ge(s["x1_rdy"], B + 2)
            ln_tensor(pe, 1)
            ln_done(pe, 1)
            for b in range(B):
                for k in range(KD):
                    last = pe.matmul(bank[7][0:S, b * E:(b + 1) * E], lnT[:, k, b * S:(b + 1) * S], wr[:, k, :],
                                     start=(k == 0), stop=(k == KD - 1))
            last.then_inc(s["r_mm"], 1)
            pe.wait_ge(s["ld_moe"], 64)
            with pe.Fori(0, NT) as t:
                for c in range(FC):
                    w = min(P, FT - c * P)
                    before = pe.to_reg(t * FC + c + 1)
                    if w < P:
                        pe.wait_ge(s["ld_moe"], 64)
                    pe.wait_ge(s["h_rdy"], before)
                    for bk, wgt in ((0, wg), (2, wu)):
                        for k in range(KD):
                            last = pe.matmul(bank[bk + c % 2][0:w, 0:N4], wgt[:, k, c * P:c * P + w],
                                             lnT[:, k, ds(t * N4, N4)], start=(k == 0), stop=(k == KD - 1))
                    last.then_inc(s["g_mm"], 1)
                pe.wait_ge(s["h_rdy"], t * FC + FC + 2)
                for lb in range(TB):
                    for n, e in enumerate([E] + list(range(E))):
                        parts = [(3 * (e // 2), 0, P), (3 * (e // 2) + 1, 0, P // 2)] if e % 2 == 0 else \
                                [(3 * (e // 2) + 1, P // 2, P), (3 * (e // 2) + 2, 0, P)]
                        slot = (lb * (E + 1) + n) % 4
                        pe.wait_ge(s["d_used"], t * TB * (E + 1) + lb * (E + 1) + n + 1)
                        for q, (c, lo, hi) in enumerate(parts):
                            last = pe.matmul(bank[4 + slot][0:S, 0:D], hT[lo:hi, c, lb * S:(lb + 1) * S],
                                             wd[lo:hi, c, :], start=(q == 0), stop=(q == 1))
                        last.then_inc(s["d_mm"], 1)

            pe.wait_ge(s["d_used"], NT * TB * (E + 1) + 4)
            ln_tensor(pe, 2)
            ln_done(pe, 2)
            with pe.Fori(0, NT) as t:
                for m in range(KD):
                    pe.wait_ge(s["f_ev"], t * KD + m + 1)
                    for k in range(KD):
                        last = pe.matmul(bank[m][:, 0:N4], wx[:, k, m * P:(m + 1) * P], lnT[:, k, ds(t * N4, N4)],
                                         start=(k == 0), stop=(k == KD - 1))
                    last.then_inc(s["f_mm"], 1)
            pe.wait_ge(s["f_ev"], NT * KD + 2)

            def project_ctx(b, par, i):
                pe.wait_ge(s[f"ld_ctx{par}"], 2 * 16 * (B // 2) + 16 * i + 16)
                pe.wait_ge(s["t_ev"], b + 1)
                for m in range(KD):
                    for k in range(KD):
                        last = pe.matmul(bank[m][:, 0:C], wsx[:, k, m * P:(m + 1) * P], ctxb[:, par, k, :],
                                         start=(k == 0), stop=(k == KD - 1))
                last.then_inc(s["t_mm"], 1)
                pe.wait_ge(s["cw_ev"], b + 1)
                for m in range(2):
                    for k in range(KD):
                        last = pe.matmul(bank[2 + m][0:S, 0:C], wcrep[:, m, k, :], ctxb[:, par, k, :],
                                         start=(k == 0), stop=(k == KD - 1))
                last.then_inc(s["ctx_x"], 1)

            def logits(b, par):
                first = pe.value_load(table[0:1, 0, ds(b, 1)], min_val=0, max_val=NU - 1)
                ends = pe.value_load(table[0:1, 1, ds(b, 1)], min_val=1, max_val=B * NU)
                this = pe.to_reg(b + 1)
                pe.wait_ge(s["tab_rdy"], 1)
                pe.wait_ge(s["rho_zero"], this)
                with pe.Fori(first, NU) as u:
                    for hf in range(2):
                        q = 2 * (ends + u) + hf
                        pe.wait_ge(s["t_done"], q + 3)
                        for t in range(HALF):
                            for k in range(KD):
                                last = pe.matmul(bank[4 + par][0:S, ds(u * UNIT + hf * HALF + t, 1)],
                                                 ht[hf][:, k, t, :], wvec[:, k:k + 1],
                                                 start=(k == 0), stop=(k == KD - 1))
                        last.then_inc(s["rho_mm"], 1)

            pe.wait_ge(s["fw_mean"], 3)
            pe.matmul(bank[7][:, 0:3], ones[:, :], fsc[:, 0, :], start=True, stop=True).then_inc(s["fw_bc"], 1)
            pe.wait_ge(s["tab_rdy"], 1)
            pe.wait_ge(s["c_done"], 1)
            pe.sem_inc(s["rho_mm"], 2 * NU + 2)
            project_ctx(0, 0, 0)
            with pe.Fori(0, NP - 1) as i:
                for par in range(2):
                    b = 2 * i + par
                    project_ctx(b + 1, 1 - par, i + par)
                    logits(b, par)
            project_ctx(B - 1, 1, NP - 1)
            logits(B - 2, 0)
            logits(B - 1, 1)

            pe.wait_ge(s["x3_rdy"], B + 2)
            ln_tensor(pe, 3)
            ln_done(pe, 3)
            pe.wait_ge(s["fw_rdy"], 9)
            pe.sem_inc(s["hT_mm"], 1)
            pe.sem_inc(s["fo_mm"], 1)

            def up(b):
                for hf in range(2):
                    for m, (bk, used) in enumerate(((0, "fs_done"), (2, "h_used"))):
                        pe.wait_ge(s[used], 2 * b + hf + 1)
                        for k in range(KD):
                            last = pe.matmul(bank[bk + hf][0:S, :], xq[:, k, ds(b * S, S)],
                                             fq[:, m, k * FI + hf * G:k * FI + (hf + 1) * G],
                                             start=(k == 0), stop=(k == KD - 1))
                        last.then_inc(s["fg_mm" if m == 0 else "fu_mm"], 1)

            def down(b, par):
                pe.wait_ge(s["hq_rdy"], b + 1)
                pe.wait_ge(s["hT_ev"], b + 1)
                for c in range(FIC):
                    last = pe.transpose(bank[4].bitcast(bf16)[:, c * S:(c + 1) * S],
                                        hq[:, c * P:(c + 1) * P], ident16[0:S, 0:S])
                last.then_inc(s["hT_mm"], 1)
                pe.wait_ge(s["hT_ev"], b + 2)
                pe.wait_ge(s["x4_rdy"], b + 1)
                for c in range(FIC):
                    last = pe.matmul(bank[6 + par][0:S, 0:D], hqT[:, c, :], fq[:, 2, c * D:(c + 1) * D],
                                     start=(c == 0), stop=(c == FIC - 1))
                last.then_inc(s["fo_mm"], 1)

            up(0)
            with pe.Fori(0, NP - 1) as i:
                for par in range(2):
                    up(2 * i + par + 1)
                    down(2 * i + par, par)
            up(B - 1)
            down(B - 2, 0)
            down(B - 1, 1)

        @block.scalar
        def _(act):
            ln_scalar(act, 0)
            act.sem_inc(s["q_ev"], 2)
            with act.Fori(0, NT) as t:
                for c in range(HC):
                    act.wait_ge(s["q_ready"], t * HC + c + 1)
                    act.activation(qT[:, c, ds(t * N4, N4)], bank[c % 2][:, 0:N4], ACT.Copy, scale=DH ** -0.5
                                   ).then_inc(s["q_ev"], 1)
            act.wait_ge(s["max_sub"], 1)
            act.activation(sim[:, :, :, :], sim[:, :, :, :], ACT.Exp).then_inc(s["exp_done"], 1)
            act.sem_inc(s["tp_ev"], 2)
            with act.Fori(0, B) as b:
                act.wait_ge(s["o_mm"], b + 1)
                for hf in range(2):
                    act.wait_ge(s["tp_done"], 2 * b + hf + 5)
                    act.activation(oT[:, 4 * hf:4 * hf + 4, :],
                                   bank[4 + hf][:, 0:4 * S].rearrange("p (c n) -> p c n", c=4), ACT.Copy
                                   ).then_inc(s["tp_ev"], 1)
            ln_scalar(act, 1)
            act.wait_ge(s["r_mm"], 1)
            act.activation(rt[:, 0, :, :], bank[7][0:S, 0:B * E].rearrange("p (b e) -> p b e", b=B), ACT.Sigmoid
                           ).then_inc(s["sig_done"], 1)
            with act.Fori(0, NT) as t:
                for c in range(FC):
                    w = min(P, FT - c * P)
                    act.wait_ge(s["g_mm"], t * FC + c + 1)
                    act.wait_ge(s["h_rdy"], t * FC + c + 1)
                    act.activation(sg[0:w, c % 2, :], bank[c % 2][0:w, 0:N4], ACT.Silu).then_inc(s["silu_done"], 1)
            ln_scalar(act, 2)
            act.sem_inc(s["f_ev"], 2)
            act.sem_inc(s["t_ev"], 1)
            act.sem_inc(s["cw_ev"], 1)
            act.sem_inc(s["t_done"], 2 * NU + 2)
            act.wait_ge(s["ld_misc"], 16 * 11)
            with act.Fori(0, NT) as t:
                for m in range(KD):
                    act.wait_ge(s["f_mm"], t * KD + m + 1)
                    act.activation(featT[:, m, ds(t * N4, N4)], bank[m][:, 0:N4], ACT.Identity, bias=bcol[:, m:m + 1]
                                   ).then_inc(s["f_ev"], 1)

            def copy_ctx(b, par):
                act.wait_ge(s["t_mm"], b + 1)
                act.activation(txtT[par][:, :, 0:C], psum[:, 0:KD, 0:C], ACT.Copy).then_inc(s["t_ev"], 1)
                act.wait_ge(s["ctx_x"], b + 1)
                act.wait_ge(s["x3_rdy"], b + 1)
                act.activation(cwb[par], psum[0:S, 2:4, 0:C], ACT.Copy).then_inc(s["cw_ev"], 1)

            def tanhs(b):
                first = act.value_load(table[0:1, 0, ds(b, 1)], min_val=0, max_val=NU - 1)
                ends = act.value_load(table[0:1, 1, ds(b, 1)], min_val=1, max_val=B * NU)
                with act.Fori(first, NU) as u:
                    for hf in range(2):
                        q = 2 * (ends + u) + hf
                        act.wait_ge(s["z_rdy"], q + 3)
                        act.wait_ge(s["rho_mm"], q + 1)
                        act.activation(ht[hf], zt[hf], ACT.Tanh).then_inc(s["t_done"], 1)

            def weigh(b):
                act.wait_ge(s["e_in"], b + 1)
                act.activation(ee[:, :], rho[:, 1, :], ACT.Exp, bias=sm[:, 0:1], accum_out=sm[:, 1:2]
                               ).then_inc(s["e_done"], 1)
                act.wait_ge(s["w_in"], b + 1)
                for m in range(2):
                    last = act.activation(sm[:, 5 + m:6 + m], sm[:, 2 + m:3 + m], ACT.Tanh,
                                          bias=bc[:, m:m + 1], scale=sm[:, 4:5])
                last.then_inc(s["w_done"], 1)

            act.wait_ge(s["tab_rdy"], 1)
            copy_ctx(0, 0)
            copy_ctx(1, 1)
            tanhs(0)
            with act.Fori(0, NP - 1) as i:
                for d in (1, 2):
                    b = 2 * i + d
                    tanhs(b)
                    weigh(b - 1)
                    copy_ctx(b + 1, (d + 1) % 2)
            tanhs(B - 1)
            weigh(B - 2)
            weigh(B - 1)
            ln_scalar(act, 3)
            act.wait_ge(s["al_rdy"], 2)
            act.sem_inc(s["fs_done"], 2)
            act.sem_inc(s["hT_ev"], 1)

            def gate(b, par):
                for hf in range(2):
                    this = act.to_reg(2 * b + hf + 1)
                    act.wait_ge(s["al_rdy"], 2)
                    act.wait_ge(s["fg_mm"], this)
                    act.wait_ge(s["h_used"], this)
                    act.activation(g2[par][:, hf * G:(hf + 1) * G], bank[hf][0:S, :], ACT.Silu,
                                   scale=alpha[:, 0, ds(b, 1)]).then_inc(s["fs_done"], 1)

            def copy_h(b):
                act.wait_ge(s["hT_mm"], b + 2)
                act.wait_ge(s["fo_mm"], b + 1)
                act.activation(hqT, bank[4].bitcast(bf16)[:, 0:FIC * S].rearrange("p (c n) -> p c n", c=FIC),
                               ACT.Copy).then_inc(s["hT_ev"], 1)

            gate(0, 0)
            with act.Fori(0, NP - 1) as i:
                for par in range(2):
                    gate(2 * i + par + 1, 1 - par)
                    copy_h(2 * i + par)
            gate(B - 1, 1)
            copy_h(B - 2)
            copy_h(B - 1)

        @block.vector
        def _(dve):
            link = chain(dve, s["tab_chain"])
            dve.wait_ge(s["ld_mrow"], 16)
            dve.wait_ge(s["const"], 1)
            link(dve.tensor_copy(kdown[:, :], kdowni[:, :]))
            link(dve.tensor_scalar(mnz[:, :], mrow[:, :], 0.0, None, ALU.not_equal))
            link(dve.tensor_reduce(kflag[:, :], mnz[:, :].rearrange("p (u t) -> p u t", t=UNIT), AX.X, ALU.max))
            link(dve.tensor_tensor(kflag[:, :], kflag[:, :], kdown[:, :], ALU.mult))
            link(dve.tensor_reduce(kcount[:, :], kflag[:, :], AX.X, ALU.max))
            dve.tensor_scalar(kcount[:, :], kcount[:, :], 1.0, None, ALU.max).then_inc(s["cnt_in"], 1)
            dve.tensor_copy(ident16[:, :], ident[:, :]).then_inc(s["d8"], 1)
            dve.tensor_copy(down8[:, :], down8i[:, :]).then_inc(s["d8"], 1)
            dve.wait_ge(s["ld_x"], 32)
            dve.wait_ge(s["cnt_mm"], 1)
            link(dve.tensor_copy(rowf[:, 0, :], bank[5][0:1, 0:B]))
            link(dve.tensor_tensor_scan(rowf[:, 1, :], ones[0:1, 0:B], rowf[:, 0, :], 0.0, ALU.mult, ALU.add))
            link(dve.tensor_scalar(rowf[:, 2, :], rowf[:, 0, :], -1.0, float(NU), ALU.mult, ALU.add))
            link(dve.tensor_copy(table[:, 0, :], rowf[:, 2, :]))
            dve.tensor_copy(table[:, 1, :], rowf[:, 1, :]).then_inc(s["tab_rdy"], 1)
            dve.wait_ge(s["ld_misc"], 16 * 11)
            dve.tensor_copy(wcrep[:, :, :, :], wc[:, :, :].unsqueeze(3).broadcast_to([P, 2, KD, S])
                            ).then_inc(s["c_done"], 1)
            ln_vector(dve, 0)
            dve.memset(sim[:, :, NJ - 1, :], NEG).then_inc(s["s_chain"], 1)
            dve.wait_ge(s["s_chain"], 1)
            dve.sem_inc(s["prod_rdy"], 2)
            dve.sem_inc(s["sim_ev"], 2)
            dve.wait_ge(s["q_ev"], NT * HC + 2)
            with dve.Fori(0, NP) as i:
                for par in range(2):
                    b = 2 * i + par
                    for m in range(HC // 2):
                        g = (HC // 2) * b + m
                        k2 = psum[:, 2 * (m % 2):2 * (m % 2) + 2, :]
                        dve.wait_ge(s["k_mm"], g + 1)
                        dve.wait_ge(s["sim_mm"], g + 1)
                        q2 = qT[:, 2 * m:2 * m + 2, ds(b * S, S)]
                        dve.tensor_tensor(prod[m % 2][:, :, 0:JF * S].rearrange("p u (j s) -> p u j s", s=S),
                                          k2[:, :, 0:JF * S].rearrange("p u (j s) -> p u j s", s=S),
                                          q2.unsqueeze(2).broadcast_to([P, 2, JF, S]), ALU.mult)
                        dve.tensor_tensor(prod[m % 2][:, :, JF * S:C], k2[:, :, JF * S:C],
                                          qT[:, 2 * m:2 * m + 2, ds(b * S, C - JF * S)], ALU.mult
                                          ).then_inc(s["prod_rdy"], 1)
                    dve.wait_ge(s["sim_mm"], (HC // 2) * (b + 1) + 2)
                    dve.tensor_copy(sim[:, ds(b, 1), 0:JF, :].rearrange("p a j h -> p (a j h)"),
                                    bank[4 + par][0:S, 0:JF * H])
                    dve.tensor_copy(sim[0:JR[-1], ds(b, 1), JF, :].rearrange("p a h -> p (a h)"),
                                    bank[4 + par][0:JR[-1], JF * H:NJ * H]).then_inc(s["sim_ev"], 1)
            link = chain(dve, s["s_chain"], 1)
            dve.wait_ge(s["sim_ev"], B + 2)
            link(dve.tensor_reduce(smax[:, :, :], sim[:, :, :, :].rearrange("p b j h -> p b h j"), AX.X, ALU.max))
            dve.tensor_tensor(sim[:, :, :, :], sim[:, :, :, :], smax[:, :, :].unsqueeze(2).broadcast_to([S, B, NJ, H]),
                              ALU.subtract).then_inc(s["max_sub"], 1)
            dve.wait_ge(s["exp_done"], 1)
            link(dve.tensor_reduce(ssum[:, :, :], sim[:, :, :, :].rearrange("p b j h -> p b h j"), AX.X, ALU.add))
            link(dve.reciprocal(ssum[:, :, :], ssum[:, :, :]))
            link(dve.tensor_tensor(sim[:, :, :, :], sim[:, :, :, :], ssum[:, :, :].unsqueeze(2).broadcast_to([S, B, NJ, H]),
                                   ALU.mult))
            dve.sem_inc(s["v_used"], 2)
            dve.sem_inc(s["x1_rdy"], 2)

            def weigh_v(b, par):
                for j in range(NJ):
                    n = JR[j]
                    dve.wait_ge(s["v_mm"], NJ * b + j + 1)
                    if j == 0:
                        dve.wait_ge(s["tp_done"], 2 * b + 2)
                        dst = pacc[par]
                    else:
                        dve.wait_ge(s["pv_done"], (NJ - 1) * b + j)
                        dst = ptmp[(par * (NJ - 1) + j - 1) % 2]
                    ins = dve.tensor_tensor(dst[0:n, :].rearrange("p (h d) -> p h d", h=H),
                                            psum[0:n, 2 * (j % 2):2 * (j % 2) + 2, :].rearrange("p w (h d) -> p (w h) d", d=DH),
                                            sim[0:n, ds(b, 1), j, :].rearrange("p a h -> p (a h)").unsqueeze(2).broadcast_to([n, H, DH]),
                                            ALU.mult)
                    ins.then_inc(s["v_used"], 1)

            def residual1(b, par):
                dve.wait_ge(s["o_mm"], b + 2)
                dve.tensor_tensor(row(x, b), bank[6 + par][0:S, 0:D], row(x, b), ALU.add).then_inc(s["x1_rdy"], 1)

            dve.wait_ge(s["bo_rdy"], 1)
            weigh_v(0, 0)
            with dve.Fori(0, NP - 1) as i:
                for par in range(2):
                    weigh_v(2 * i + par + 1, 1 - par)
                    residual1(2 * i + par, par)
            weigh_v(B - 1, 1)
            residual1(B - 2, 0)
            residual1(B - 1, 1)
            dve.wait_ge(s["x1_rdy"], B + 2)
            ln_vector(dve, 1)
            link = chain(dve, s["r_chain"])
            dve.wait_ge(s["sig_done"], 1)
            dve.wait_ge(s["d8"], 2)

            def each(t):
                return t.unsqueeze(2).broadcast_to([S, B, E])
            score, biased, hit, one, two, w = [rt[:, n, :, :] for n in range(6)]
            best, order, total = [rsm[:, n, :] for n in range(3)]
            link(dve.tensor_tensor(biased, score, ebias[:, :].unsqueeze(1).broadcast_to([S, B, E]), ALU.add))
            for n, pick in enumerate((one, two)):
                link(dve.tensor_reduce(best, biased, AX.X, ALU.max))
                link(dve.tensor_tensor(hit, biased, each(best), ALU.is_equal))
                link(dve.tensor_tensor(hit, hit, down8[:, :].unsqueeze(1).broadcast_to([S, B, E]), ALU.mult))
                link(dve.tensor_reduce(order, hit, AX.X, ALU.max))
                link(dve.tensor_tensor(pick, hit, each(order), ALU.is_equal))
                if n == 0:
                    link(dve.scalar_tensor_tensor(biased, pick, NEG, biased, ALU.mult, ALU.add))
            link(dve.tensor_tensor(w, one, two, ALU.add))
            link(dve.tensor_tensor(w, w, score, ALU.mult))
            link(dve.tensor_reduce(total, w, AX.X, ALU.add))
            link(dve.tensor_scalar(total, total, 1e-20, None, ALU.add))
            link(dve.reciprocal(total, total))
            link(dve.tensor_tensor(gate_w[:, :, :], w, each(total), ALU.mult))
            dve.sem_inc(s["h_rdy"], 2)
            dve.sem_inc(s["d_used"], 4)
            with dve.Fori(0, NT) as t:
                for c in range(FC):
                    w_ = min(P, FT - c * P)
                    dve.wait_ge(s["silu_done"], t * FC + c + 1)
                    dve.tensor_tensor(hT[0:w_, c, :], sg[0:w_, c % 2, :], bank[2 + c % 2][0:w_, 0:N4], ALU.mult
                                      ).then_inc(s["h_rdy"], 1)
                for lb in range(TB):
                    b = t * TB + lb
                    for n, e in enumerate([E] + list(range(E))):
                        d = t * TB * (E + 1) + lb * (E + 1) + n
                        dve.wait_ge(s["d_mm"], d + 1)
                        dve.wait_ge(s["d_used"], d + 4)
                        pd = bank[4 + (lb * (E + 1) + n) % 4][0:S, 0:D]
                        if e == E:
                            ins = dve.tensor_tensor(row(x, b), pd, row(x, b), ALU.add)
                        else:
                            ins = dve.scalar_tensor_tensor(row(x, b), pd, gate_w[:, ds(b, 1), e], row(x, b),
                                                           ALU.mult, ALU.add)
                        ins.then_inc(s["d_used"], 1)
            dve.wait_ge(s["d_used"], NT * TB * (E + 1) + 4)
            dve.wait_ge(s["ld_ff"], 48)
            for m in range(3):
                dve.tensor_reduce(fsc[:, 0, m:m + 1], fw[m], AX.X, ALU.add, apply_absolute_value=True).then_inc(s["fw_mean"], 1)
            ln_vector(dve, 2)
            link = chain(dve, s["fw_chain"])
            dve.wait_ge(s["fw_bc"], 1)
            link(dve.tensor_scalar(fsc[:, 1, :], bank[7][:, 0:3], 1.0 / (D * FI), 1e-5, ALU.mult, ALU.max))
            link(dve.reciprocal(fsc[:, 2, :], fsc[:, 1, :]))
            for par in range(2):
                link(dve.memset(txtT[par][:, :, C:CP], 0.0))
            dve.sem_inc(s["x3_rdy"], 2)
            dve.sem_inc(s["z_rdy"], 2 * NU + 2)
            dve.wait_ge(s["f_ev"], NT * KD + 2)

            def sums(b, par):
                first = dve.value_load(table[0:1, 0, ds(b, 1)], min_val=0, max_val=NU - 1)
                ends = dve.value_load(table[0:1, 1, ds(b, 1)], min_val=1, max_val=B * NU)
                dve.memset(bank[4 + par][0:S, 0:CP], 0.0).then_inc(s["rho_zero"], 1)
                this = dve.to_reg(b + 2)
                dve.wait_ge(s["tab_rdy"], 1)
                dve.wait_ge(s["t_ev"], this)
                with dve.Fori(first, NU) as u:
                    for hf in range(2):
                        q = 2 * (ends + u) + hf
                        dve.wait_ge(s["t_done"], q + 1)
                        dve.tensor_tensor(zt[hf], featT[:, :, ds(b * S, S)].unsqueeze(2).broadcast_to([P, KD, HALF, S]),
                                          txtT[par][:, :, ds(u * UNIT + hf * HALF, HALF)].unsqueeze(3).broadcast_to([P, KD, HALF, S]),
                                          ALU.add).then_inc(s["z_rdy"], 1)
                return ends

            NS = 6

            def attend(b, par, i):
                ends = dve.value_load(table[0:1, 1, ds(b, 1)], min_val=1, max_val=B * NU)
                link = chain(dve, s["a_chain"], NS * b)
                dve.wait_ge(s["rho_zero"], b + 1)
                dve.wait_ge(s["rho_mm"], 2 * ends + 2 * NU + 2)
                dve.wait_ge(s[f"ld_mask{par}"], 16 * i + 16)
                link(dve.tensor_scalar(rho[:, 0, :], maskb[:, par, :], -1.0, 1.0, ALU.mult, ALU.add))
                link(dve.scalar_tensor_tensor(rho[:, 1, :], rho[:, 0, :], NEG, bank[4 + par][0:S, 0:C],
                                              ALU.mult, ALU.add))
                dve.tensor_reduce(sm[:, 0:1], rho[:, 1, :], AX.X, ALU.max, negate=True).then_inc(s["e_in"], 1)
                dve.wait_ge(s["e_in"], b + 1)
                dve.wait_ge(s["e_done"], b + 1)
                dve.wait_ge(s["cw_ev"], b + 2)
                for m in range(2):
                    link(dve.tensor_tensor_reduce(out=rho[:, 2, :], in0=ee[:, :], in1=cwb[par][:, m, :], scale=1.0,
                                                  scalar=0.0, op0=ALU.mult, op1=ALU.add, accum_out=sm[:, 2 + m:3 + m]))
                dve.reciprocal(sm[:, 4:5], sm[:, 1:2]).then_inc(s["w_in"], 1)
                link(dve.tensor_scalar(lnN[:, 0, :], row(x, b), meanvar[:, ds(b, 1), 0], rstd[:, ds(b, 1)],
                                       ALU.subtract, ALU.mult))
                dve.wait_ge(s["w_done"], b + 1)
                link(dve.tensor_scalar(lnN[:, 0, :], lnN[:, 0, :], sm[:, 5:6], sm[:, 6:7], ALU.mult, ALU.add))
                dve.tensor_tensor(row(x, b), row(x, b), lnN[:, 0, :], ALU.add).then_inc(s["x3_rdy"], 1)

            sums(0, 0)
            with dve.Fori(0, NP - 1) as i:
                for d in (1, 2):
                    sums(2 * i + d, d % 2)
                    attend(2 * i + d - 1, (d + 1) % 2, i)
            sums(B - 1, 1)
            attend(B - 2, 0, NP - 1)
            attend(B - 1, 1, NP - 1)
            dve.wait_ge(s["x3_rdy"], B + 2)
            ln_vector(dve, 3)
            for m in range(2):
                dve.tensor_scalar(alpha[:, m, :], amax[:, 1, :], fsc[0:S, 1, m:m + 1], None, ALU.mult).then_inc(s["al_rdy"], 1)
            dve.wait_ge(s["al_rdy"], 2)
            dve.sem_inc(s["h_used"], 2)
            dve.sem_inc(s["x4_rdy"], 2)
            NH = 7

            def hidden(b, par):
                link = chain(dve, s["fh_chain"], NH * b)
                for hf in range(2):
                    dve.wait_ge(s["fu_mm"], 2 * b + hf + 1)
                    dve.wait_ge(s["fs_done"], 2 * b + hf + 3)
                    dve.scalar_tensor_tensor(h2[par][:, hf * G:(hf + 1) * G], bank[2 + hf][0:S, :], alpha[:, 1, ds(b, 1)],
                                             g2[par][:, hf * G:(hf + 1) * G], ALU.mult, ALU.mult).then_inc(s["h_used"], 1)
                dve.wait_ge(s["h_used"], 2 * b + 4)
                m = hm[:, par, :]
                link(dve.tensor_reduce(m[:, 0:1], h2[par], AX.X, ALU.max, apply_absolute_value=True))
                link(dve.tensor_scalar(m[:, 0:1], m[:, 0:1], 1e-5, None, ALU.max))
                link(dve.reciprocal(m[:, 1:2], m[:, 0:1]))
                link(dve.tensor_scalar(m[:, 1:2], m[:, 1:2], 127.0, None, ALU.mult))
                link(dve.tensor_scalar(m[:, 2:3], m[:, 0:1], 1.0 / 127.0, fsc[0:S, 1, 2:3], ALU.mult, ALU.mult))
                link(dve.tensor_scalar(h2[par], h2[par], m[:, 1:2], 127.0, ALU.mult, ALU.min))
                link(dve.tensor_scalar(h2[par], h2[par], -128.0, ROUND, ALU.max, ALU.add))
                dve.wait_ge(s["hT_mm"], b + 1)
                dve.tensor_scalar(hq, h2[par], ROUND, None, ALU.subtract).then_inc(s["hq_rdy"], 1)

            def residual4(b, par):
                dve.wait_ge(s["fo_mm"], b + 2)
                dve.scalar_tensor_tensor(row(x, b), bank[6 + par][0:S, 0:D], hm[:, par, 2:3], row(x, b),
                                         ALU.mult, ALU.add).then_inc(s["x4_rdy"], 1)

            hidden(0, 0)
            with dve.Fori(0, NP - 1) as i:
                for par in range(2):
                    hidden(2 * i + par + 1, 1 - par)
                    residual4(2 * i + par, par)
            hidden(B - 1, 1)
            residual4(B - 2, 0)
            residual4(B - 1, 1)


def kernel(**inputs):
    import numpy as _np
    import concourse.bacc as _bacc
    from concourse import mybir as _mybir
    from concourse.bass_utils import run_bass_kernel_spmd as _run

    v = {n: _np.asarray(a) for n, a in inputs.items()}

    def experts(routed, shared):
        e, d, f = routed.shape
        return _np.concatenate([routed.transpose(1, 0, 2).reshape(d, e * f), shared], axis=1)

    laid = {
        "x": v["x"],
        "ctx_t": v["ctx_1024"].transpose(0, 2, 1),
        "mask": v["mask_BxS2_ik0"],
        "wq": v["L0_xattn_Wq"], "wkv": v["L0_xattn_Wkv"], "wout": v["L0_xattn_Wout"], "bout": v["L0_xattn_bout"],
        "wr": v["L0_ffn_W_gate_router"], "ebias": v["L0_ffn_expert_bias"],
        "wg": experts(v["L0_ffn_Wg"], v["L0_ffn_Wg_s"]),
        "wu": experts(v["L0_ffn_Wu"], v["L0_ffn_Wu_s"]),
        "wd": _np.concatenate([v["L0_ffn_Wd"].reshape(-1, v["L0_ffn_Wd"].shape[2]), v["L0_ffn_Wd_s"]], axis=0),
        "ws": v["L1_xattn_Ws"], "w": v["L1_xattn_W"], "wvec": v["L1_xattn_w"], "b": v["L1_xattn_b"],
        "wcw": v["L1_xattn_Wcw"], "bcw": v["L1_xattn_bcw"], "wcb": v["L1_xattn_Wcb"], "bcb": v["L1_xattn_bcb"],
        "fg": v["L1_ffn_w_gate"].T, "fu": v["L1_ffn_w_up"].T, "fd": v["L1_ffn_w_down"].T,
    }
    nc = _bacc.Bacc("TRN2", target_bir_lowering=False, num_devices=1)
    arrays, args = {}, []
    for name, a in laid.items():
        a = _np.ascontiguousarray(a)
        arrays[f"in_{name}_dram"] = a
        args.append(nc.dram_tensor(f"in_{name}_dram", a.shape, _mybir.dt.from_np(a.dtype), kind="ExternalInput").ap())
    shape, dtype = v["x"].shape, v["x"].dtype
    args.append(nc.dram_tensor("out_0_dram", shape, _mybir.dt.from_np(dtype), kind="ExternalOutput").ap())
    bass_xattn_moe_additive_attn_bitlinear_ffn_kernel(nc, *args)
    r = _run(nc, [arrays], core_ids=[0])
    return r.results[0]["out_0_dram"]
```

```python
import concourse.bass as bass
from concourse import mybir
from contextlib import ExitStack


def bass_xattn_moe_additive_attn_bitlinear_ffn_kernel(
    nc, x_in, ctx_t, mask_in, wq_in, wkv_in, wout_in, bout_in, wr_in, ebias_in,
    wg_in, wu_in, wd_in, ws_in, w_in, wvec_in, b_in, wcw_in, bcw_in, wcb_in, bcb_in,
    fg_in, fu_in, fd_in, out,
):
    fp32 = mybir.dt.float32
    bf16 = mybir.dt.bfloat16
    i32 = mybir.dt.int32
    ALU = mybir.AluOpType
    ACT = mybir.ActivationFunctionType
    AX = mybir.AxisListType
    ds = bass.ds

    B, S, D = x_in.shape
    C = ctx_t.shape[2]
    P = 128
    KD = D // P
    INNER = wq_in.shape[1]
    DH = 64
    H = INNER // DH
    HC = INNER // P
    NJ = (C + S - 1) // S
    JR = [min(S, C - j * S) for j in range(NJ)]
    JF = C // S
    E = wr_in.shape[1]
    F = wg_in.shape[1] // (E + 1)
    FT = F * (E + 1)
    FC = (FT + P - 1) // P
    TB = 4
    N4 = TB * S
    NT = B // TB
    G = 512
    FI = fg_in.shape[1]
    FIC = FI // P
    HALF = 4
    HALVES = 4
    UNIT = HALVES * HALF
    NU = (C + UNIT - 1) // UNIT
    CP = NU * UNIT
    PAD = CP - C
    NEG = -1e30
    ROUND = 12582912.0
    EPS = 1e-5
    NP = B // 2

    ctx = ExitStack()
    with ctx:
        def sb(name, shape, dt=fp32):
            return ctx.enter_context(nc.sbuf_tensor(name, shape, dt))

        def sem(name):
            return ctx.enter_context(nc.semaphore(name))

        x = sb("x", [S, B, D])
        lnT = sb("lnT", [P, KD, B * S])
        ident = sb("ident", [P, P])
        ident16 = sb("ident16", [P, P], bf16)
        ones = sb("ones", [P, P])
        headsel = sb("headsel", [P, 2, 4])
        simT = sb("simT", [P, C])
        half = sb("half", [S, B])
        stats = sb("stats", [S, B, 6])
        meanvar = sb("meanvar", [S, B, 2])
        vareps = sb("vareps", [S, B])
        rstd = sb("rstd", [S, B])
        lnN = sb("lnN", [S, 2, D])
        ctxb = sb("ctxb", [P, 2, KD, C])
        att_w = sb("att_w", [P, 6144])
        wq = att_w[:, 0:2048].rearrange("p (k n) -> p k n", k=KD)
        wkv = att_w[:, 2048:6144].rearrange("p (k n) -> p k n", k=KD)
        fw = [att_w[:, 2048 * m:2048 * (m + 1)] for m in range(3)]
        wout = sb("wout", [P, HC, D])
        bout = sb("bout", [S, D])
        big = sb("big", [P, 12800])
        qT = big[:, :].rearrange("p (c n) -> p c n", c=HC)
        wg = big[:, 0:KD * FT].rearrange("p (k n) -> p k n", k=KD)
        wu = big[:, KD * FT:2 * KD * FT].rearrange("p (k n) -> p k n", k=KD)
        wd = big[:, 2 * KD * FT:2 * KD * FT + FC * D].rearrange("p (c n) -> p c n", c=FC)
        HW = KD * HALF * S
        zt = [big[:, HW * m:HW * (m + 1)].rearrange("p (k t f) -> p k t f", k=KD, t=HALF) for m in range(HALVES)]
        ht = [big[:, HW * m:HW * (m + 1)].rearrange("p (k t f) -> p k t f", k=KD, t=HALF) for m in range(HALVES, 2 * HALVES)]
        txtT = [big[:, 6400 + KD * CP * m:6400 + KD * CP * (m + 1)].rearrange("p (k t) -> p k t", k=KD) for m in range(2)]
        o = 6400 + 2 * KD * CP
        cwb = [big[0:S, o + 2 * C * m:o + 2 * C * (m + 1)].rearrange("p (w t) -> p w t", w=2) for m in range(2)]
        o += 4 * C
        assert o <= 12800
        work = sb("work", [P, FC * N4])
        hT = work[:, :].rearrange("p (c n) -> p c n", c=FC)
        prod = [work[:, 2 * C * m:2 * C * (m + 1)].rearrange("p (c n) -> p c n", c=2) for m in range(2)]
        pacc = [work[0:S, 1024 * m:1024 * (m + 1)] for m in range(2)]
        ptmp = [work[0:S, 2048 + 1024 * m:2048 + 1024 * (m + 1)] for m in range(2)]
        oT = work[:, 4096:4096 + HC * S].rearrange("p (c n) -> p c n", c=HC)
        g2 = [work[0:S, 1024 * m:1024 * m + FI] for m in range(2)]
        h2 = [work[0:S, 2048 + 1024 * m:2048 + 1024 * m + FI] for m in range(2)]
        hq = [work[0:S, 4096 + 512 * m:4096 + 512 * (m + 1)].bitcast(bf16) for m in range(1)][0]
        hqT = work[:, 4608:4608 + FIC * S // 2].bitcast(bf16).rearrange("p (c n) -> p c n", c=FIC)
        rho = work[0:S, 0:3 * C].rearrange("p (a t) -> p a t", a=3)
        ee = work[0:S, 3 * C:4 * C]
        lrow = work[:, 4 * C:4 * C + HALF * S]
        sim = sb("sim", [S, B, NJ, H])
        smax = sb("smax", [S, B, H])
        ssum = sb("ssum", [S, B, H])
        wr = sb("wr", [P, KD, E])
        ebias = sb("ebias", [S, E])
        down8 = sb("down8", [S, E])
        down8i = sb("down8i", [S, E], i32)
        rt = sb("rt", [S, 6, B, E])
        rsm = sb("rsm", [S, 3, B])
        gate_w = sb("gate_w", [S, B, E])
        sg = sb("sg", [P, 2, N4])
        wsx = sb("wsx", [P, KD, D])
        wx = sb("wx", [P, KD, D])
        bcol = sb("bcol", [P, KD])
        wvec = sb("wvec", [P, KD])
        wpair = sb("wpair", [P, KD, 3])
        rowsel = sb("rowsel", [P, HALVES])
        wc = sb("wc", [P, 2, KD])
        wcrep = sb("wcrep", [P, 2, KD, S])
        bc = sb("bc", [S, 2])
        featT = sb("featT", [P, KD, B * S])
        mrow = sb("mrow", [B, CP], i32)
        mnz = sb("mnz", [B, CP])
        kflag = sb("kflag", [B, NU])
        kdown = sb("kdown", [B, NU])
        kdowni = sb("kdowni", [B, NU], i32)
        kcount = sb("kcount", [B, 1])
        rowf = sb("rowf", [1, 3, B])
        table = sb("table", [1, 2, B], i32)
        maskb = sb("maskb", [S, 2, C], i32)
        sm = sb("sm", [S, 9])
        xq = sb("xq", [P, KD, B * S], bf16)
        fq = sb("fq", [P, 3, 2048], bf16)
        fsc = sb("fsc", [P, 4, 3])
        amax = sb("amax", [S, 4, B])
        alpha = sb("alpha", [S, 2, B])
        hm = sb("hm", [S, 2, 4])
        xl = big[0:S, 0:B * D].rearrange("p (b d) -> p b d", b=B)

        psum = ctx.enter_context(nc.psum_tensor("psum", [P, 8, G], fp32))
        bank = [psum[:, i, :] for i in range(8)]

        s = {}
        for name in (
            "ld_x0 ld_x1 ld_x2 ld_x3 ld_misc ld_wq ld_wkv ld_wout ld_moe ld_ff ld_ctx0 ld_ctx1 ld_mrow ld_mask0 ld_mask1 st_out ident_rdy "
            "sim_zero act_set wp_rdy const p_chain q_ready q_ev qT_ev k_mm prod_rdy sim_mm sim_tp st_ev sim_ev s_chain max_sub exp_done p_rdy "
            "v_mm v_used pv_done tp_done tp_ev o_mm x1_rdy bo_rdy "
            "r_mm sig_done r_chain gw_rdy g_mm silu_done h_rdy d_mm d_used x2_chain "
            "f_mm f_ev tab_chain tab_rdy t_mm t_ev cw_mm cw_ev rho_zero z_rdy t_done rho_mm rho_tp row_ev "
            "a_chain e_in e_done w_in w_done x3_rdy "
            "fw_mean fw_bc fw_chain fw_rdy fg_mm fu_mm fs_done fh_chain hq_rdy hT_mm hT_ev fo_mm x4_rdy h_used "
            "c_in c_done ctx_x cnt_mm cnt_in d8 al_rdy").split():
            s[name] = sem(name)
        lns = [{k: sem(f"ln{n}_{k}") for k in ("stat", "rstd", "x", "T", "ev", "ch", "pch")} for n in range(4)]

        block = ctx.enter_context(nc.Block())

        def sum_of(b, par, u, hf):
            return (zt[hf], featT[:, :, ds(b * S, S)].unsqueeze(2).broadcast_to([P, KD, HALF, S]),
                    txtT[par][:, :, ds(u * UNIT + hf * HALF, HALF)].unsqueeze(3).broadcast_to([P, KD, HALF, S]))

        def row(t, b):
            return t[:, ds(b, 1), :].rearrange("p a d -> p (a d)")

        def chain(eng, sm_, base=0):
            n = [0]

            def link(ins):
                n[0] += 1
                ins.then_inc(sm_, 1)
                eng.wait_ge(sm_, base + n[0])
            return link

        def ln_stats(dve, n, b):
            dve.bn_stats(row(stats, b), row(x, b)).then_inc(lns[n]["ch"], 1)

        def ln_vector(dve, n):
            q = lns[n]
            if n == 0:
                for b in range(B):
                    if b % 4 == 0:
                        dve.wait_ge(s[f"ld_x{b // 4}"], 16)
                    ln_stats(dve, n, b)
            for b in range(B):
                dve.wait_ge(q["ch"], b + 1)
                dve.bn_aggr(meanvar[:, b, :], stats[:, b, :]).then_inc(q["stat"], 1)
            dve.wait_ge(q["stat"], B)
            dve.wait_ge(q["rstd"], 1)
            if n == 3:
                with dve.Fori(0, B) as b:
                    dve.tensor_scalar(row(xl, b), row(x, b),
                                      meanvar[:, ds(b, 1), 0:1].rearrange("p a s -> p (a s)"), rstd[:, ds(b, 1)],
                                      ALU.subtract, ALU.mult).then_inc(q["ch"], 1)
                dve.wait_ge(q["ch"], 2 * B)
                link = chain(dve, q["ch"], 2 * B)
                link(dve.tensor_reduce(amax[:, 0, :], xl[:, :, :], AX.X, ALU.max, apply_absolute_value=True))
                link(dve.tensor_scalar(amax[:, 1, :], amax[:, 0, :], 1e-5, None, ALU.max))
                link(dve.reciprocal(amax[:, 2, :], amax[:, 1, :]))
                link(dve.tensor_scalar(amax[:, 2, :], amax[:, 2, :], 127.0, None, ALU.mult))
                link(dve.tensor_scalar(amax[:, 1, :], amax[:, 1, :], 1.0 / 127.0, None, ALU.mult))
                with dve.Fori(0, NP) as i:
                    for par in range(2):
                        b = 2 * i + par
                        xb = row(xl, b)
                        base = 2 * B + 5 + 4 * i + 2 * par
                        dve.tensor_scalar(xb, xb, amax[:, 2, ds(b, 1)], 127.0, ALU.mult, ALU.min).then_inc(q["ch"], 1)
                        dve.wait_ge(q["ch"], base + 1)
                        dve.tensor_scalar(xb, xb, -128.0, ROUND, ALU.max, ALU.add).then_inc(q["ch"], 1)
                        dve.wait_ge(q["ch"], base + 2)
                        dve.wait_ge(q["T"], b + 1)
                        dve.tensor_scalar(lnN[:, par, :], xb, ROUND, None, ALU.subtract).then_inc(q["x"], 1)
            else:
                with dve.Fori(0, NP) as i:
                    for par in range(2):
                        b = 2 * i + par
                        dve.wait_ge(q["T"], b + 1)
                        dve.tensor_scalar(lnN[:, par, :], row(x, b),
                                          meanvar[:, ds(b, 1), 0:1].rearrange("p a s -> p (a s)"), rstd[:, ds(b, 1)],
                                          ALU.subtract, ALU.mult).then_inc(q["x"], 1)

        def ln_gpsimd(pool, n):
            q = lns[n]
            pool.wait_ge(q["stat"], B)
            pool.tensor_scalar(vareps[:, :], meanvar[:, :, 1], EPS, None, ALU.add).then_inc(q["pch"], 1)
            pool.wait_ge(q["pch"], 1)
            pool.tensor_tensor(rstd[:, :], vareps[:, :], half[:, :], ALU.pow).then_inc(q["rstd"], 1)

        def ln_tensor(pe, n):
            q = lns[n]
            pe.sem_inc(q["T"], 2)
            with pe.Fori(0, NP) as i:
                for par in range(2):
                    b = 2 * i + par
                    pe.wait_ge(q["x"], b + 1)
                    pe.wait_ge(q["ev"], b + 1)
                    for k in range(KD):
                        last = pe.transpose(bank[6 + par][:, k * S:(k + 1) * S],
                                            lnN[:, par, k * P:(k + 1) * P], ident[0:S, 0:S])
                    last.then_inc(q["T"], 1)

        def ln_scalar(act, n):
            q = lns[n]
            dst = xq if n == 3 else lnT
            act.sem_inc(q["ev"], 2)
            with act.Fori(0, NP) as i:
                for par in range(2):
                    b = 2 * i + par
                    act.wait_ge(q["T"], b + 3)
                    act.activation(dst[:, :, ds(b * S, S)],
                                   bank[6 + par][:, 0:KD * S].rearrange("p (k s) -> p k s", k=KD),
                                   ACT.Copy).then_inc(q["ev"], 1)

        def ln_done(eng, n):
            eng.wait_ge(lns[n]["ev"], B + 2)

        @block.sync
        def _(sp):
            for g in range(0, B, 4):
                sp.dma_start(x[:, g:g + 4, :], x_in[g:g + 4].rearrange("b s d -> s b d")).then_inc(s[f"ld_x{g // 4}"], 16)
            sp.dma_start(wq, wq_in.rearrange("(k p) n -> p k n", p=P)).then_inc(s["ld_wq"], 16)
            sp.dma_start(wkv, wkv_in.rearrange("(k p) n -> p k n", p=P)).then_inc(s["ld_wkv"], 16)

            def load_ctx(b, par, used, count):
                if used is not None:
                    sp.wait_ge(used, count)
                sp.dma_start(ctxb[:, par, :, :], ctx_t[ds(b, 1), :, :].rearrange("a (k p) c -> p (a k) c", p=P)
                             ).then_inc(s[f"ld_ctx{par}"], 16)
            load_ctx(0, 0, None, 0)
            load_ctx(1, 1, None, 0)
            sp.dma_start(wout[:, :, :], wout_in.rearrange("(c p) n -> p c n", p=P)).then_inc(s["ld_wout"], 16)
            with sp.Fori(1, NP) as i:
                for par in range(2):
                    load_ctx(2 * i + par, par, s["k_mm"], HC // 2 * (2 * i + par - 1))
            sp.wait_ge(s["k_mm"], HC // 2 * B)
            load_ctx(0, 0, None, 0)
            load_ctx(1, 1, None, 0)
            sp.wait_ge(s["prod_rdy"], B * (HC // 2) + 2)
            sp.dma_start(wg, wg_in.rearrange("(k p) n -> p k n", p=P)).then_inc(s["ld_moe"], 16)
            sp.dma_start(wu, wu_in.rearrange("(k p) n -> p k n", p=P)).then_inc(s["ld_moe"], 16)
            with sp.Fori(1, NP) as i:
                for par in range(2):
                    load_ctx(2 * i + par, par, s["v_mm"], NJ * (2 * i + par - 1))
            full = FT // P
            sp.dma_start(wd[:, 0:full, :], wd_in[0:full * P].rearrange("(c p) n -> p c n", p=P)).then_inc(s["ld_moe"], 16)
            sp.dma_start(wd[0:FT - full * P, full, :], wd_in[full * P:FT, :]).then_inc(s["ld_moe"], 16)
            sp.wait_ge(s["v_mm"], NJ * B)

            def load_mask(b, par):
                sp.dma_start(maskb[:, par, :], mask_in[ds(b, 1), :].broadcast_to([S, C])
                             ).then_inc(s[f"ld_mask{par}"], 16)
            for par in range(2):
                load_ctx(par, par, None, 0)
                load_mask(par, par)
            sp.dma_start(fw[0].rearrange("p (k n) -> p k n", k=KD), fg_in.rearrange("(k p) n -> p k n", p=P)).then_inc(s["ld_ff"], 16)
            sp.dma_start(fw[1].rearrange("p (k n) -> p k n", k=KD), fu_in.rearrange("(k p) n -> p k n", p=P)).then_inc(s["ld_ff"], 16)
            sp.dma_start(fw[2].rearrange("p (k n) -> p k n", k=FIC), fd_in.rearrange("(k p) n -> p k n", p=P)).then_inc(s["ld_ff"], 16)
            with sp.Fori(1, NP) as i:
                for par in range(2):
                    b = 2 * i + par
                    load_ctx(b, par, s["ctx_x"], b - 1)
                    sp.wait_ge(s["e_in"], b + 1)
                    load_mask(b, par)
            with sp.Fori(0, NP) as i:
                sp.wait_ge(s["x4_rdy"], 2 * i + 4)
                sp.dma_start(out[ds(2 * i, 2)].rearrange("b s d -> s b d"), x[:, ds(2 * i, 2), :]).then_inc(s["st_out"], 16)
            sp.wait_ge(s["st_out"], 16 * NP)

        @block.gpsimd
        def _(pool):
            link = chain(pool, s["p_chain"])
            link(pool.memset(ident[:, :], 0.0))
            pool.affine_select(out=ident[:, :], in_=ident[:, :], compare_op=ALU.not_equal, fill=1.0,
                               base=0, pattern=[[-1, P]], channel_multiplier=1).then_inc(s["ident_rdy"], 1)
            pool.wait_ge(s["ident_rdy"], 1)
            link(pool.memset(half[:, :], -0.5))
            link(pool.memset(ones[:, :], 1.0))
            link(pool.memset(rowsel[:, :], 0.0))
            for n in range(4):
                link(pool.affine_select(out=rowsel[32 * n:32 * n + 2, n // 2::2], in_=rowsel[32 * n:32 * n + 2, n // 2::2],
                                        compare_op=ALU.not_equal, fill=1.0, base=0, pattern=[[-1, 2]],
                                        channel_multiplier=1))
            link(pool.memset(headsel[:, :, :], 0.0))
            link(pool.memset(headsel[0:DH, 0, 0:1], 1.0))
            link(pool.memset(headsel[0:DH, 1, 2:3], 1.0))
            link(pool.memset(headsel[DH:P, 1, 3:4], 1.0))
            link(pool.memset(mrow[:, 0:PAD], 0))
            link(pool.iota(kdowni[:, :], pattern=[[-1, NU]], base=NU, channel_multiplier=0))
            link(pool.iota(down8i[:, :], pattern=[[-1, E]], base=E, channel_multiplier=0))
            pool.memset(headsel[DH:P, 0, 1:2], 1.0).then_inc(s["const"], 1)
            pool.dma_start(mrow[:, PAD:CP], mask_in).then_inc(s["ld_mrow"], 16)
            small = [(wr[:, :, :], wr_in.rearrange("(k p) n -> p k n", p=P)),
                     (ebias[:, :], ebias_in.rearrange("(a n) -> a n", a=1).broadcast_to([S, E])),
                     (bout[:, :], bout_in.rearrange("(a n) -> a n", a=1).broadcast_to([S, D])),
                     (wsx[:, :, :], ws_in.rearrange("(k p) n -> p k n", p=P)),
                     (wx[:, :, :], w_in.rearrange("(k p) n -> p k n", p=P)),
                     (bc[:, 0:1], bcw_in.rearrange("(a n) -> a n", a=1).broadcast_to([S, 1])),
                     (bc[:, 1:2], bcb_in.rearrange("(a n) -> a n", a=1).broadcast_to([S, 1]))]
            for dst, src in small:
                pool.dma_start(dst, src).then_inc(s["ld_misc"], 16)
            with nc.allow_non_contiguous_dma(reason="256 values each, once"):
                for dst, src in ((bcol[:, :], b_in.rearrange("a (k p) -> p (a k)", p=P)),
                                 (wvec[:, :], wvec_in.rearrange("(k p) a -> p (k a)", p=P)),
                                 (wc[:, 0, :], wcw_in.rearrange("a (k p) -> p (a k)", p=P)),
                                 (wc[:, 1, :], wcb_in.rearrange("a (k p) -> p (a k)", p=P))):
                    pool.dma_start(dst, src).then_inc(s["ld_misc"], 16)
            pool.wait_ge(s["const"], 1)
            ln_gpsimd(pool, 0)
            pool.wait_ge(s["ld_misc"], 16 * 11)
            pool.wait_ge(lns[0]["x"], B)
            pool.tensor_tensor(x[:, :, :], x[:, :, :], bout[:, :].unsqueeze(1).broadcast_to([S, B, D]), ALU.add
                               ).then_inc(s["bo_rdy"], 1)
            pool.sem_inc(s["pv_done"], 2)
            with pool.Fori(0, NP) as i:
                for par in range(2):
                    b = 2 * i + par
                    for j in range(1, NJ):
                        n = JR[j]
                        pool.wait_ge(s["v_used"], NJ * b + j + 3)
                        if j > 1:
                            pool.wait_ge(s["pv_done"], (NJ - 1) * b + j + 1)
                        pool.tensor_tensor(pacc[par][0:n, :], pacc[par][0:n, :], ptmp[(par * (NJ - 1) + j - 1) % 2][0:n, :],
                                           ALU.add).then_inc(s["pv_done"], 1)
            ln_gpsimd(pool, 1)
            ln_gpsimd(pool, 2)
            ln_gpsimd(pool, 3)

        @block.tensor
        def _(pe):
            pe.wait_ge(s["ident_rdy"], 1)
            ln_tensor(pe, 0)
            ln_done(pe, 0)
            pe.wait_ge(s["ld_wq"], 16)
            with pe.Fori(0, NT) as t:
                for c in range(HC):
                    pe.wait_ge(s["q_ev"], t * HC + c + 1)
                    for k in range(KD):
                        last = pe.matmul(bank[c % 2][:, 0:N4], wq[:, k, c * P:(c + 1) * P],
                                         lnT[:, k, ds(t * N4, N4)], start=(k == 0), stop=(k == KD - 1))
                    last.then_inc(s["q_ready"], 1)
            pe.wait_ge(s["cnt_in"], 1)
            pe.transpose(bank[5][0:1, 0:B], kcount[:, :], ident[0:B, 0:B]).then_inc(s["cnt_mm"], 1)
            pe.wait_ge(s["ld_wkv"], 16)
            pe.wait_ge(s["const"], 1)
            pe.wait_ge(s["q_ev"], NT * HC + 2)

            def sims(b, par, m, turn):
                pe.wait_ge(s["prod_rdy"], (HC // 2) * b + m + 3)
                if m == 0:
                    pe.wait_ge(s["st_ev"], b + 1)
                for u in range(2):
                    c = 2 * m + u
                    n = 32 * (c % 4)
                    last = pe.matmul(bank[4 + par][n:n + 4, 0:C], headsel[:, c // 4, :], prod[m % 2][:, u, :],
                                     start=(c < 4), stop=(c >= 4), skip_group_check=True)
                last.then_inc(s["sim_mm"], 1)
                if m == 1 and turn:
                    turn_sims(b - 1)

            def turn_sims(b):
                pe.wait_ge(s["st_ev"], b + 3)
                pe.wait_ge(s["sim_ev"], b + 1)
                for j in range(NJ):
                    last = pe.transpose(bank[6][0:JR[j], j * P:(j + 1) * P], simT[:, j * S:j * S + JR[j]], ident[:, :])
                last.then_inc(s["sim_tp"], 1)

            pe.wait_ge(s["sim_zero"], 2)
            pe.sem_inc(s["sim_mm"], 2)

            def keys(b, par, m, i):
                if m == 0:
                    pe.wait_ge(s[f"ld_ctx{par}"], 16 * i + 16)
                pe.wait_ge(s["prod_rdy"], (HC // 2) * b + m + 1)
                for u in range(2):
                    c = 2 * m + u
                    for k in range(KD):
                        last = pe.matmul(bank[2 * (m % 2) + u][:, 0:C], wkv[:, k, c * P:(c + 1) * P],
                                         ctxb[:, par, k, :], start=(k == 0), stop=(k == KD - 1))
                last.then_inc(s["k_mm"], 1)

            def keys_and_sims(b, par, i, more=True, turn=True):
                for m in range(HC // 2):
                    if m < HC // 2 - 1:
                        keys(b, par, m + 1, i)
                    elif more:
                        keys(b + 1, 1 - par, 0, i + par)
                    sims(b, par, m, turn)

            keys(0, 0, 0, 0)
            keys_and_sims(0, 0, 0, turn=False)
            with pe.Fori(0, NP - 1) as i:
                keys_and_sims(2 * i + 1, 1, i)
                keys_and_sims(2 * i + 2, 0, i + 1)
            keys_and_sims(B - 1, 1, NP - 1, more=False)
            turn_sims(B - 1)
            pe.wait_ge(s["sim_ev"], B + 1)

            def values(b, par, i):
                pe.wait_ge(s[f"ld_ctx{par}"], 16 * (B // 2) + 16 * i + 16)
                for j in range(NJ):
                    pe.wait_ge(s["v_used"], NJ * b + j + 1)
                    for n in range(2):
                        for k in range(KD):
                            last = pe.matmul(bank[2 * (j % 2) + n][0:JR[j], :], ctxb[:, par, k, j * S:j * S + JR[j]],
                                             wkv[:, k, INNER + n * G:INNER + (n + 1) * G],
                                             start=(k == 0), stop=(k == KD - 1))
                    last.then_inc(s["v_mm"], 1)

            def project(b, par):
                pe.wait_ge(s["pv_done"], (NJ - 1) * (b + 1) + 2)
                for c in range(HC):
                    if c % 4 == 0:
                        pe.wait_ge(s["tp_ev"], 2 * b + c // 4 + 1)
                    last = pe.transpose(bank[4 + c // 4][:, (c % 4) * S:(c % 4 + 1) * S],
                                        pacc[par][:, c * P:(c + 1) * P], ident[0:S, 0:S])
                    if c % 4 == 3:
                        last.then_inc(s["tp_done"], 1)
                pe.wait_ge(s["tp_ev"], 2 * b + 4)
                pe.wait_ge(s["x1_rdy"], b + 1)
                for c in range(HC):
                    last = pe.matmul(bank[6 + par][0:S, 0:D], oT[:, c, :], wout[:, c, :],
                                     start=(c == 0), stop=(c == HC - 1))
                last.then_inc(s["o_mm"], 1)

            pe.wait_ge(s["ld_wout"], 16)
            pe.sem_inc(s["tp_done"], 4)
            pe.sem_inc(s["o_mm"], 1)
            values(0, 0, 0)
            with pe.Fori(0, NP - 1) as i:
                for par in range(2):
                    b = 2 * i + par
                    values(b + 1, 1 - par, i + par)
                    project(b, par)
            values(B - 1, 1, NP - 1)
            project(B - 2, 0)
            project(B - 1, 1)

            pe.wait_ge(s["x1_rdy"], B + 2)
            ln_tensor(pe, 1)
            ln_done(pe, 1)
            for b in range(B):
                for k in range(KD):
                    last = pe.matmul(bank[7][0:S, b * E:(b + 1) * E], lnT[:, k, b * S:(b + 1) * S], wr[:, k, :],
                                     start=(k == 0), stop=(k == KD - 1))
            last.then_inc(s["r_mm"], 1)
            pe.wait_ge(s["ld_moe"], 64)
            with pe.Fori(0, NT) as t:
                for c in range(FC):
                    w = min(P, FT - c * P)
                    before = pe.to_reg(t * FC + c + 1)
                    if w < P:
                        pe.wait_ge(s["ld_moe"], 64)
                    pe.wait_ge(s["h_rdy"], before)
                    for bk, wgt in ((0, wg), (2, wu)):
                        for k in range(KD):
                            last = pe.matmul(bank[bk + c % 2][0:w, 0:N4], wgt[:, k, c * P:c * P + w],
                                             lnT[:, k, ds(t * N4, N4)], start=(k == 0), stop=(k == KD - 1))
                    last.then_inc(s["g_mm"], 1)
                pe.wait_ge(s["h_rdy"], t * FC + FC + 2)
                for lb in range(TB):
                    for n, e in enumerate([E] + list(range(E))):
                        parts = [(3 * (e // 2), 0, P), (3 * (e // 2) + 1, 0, P // 2)] if e % 2 == 0 else \
                                [(3 * (e // 2) + 1, P // 2, P), (3 * (e // 2) + 2, 0, P)]
                        slot = (lb * (E + 1) + n) % 4
                        pe.wait_ge(s["d_used"], t * TB * (E + 1) + lb * (E + 1) + n + 1)
                        for q, (c, lo, hi) in enumerate(parts):
                            last = pe.matmul(bank[4 + slot][0:S, 0:D], hT[lo:hi, c, lb * S:(lb + 1) * S],
                                             wd[lo:hi, c, :], start=(q == 0), stop=(q == 1))
                        last.then_inc(s["d_mm"], 1)

            pe.wait_ge(s["d_used"], NT * TB * (E + 1) + 4)
            ln_tensor(pe, 2)
            ln_done(pe, 2)
            with pe.Fori(0, NT) as t:
                for m in range(KD):
                    pe.wait_ge(s["f_ev"], t * KD + m + 1)
                    for k in range(KD):
                        last = pe.matmul(bank[m][:, 0:N4], wx[:, k, m * P:(m + 1) * P], lnT[:, k, ds(t * N4, N4)],
                                         start=(k == 0), stop=(k == KD - 1))
                    last.then_inc(s["f_mm"], 1)
            pe.wait_ge(s["f_ev"], NT * KD + 2)

            def project_ctx(b, par, i):
                pe.wait_ge(s[f"ld_ctx{par}"], 2 * 16 * (B // 2) + 16 * i + 16)
                pe.wait_ge(s["t_ev"], b + 1)
                for m in range(KD):
                    for k in range(KD):
                        last = pe.matmul(bank[m][:, 0:C], wsx[:, k, m * P:(m + 1) * P], ctxb[:, par, k, :],
                                         start=(k == 0), stop=(k == KD - 1))
                last.then_inc(s["t_mm"], 1)
                pe.wait_ge(s["cw_ev"], b + 1)
                for m in range(2):
                    for k in range(KD):
                        last = pe.matmul(bank[2 + m][0:S, 0:C], wcrep[:, m, k, :], ctxb[:, par, k, :],
                                         start=(k == 0), stop=(k == KD - 1))
                last.then_inc(s["ctx_x"], 1)

            def logits(unit, h):
                pe.wait_ge(s["t_done"], HALVES * unit + h + HALVES + 1)
                if h == 0:
                    pe.wait_ge(s["row_ev"], unit + 1)
                for k in range(KD):
                    n = 32 * (KD * (h % 2) + k)
                    last = pe.matmul(bank[4][n:n + 2, 0:HALF * S], wpair[:, k, 1 - h // 2:3 - h // 2],
                                     ht[h][:, k, :, :], start=(h < 2), stop=(h >= 2), skip_group_check=True)
                last.then_inc(s["rho_mm"], 1)

            def turn_logits(unit, u, par):
                pe.wait_ge(s["row_ev"], unit + 2)
                turned = bank[6 + par][0:S, 0:CP].rearrange("p (u h t) -> p u t h", h=HALVES, t=HALF)
                for t in range(HALF):
                    last = pe.matmul(turned[:, ds(u, 1), t, :].rearrange("p a h -> p (a h)"),
                                     lrow[:, t * S:(t + 1) * S], rowsel[:, :], start=True, stop=True)
                last.then_inc(s["rho_tp"], 1)

            def all_logits(b, par):
                first = pe.value_load(table[0:1, 0, ds(b, 1)], min_val=0, max_val=NU - 1)
                ends = pe.value_load(table[0:1, 1, ds(b, 1)], min_val=1, max_val=B * NU)
                this = pe.to_reg(b + 1)
                pe.wait_ge(s["tab_rdy"], 1)
                pe.wait_ge(s["e_in"], this)
                with pe.Fori(first, NU) as u:
                    for h in range(1, HALVES):
                        logits(ends + u, h)
                    logits(ends + u + 1, 0)
                    turn_logits(ends + u, u, par)

            pe.wait_ge(s["fw_mean"], 3)
            pe.matmul(bank[7][:, 0:3], ones[:, :], fsc[:, 0, :], start=True, stop=True).then_inc(s["fw_bc"], 1)
            pe.wait_ge(s["tab_rdy"], 1)
            pe.wait_ge(s["rho_zero"], 1)
            pe.wait_ge(s["c_done"], 1)
            pe.wait_ge(s["wp_rdy"], 2)
            pe.sem_inc(s["rho_tp"], NU + 1)
            pe.sem_inc(s["rho_mm"], HALVES * (NU + 1))
            project_ctx(0, 0, 0)
            logits(NU, 0)
            with pe.Fori(0, NP - 1) as i:
                for par in range(2):
                    b = 2 * i + par
                    project_ctx(b + 1, 1 - par, i + par)
                    all_logits(b, par)
            project_ctx(B - 1, 1, NP - 1)
            all_logits(B - 2, 0)
            all_logits(B - 1, 1)

            pe.wait_ge(s["x3_rdy"], B + 2)
            ln_tensor(pe, 3)
            ln_done(pe, 3)
            pe.wait_ge(s["fw_rdy"], 9)
            pe.sem_inc(s["hT_mm"], 1)
            pe.sem_inc(s["fo_mm"], 1)

            def up(b):
                for hf in range(2):
                    for m, (bk, used) in enumerate(((0, "fs_done"), (2, "h_used"))):
                        pe.wait_ge(s[used], 2 * b + hf + 1)
                        for k in range(KD):
                            last = pe.matmul(bank[bk + hf][0:S, :], xq[:, k, ds(b * S, S)],
                                             fq[:, m, k * FI + hf * G:k * FI + (hf + 1) * G],
                                             start=(k == 0), stop=(k == KD - 1))
                        last.then_inc(s["fg_mm" if m == 0 else "fu_mm"], 1)

            def down(b, par):
                pe.wait_ge(s["hq_rdy"], b + 1)
                pe.wait_ge(s["hT_ev"], b + 1)
                for c in range(FIC):
                    last = pe.transpose(bank[4].bitcast(bf16)[:, c * S:(c + 1) * S],
                                        hq[:, c * P:(c + 1) * P], ident16[0:S, 0:S])
                last.then_inc(s["hT_mm"], 1)
                pe.wait_ge(s["hT_ev"], b + 2)
                pe.wait_ge(s["x4_rdy"], b + 1)
                for c in range(FIC):
                    last = pe.matmul(bank[6 + par][0:S, 0:D], hqT[:, c, :], fq[:, 2, c * D:(c + 1) * D],
                                     start=(c == 0), stop=(c == FIC - 1))
                last.then_inc(s["fo_mm"], 1)

            up(0)
            with pe.Fori(0, NP - 1) as i:
                for par in range(2):
                    up(2 * i + par + 1)
                    down(2 * i + par, par)
            up(B - 1)
            down(B - 2, 0)
            down(B - 1, 1)

        @block.scalar
        def _(act):
            act.wait_ge(s["const"], 1)
            act.activation(sm[:, 7:8], half[:, 0:1], ACT.Copy).then_inc(s["act_set"], 1)
            act.wait_ge(s["act_set"], 1)
            ln_scalar(act, 0)
            act.sem_inc(s["q_ev"], 2)
            with act.Fori(0, NT) as t:
                for c in range(HC):
                    act.wait_ge(s["q_ready"], t * HC + c + 1)
                    act.activation(qT[:, c, ds(t * N4, N4)], bank[c % 2][:, 0:N4], ACT.Copy, scale=DH ** -0.5
                                   ).then_inc(s["q_ev"], 1)
            act.sem_inc(s["st_ev"], 2)
            with act.Fori(0, NP) as i:
                for par in range(2):
                    b = 2 * i + par
                    act.wait_ge(s["sim_mm"], (HC // 2) * (b + 1) + 2)
                    act.wait_ge(s["sim_ev"], b + 1)
                    act.activation(simT[:, :], bank[4 + par][:, 0:C], ACT.Copy).then_inc(s["st_ev"], 1)
            act.wait_ge(s["max_sub"], 1)
            act.activation(sim[:, :, :, :], sim[:, :, :, :], ACT.Exp).then_inc(s["exp_done"], 1)
            act.sem_inc(s["tp_ev"], 2)
            with act.Fori(0, B) as b:
                act.wait_ge(s["o_mm"], b + 1)
                for hf in range(2):
                    act.wait_ge(s["tp_done"], 2 * b + hf + 5)
                    act.activation(oT[:, 4 * hf:4 * hf + 4, :],
                                   bank[4 + hf][:, 0:4 * S].rearrange("p (c n) -> p c n", c=4), ACT.Copy
                                   ).then_inc(s["tp_ev"], 1)
            ln_scalar(act, 1)
            act.wait_ge(s["r_mm"], 1)
            act.activation(rt[:, 0, :, :], bank[7][0:S, 0:B * E].rearrange("p (b e) -> p b e", b=B), ACT.Sigmoid
                           ).then_inc(s["sig_done"], 1)
            act.activation(sm[:, 7:8], half[:, 0:1], ACT.Silu).then_inc(s["act_set"], 1)
            act.wait_ge(s["act_set"], 2)
            with act.Fori(0, NT) as t:
                for c in range(FC):
                    w = min(P, FT - c * P)
                    act.wait_ge(s["g_mm"], t * FC + c + 1)
                    act.wait_ge(s["h_rdy"], t * FC + c + 1)
                    act.activation(sg[0:w, c % 2, :], bank[c % 2][0:w, 0:N4], ACT.Silu).then_inc(s["silu_done"], 1)
            ln_scalar(act, 2)
            act.sem_inc(s["f_ev"], 2)
            act.sem_inc(s["t_ev"], 1)
            act.sem_inc(s["cw_ev"], 1)
            act.sem_inc(s["row_ev"], NU)
            act.sem_inc(s["t_done"], HALVES * (NU + 1))
            act.wait_ge(s["ld_misc"], 16 * 11)
            with act.Fori(0, NT) as t:
                for m in range(KD):
                    act.wait_ge(s["f_mm"], t * KD + m + 1)
                    act.activation(featT[:, m, ds(t * N4, N4)], bank[m][:, 0:N4], ACT.Identity, bias=bcol[:, m:m + 1]
                                   ).then_inc(s["f_ev"], 1)

            def copy_txt(b, par):
                act.wait_ge(s["t_mm"], b + 1)
                act.activation(txtT[par][:, :, PAD:CP], psum[:, 0:KD, 0:C], ACT.Copy).then_inc(s["t_ev"], 1)

            def copy_cw(b, par):
                act.wait_ge(s["ctx_x"], b + 1)
                act.activation(cwb[par], psum[0:S, 2:4, 0:C], ACT.Copy).then_inc(s["cw_ev"], 1)

            def copy_rows(unit):
                act.wait_ge(s["rho_mm"], HALVES * unit + 2 * HALVES)
                act.wait_ge(s["rho_tp"], unit + 1)
                act.activation(lrow, bank[4][:, 0:HALF * S], ACT.Copy).then_inc(s["row_ev"], 1)

            def tanhs(b):
                first = act.value_load(table[0:1, 0, ds(b, 1)], min_val=0, max_val=NU - 1)
                ends = act.value_load(table[0:1, 1, ds(b, 1)], min_val=1, max_val=B * NU)
                with act.Fori(first, NU) as u:
                    for h in range(HALVES):
                        q = HALVES * (ends + u) + h
                        act.wait_ge(s["z_rdy"], q + HALVES + 1)
                        act.wait_ge(s["rho_mm"], q + 1)
                        act.activation(ht[h], zt[h], ACT.Tanh).then_inc(s["t_done"], 1)
                        if h == 0:
                            copy_rows(ends + u - 1)

            def exps(b):
                act.wait_ge(s["e_in"], b + 3)
                act.activation(ee[:, :], rho[:, 1, :], ACT.Exp, bias=sm[:, 0:1], accum_out=sm[:, 1:2]
                               ).then_inc(s["e_done"], 1)

            def weights(b):
                act.wait_ge(s["w_in"], b + 1)
                for m in range(2):
                    last = act.activation(sm[:, 5 + m:6 + m], sm[:, 2 + m:3 + m], ACT.Tanh,
                                          bias=bc[:, m:m + 1], scale=sm[:, 4:5])
                last.then_inc(s["w_done"], 1)

            act.activation(sm[:, 7:8], half[:, 0:1], ACT.Exp).then_inc(s["act_set"], 1)
            act.wait_ge(s["rho_zero"], 1)
            for b in range(2):
                copy_txt(b, b)
                copy_cw(b, b)
                tanhs(b)
            with act.Fori(0, NP - 1) as i:
                for par in range(2):
                    b = 2 * i + par
                    exps(b)
                    copy_txt(b + 2, par)
                    weights(b)
                    copy_cw(b + 2, par)
                    tanhs(b + 2)
            ends = act.value_load(table[0:1, 1, B - 1:B], min_val=1, max_val=B * NU)
            copy_rows(ends + NU - 1)
            act.sem_inc(s["t_done"], 1)
            for b in (B - 2, B - 1):
                exps(b)
                weights(b)
            ln_scalar(act, 3)
            act.wait_ge(s["al_rdy"], 2)
            act.sem_inc(s["fs_done"], 2)
            act.sem_inc(s["hT_ev"], 1)

            def gate(b, par):
                for hf in range(2):
                    this = act.to_reg(2 * b + hf + 1)
                    act.wait_ge(s["al_rdy"], 2)
                    act.wait_ge(s["fg_mm"], this)
                    act.wait_ge(s["h_used"], this)
                    act.activation(g2[par][:, hf * G:(hf + 1) * G], bank[hf][0:S, :], ACT.Silu,
                                   scale=alpha[:, 0, ds(b, 1)]).then_inc(s["fs_done"], 1)

            def copy_h(b):
                act.wait_ge(s["hT_mm"], b + 2)
                act.wait_ge(s["fo_mm"], b + 1)
                act.activation(hqT, bank[4].bitcast(bf16)[:, 0:FIC * S].rearrange("p (c n) -> p c n", c=FIC),
                               ACT.Copy).then_inc(s["hT_ev"], 1)

            gate(0, 0)
            with act.Fori(0, NP - 1) as i:
                for par in range(2):
                    gate(2 * i + par + 1, 1 - par)
                    copy_h(2 * i + par)
            gate(B - 1, 1)
            copy_h(B - 2)
            copy_h(B - 1)

        @block.vector
        def _(dve):
            ln_vector(dve, 0)
            link = chain(dve, s["tab_chain"])
            dve.wait_ge(s["ld_mrow"], 16)
            dve.wait_ge(s["const"], 1)
            link(dve.tensor_copy(kdown[:, :], kdowni[:, :]))
            link(dve.tensor_scalar(mnz[:, :], mrow[:, :], 0.0, None, ALU.not_equal))
            link(dve.tensor_reduce(kflag[:, :], mnz[:, :].rearrange("p (u t) -> p u t", t=UNIT), AX.X, ALU.max))
            link(dve.tensor_tensor(kflag[:, :], kflag[:, :], kdown[:, :], ALU.mult))
            link(dve.tensor_reduce(kcount[:, :], kflag[:, :], AX.X, ALU.max))
            dve.tensor_scalar(kcount[:, :], kcount[:, :], 1.0, None, ALU.max).then_inc(s["cnt_in"], 1)
            dve.tensor_copy(ident16[:, :], ident[:, :]).then_inc(s["d8"], 1)
            dve.tensor_copy(down8[:, :], down8i[:, :]).then_inc(s["d8"], 1)
            dve.wait_ge(s["cnt_mm"], 1)
            link(dve.tensor_copy(rowf[:, 0, :], bank[5][0:1, 0:B]))
            link(dve.tensor_tensor_scan(rowf[:, 1, :], ones[0:1, 0:B], rowf[:, 0, :], 0.0, ALU.mult, ALU.add))
            link(dve.tensor_scalar(rowf[:, 2, :], rowf[:, 0, :], -1.0, float(NU), ALU.mult, ALU.add))
            link(dve.tensor_copy(table[:, 0, :], rowf[:, 2, :]))
            dve.tensor_copy(table[:, 1, :], rowf[:, 1, :]).then_inc(s["tab_rdy"], 1)
            dve.wait_ge(s["ld_misc"], 16 * 11)
            dve.tensor_copy(wcrep[:, :, :, :], wc[:, :, :].unsqueeze(3).broadcast_to([P, 2, KD, S])
                            ).then_inc(s["c_done"], 1)
            dve.memset(wpair[:, :, :], 0.0).then_inc(s["wp_rdy"], 1)
            dve.wait_ge(s["wp_rdy"], 1)
            dve.tensor_copy(wpair[:, :, 1], wvec[:, :]).then_inc(s["wp_rdy"], 1)
            dve.memset(sim[:, :, NJ - 1, :], NEG).then_inc(s["s_chain"], 1)
            dve.wait_ge(s["s_chain"], 1)
            for n in (4, 5):
                dve.memset(bank[n][:, 0:C], 0.0).then_inc(s["sim_zero"], 1)
            dve.sem_inc(s["prod_rdy"], 2)
            dve.sem_inc(s["sim_ev"], 1)
            dve.wait_ge(s["q_ev"], NT * HC + 2)

            def products(b, m):
                g = (HC // 2) * b + m
                k2 = psum[:, 2 * (m % 2):2 * (m % 2) + 2, :]
                dve.wait_ge(s["k_mm"], g + 1)
                dve.wait_ge(s["sim_mm"], g + 1)
                q2 = qT[:, 2 * m:2 * m + 2, ds(b * S, S)]
                dve.tensor_tensor(prod[m % 2][:, :, 0:JF * S].rearrange("p u (j s) -> p u j s", s=S),
                                  k2[:, :, 0:JF * S].rearrange("p u (j s) -> p u j s", s=S),
                                  q2.unsqueeze(2).broadcast_to([P, 2, JF, S]), ALU.mult)
                dve.tensor_tensor(prod[m % 2][:, :, JF * S:C], k2[:, :, JF * S:C],
                                  qT[:, 2 * m:2 * m + 2, ds(b * S, C - JF * S)], ALU.mult).then_inc(s["prod_rdy"], 1)

            def copy_sims(b):
                dve.wait_ge(s["sim_tp"], b + 1)
                turned = bank[6].rearrange("p (j q r) -> p j q r", j=NJ, q=4)
                rows = row(sim.rearrange("p b j h -> p b (j h)"), b).rearrange("p (j h) -> p j h", j=NJ)
                for n, j0, j1 in ((S, 0, JF), (JR[-1], JF, NJ)):
                    for r in range(2):
                        last = dve.tensor_copy(rows[0:n, j0:j1, 8 * r:8 * r + 8].rearrange("p j (q h) -> p j q h", h=2),
                                               turned[0:n, j0:j1, :, 2 * r:2 * r + 2])
                last.then_inc(s["sim_ev"], 1)

            for m in range(HC // 2):
                products(0, m)
            with dve.Fori(1, B) as b:
                for m in range(HC // 2):
                    products(b, m)
                copy_sims(b - 1)
            copy_sims(B - 1)
            link = chain(dve, s["s_chain"], 1)
            dve.wait_ge(s["sim_ev"], B + 1)
            link(dve.tensor_reduce(smax[:, :, :], sim[:, :, :, :].rearrange("p b j h -> p b h j"), AX.X, ALU.max))
            dve.tensor_tensor(sim[:, :, :, :], sim[:, :, :, :], smax[:, :, :].unsqueeze(2).broadcast_to([S, B, NJ, H]),
                              ALU.subtract).then_inc(s["max_sub"], 1)
            dve.wait_ge(s["exp_done"], 1)
            link(dve.tensor_reduce(ssum[:, :, :], sim[:, :, :, :].rearrange("p b j h -> p b h j"), AX.X, ALU.add))
            link(dve.reciprocal(ssum[:, :, :], ssum[:, :, :]))
            link(dve.tensor_tensor(sim[:, :, :, :], sim[:, :, :, :], ssum[:, :, :].unsqueeze(2).broadcast_to([S, B, NJ, H]),
                                   ALU.mult))
            dve.sem_inc(s["v_used"], 2)
            dve.sem_inc(s["x1_rdy"], 2)

            def weigh_v(b, par):
                for j in range(NJ):
                    n = JR[j]
                    dve.wait_ge(s["v_mm"], NJ * b + j + 1)
                    if j == 0:
                        dve.wait_ge(s["tp_done"], 2 * b + 2)
                        dst = pacc[par]
                    else:
                        dve.wait_ge(s["pv_done"], (NJ - 1) * b + j)
                        dst = ptmp[(par * (NJ - 1) + j - 1) % 2]
                    ins = dve.tensor_tensor(dst[0:n, :].rearrange("p (h d) -> p h d", h=H),
                                            psum[0:n, 2 * (j % 2):2 * (j % 2) + 2, :].rearrange("p w (h d) -> p (w h) d", d=DH),
                                            sim[0:n, ds(b, 1), j, :].rearrange("p a h -> p (a h)").unsqueeze(2).broadcast_to([n, H, DH]),
                                            ALU.mult)
                    ins.then_inc(s["v_used"], 1)

            def residual1(b, par):
                dve.wait_ge(s["o_mm"], b + 2)
                dve.tensor_tensor(row(x, b), bank[6 + par][0:S, 0:D], row(x, b), ALU.add).then_inc(s["x1_rdy"], 1)
                dve.wait_ge(s["x1_rdy"], b + 3)
                ln_stats(dve, 1, b)

            dve.wait_ge(s["bo_rdy"], 1)
            weigh_v(0, 0)
            with dve.Fori(0, NP - 1) as i:
                for par in range(2):
                    weigh_v(2 * i + par + 1, 1 - par)
                    residual1(2 * i + par, par)
            weigh_v(B - 1, 1)
            residual1(B - 2, 0)
            residual1(B - 1, 1)
            dve.wait_ge(s["x1_rdy"], B + 2)
            ln_vector(dve, 1)
            link = chain(dve, s["r_chain"])
            dve.wait_ge(s["sig_done"], 1)
            dve.wait_ge(s["d8"], 2)

            def each(t):
                return t.unsqueeze(2).broadcast_to([S, B, E])
            score, biased, hit, one, two, w = [rt[:, n, :, :] for n in range(6)]
            best, order, total = [rsm[:, n, :] for n in range(3)]
            link(dve.tensor_tensor(biased, score, ebias[:, :].unsqueeze(1).broadcast_to([S, B, E]), ALU.add))
            for n, pick in enumerate((one, two)):
                link(dve.tensor_reduce(best, biased, AX.X, ALU.max))
                link(dve.tensor_tensor(hit, biased, each(best), ALU.is_equal))
                link(dve.tensor_tensor(hit, hit, down8[:, :].unsqueeze(1).broadcast_to([S, B, E]), ALU.mult))
                link(dve.tensor_reduce(order, hit, AX.X, ALU.max))
                link(dve.tensor_tensor(pick, hit, each(order), ALU.is_equal))
                if n == 0:
                    link(dve.scalar_tensor_tensor(biased, pick, NEG, biased, ALU.mult, ALU.add))
            link(dve.tensor_tensor(w, one, two, ALU.add))
            link(dve.tensor_tensor(w, w, score, ALU.mult))
            link(dve.tensor_reduce(total, w, AX.X, ALU.add))
            link(dve.tensor_scalar(total, total, 1e-20, None, ALU.add))
            link(dve.reciprocal(total, total))
            link(dve.tensor_tensor(gate_w[:, :, :], w, each(total), ALU.mult))
            dve.sem_inc(s["h_rdy"], 2)
            dve.sem_inc(s["d_used"], 4)
            with dve.Fori(0, NT) as t:
                for c in range(FC):
                    w_ = min(P, FT - c * P)
                    dve.wait_ge(s["silu_done"], t * FC + c + 1)
                    dve.tensor_tensor(hT[0:w_, c, :], sg[0:w_, c % 2, :], bank[2 + c % 2][0:w_, 0:N4], ALU.mult
                                      ).then_inc(s["h_rdy"], 1)
                for lb in range(TB):
                    b = t * TB + lb
                    for n, e in enumerate([E] + list(range(E))):
                        d = t * TB * (E + 1) + lb * (E + 1) + n
                        dve.wait_ge(s["d_mm"], d + 1)
                        dve.wait_ge(s["d_used"], d + 4)
                        pd = bank[4 + (lb * (E + 1) + n) % 4][0:S, 0:D]
                        if e == E:
                            ins = dve.tensor_tensor(row(x, b), pd, row(x, b), ALU.add)
                        else:
                            ins = dve.scalar_tensor_tensor(row(x, b), pd, gate_w[:, ds(b, 1), e], row(x, b),
                                                           ALU.mult, ALU.add)
                        ins.then_inc(s["d_used"], 1)
                    dve.wait_ge(s["d_used"], t * TB * (E + 1) + (lb + 1) * (E + 1) + 4)
                    ln_stats(dve, 2, b)
            dve.wait_ge(s["d_used"], NT * TB * (E + 1) + 4)
            dve.wait_ge(s["ld_ff"], 48)
            for m in range(3):
                dve.tensor_reduce(fsc[:, 0, m:m + 1], fw[m], AX.X, ALU.add, apply_absolute_value=True).then_inc(s["fw_mean"], 1)
            ln_vector(dve, 2)
            link = chain(dve, s["fw_chain"])
            dve.wait_ge(s["fw_bc"], 1)
            link(dve.tensor_scalar(fsc[:, 1, :], bank[7][:, 0:3], 1.0 / (D * FI), 1e-5, ALU.mult, ALU.max))
            link(dve.reciprocal(fsc[:, 2, :], fsc[:, 1, :]))
            qlink = chain(dve, s["fw_rdy"])
            for m in range(3):
                qlink(dve.tensor_scalar(fw[m], fw[m], fsc[:, 2, m:m + 1], 1.0, ALU.mult, ALU.min))
                qlink(dve.tensor_scalar(fw[m], fw[m], -1.0, ROUND, ALU.max, ALU.add))
                qlink(dve.tensor_scalar(fq[:, m, :], fw[m], ROUND, None, ALU.subtract))
            dve.wait_ge(s["f_ev"], NT * KD + 2)
            for par in range(2):
                link(dve.memset(txtT[par][:, :, 0:PAD], 0.0))
                link(dve.memset(bank[6 + par][:, 0:CP], 0.0))
            dve.memset(bank[4][:, 0:HALF * S], 0.0).then_inc(s["rho_zero"], 1)
            dve.sem_inc(s["x3_rdy"], 2)
            dve.sem_inc(s["e_in"], 2)
            dve.sem_inc(s["z_rdy"], HALVES * (NU + 1))

            def sums(b, par):
                first = dve.value_load(table[0:1, 0, ds(b, 1)], min_val=0, max_val=NU - 1)
                ends = dve.value_load(table[0:1, 1, ds(b, 1)], min_val=1, max_val=B * NU)
                this = dve.to_reg(b + 2)
                dve.wait_ge(s["tab_rdy"], 1)
                dve.wait_ge(s["t_ev"], this)
                with dve.Fori(first, NU) as u:
                    for h in range(HALVES):
                        q = HALVES * (ends + u) + h
                        dve.wait_ge(s["t_done"], q + 1)
                        dve.tensor_tensor(*sum_of(b, par, u, h), ALU.add).then_inc(s["z_rdy"], 1)

            NS = 6

            def mask_logits(b, par, i):
                ends = dve.value_load(table[0:1, 1, ds(b, 1)], min_val=1, max_val=B * NU)
                link = chain(dve, s["a_chain"], NS * b)
                this = dve.to_reg(ends + NU + 1)
                dve.wait_ge(s[f"ld_mask{par}"], 16 * i + 16)
                link(dve.tensor_scalar(rho[:, 0, :], maskb[:, par, :], -1.0, 1.0, ALU.mult, ALU.add))
                dve.wait_ge(s["rho_tp"], this)
                link(dve.scalar_tensor_tensor(rho[:, 1, :], rho[:, 0, :], NEG, bank[6 + par][0:S, PAD:CP],
                                              ALU.mult, ALU.add))
                dve.tensor_reduce(sm[:, 0:1], rho[:, 1, :], AX.X, ALU.max, negate=True).then_inc(s["e_in"], 1)

            def sum_ctx(b, par):
                link = chain(dve, s["a_chain"], NS * b + 4)
                dve.wait_ge(s["e_done"], b + 1)
                dve.wait_ge(s["cw_ev"], b + 2)
                link(dve.tensor_tensor_reduce(out=rho[:, 2, :], in0=ee[:, :], in1=cwb[par][:, 0, :], scale=1.0,
                                              scalar=0.0, op0=ALU.mult, op1=ALU.add, accum_out=sm[:, 2:3]))
                link(dve.tensor_tensor_reduce(out=rho[:, 2, :], in0=ee[:, :], in1=cwb[par][:, 1, :], scale=1.0,
                                              scalar=0.0, op0=ALU.mult, op1=ALU.add, accum_out=sm[:, 3:4]))
                dve.reciprocal(sm[:, 4:5], sm[:, 1:2]).then_inc(s["w_in"], 1)

            def residual3(b):
                link = chain(dve, s["a_chain"], NS * b + 2 + NS)
                link(dve.tensor_scalar(lnN[:, 0, :], row(x, b), meanvar[:, ds(b, 1), 0], rstd[:, ds(b, 1)],
                                       ALU.subtract, ALU.mult))
                dve.wait_ge(s["w_done"], b + 1)
                link(dve.tensor_scalar(lnN[:, 0, :], lnN[:, 0, :], sm[:, 5:6], sm[:, 6:7], ALU.mult, ALU.add))
                dve.tensor_tensor(row(x, b), row(x, b), lnN[:, 0, :], ALU.add).then_inc(s["x3_rdy"], 1)
                dve.wait_ge(s["x3_rdy"], b + 3)
                ln_stats(dve, 3, b)

            sums(0, 0)
            sums(1, 1)
            mask_logits(0, 0, 0)
            dve.sem_inc(s["a_chain"], 2)
            sum_ctx(0, 0)
            with dve.Fori(1, NP) as i:
                for par in range(2):
                    b = 2 * i + par
                    sums(b, par)
                    mask_logits(b - 1, 1 - par, i + par - 1)
                    residual3(b - 2)
                    sum_ctx(b - 1, 1 - par)
            mask_logits(B - 1, 1, NP - 1)
            residual3(B - 2)
            sum_ctx(B - 1, 1)
            dve.sem_inc(s["a_chain"], 2)
            residual3(B - 1)
            dve.wait_ge(s["x3_rdy"], B + 2)
            ln_vector(dve, 3)
            for m in range(2):
                dve.tensor_scalar(alpha[:, m, :], amax[:, 1, :], fsc[0:S, 1, m:m + 1], None, ALU.mult).then_inc(s["al_rdy"], 1)
            dve.wait_ge(s["al_rdy"], 2)
            dve.sem_inc(s["h_used"], 2)
            dve.sem_inc(s["x4_rdy"], 2)
            NH = 7

            def hidden(b, par):
                link = chain(dve, s["fh_chain"], NH * b)
                for hf in range(2):
                    dve.wait_ge(s["fu_mm"], 2 * b + hf + 1)
                    dve.wait_ge(s["fs_done"], 2 * b + hf + 3)
                    dve.scalar_tensor_tensor(h2[par][:, hf * G:(hf + 1) * G], bank[2 + hf][0:S, :], alpha[:, 1, ds(b, 1)],
                                             g2[par][:, hf * G:(hf + 1) * G], ALU.mult, ALU.mult).then_inc(s["h_used"], 1)
                dve.wait_ge(s["h_used"], 2 * b + 4)
                m = hm[:, par, :]
                link(dve.tensor_reduce(m[:, 0:1], h2[par], AX.X, ALU.max, apply_absolute_value=True))
                link(dve.tensor_scalar(m[:, 0:1], m[:, 0:1], 1e-5, None, ALU.max))
                link(dve.reciprocal(m[:, 1:2], m[:, 0:1]))
                link(dve.tensor_scalar(m[:, 1:2], m[:, 1:2], 127.0, None, ALU.mult))
                link(dve.tensor_scalar(m[:, 2:3], m[:, 0:1], 1.0 / 127.0, fsc[0:S, 1, 2:3], ALU.mult, ALU.mult))
                link(dve.tensor_scalar(h2[par], h2[par], m[:, 1:2], 127.0, ALU.mult, ALU.min))
                link(dve.tensor_scalar(h2[par], h2[par], -128.0, ROUND, ALU.max, ALU.add))
                dve.wait_ge(s["hT_mm"], b + 1)
                dve.tensor_scalar(hq, h2[par], ROUND, None, ALU.subtract).then_inc(s["hq_rdy"], 1)

            def residual4(b, par):
                dve.wait_ge(s["fo_mm"], b + 2)
                dve.scalar_tensor_tensor(row(x, b), bank[6 + par][0:S, 0:D], hm[:, par, 2:3], row(x, b),
                                         ALU.mult, ALU.add).then_inc(s["x4_rdy"], 1)

            hidden(0, 0)
            with dve.Fori(0, NP - 1) as i:
                for par in range(2):
                    hidden(2 * i + par + 1, 1 - par)
                    residual4(2 * i + par, par)
            hidden(B - 1, 1)
            residual4(B - 2, 0)
            residual4(B - 1, 1)


def kernel(**inputs):
    import numpy as _np
    import concourse.bacc as _bacc
    from concourse import mybir as _mybir
    from concourse.bass_utils import run_bass_kernel_spmd as _run

    v = {n: _np.asarray(a) for n, a in inputs.items()}

    def experts(routed, shared):
        e, d, f = routed.shape
        return _np.concatenate([routed.transpose(1, 0, 2).reshape(d, e * f), shared], axis=1)

    laid = {
        "x": v["x"],
        "ctx_t": v["ctx_1024"].transpose(0, 2, 1),
        "mask": v["mask_BxS2_ik0"],
        "wq": v["L0_xattn_Wq"], "wkv": v["L0_xattn_Wkv"], "wout": v["L0_xattn_Wout"], "bout": v["L0_xattn_bout"],
        "wr": v["L0_ffn_W_gate_router"], "ebias": v["L0_ffn_expert_bias"],
        "wg": experts(v["L0_ffn_Wg"], v["L0_ffn_Wg_s"]),
        "wu": experts(v["L0_ffn_Wu"], v["L0_ffn_Wu_s"]),
        "wd": _np.concatenate([v["L0_ffn_Wd"].reshape(-1, v["L0_ffn_Wd"].shape[2]), v["L0_ffn_Wd_s"]], axis=0),
        "ws": v["L1_xattn_Ws"], "w": v["L1_xattn_W"], "wvec": v["L1_xattn_w"], "b": v["L1_xattn_b"],
        "wcw": v["L1_xattn_Wcw"], "bcw": v["L1_xattn_bcw"], "wcb": v["L1_xattn_Wcb"], "bcb": v["L1_xattn_bcb"],
        "fg": v["L1_ffn_w_gate"].T, "fu": v["L1_ffn_w_up"].T, "fd": v["L1_ffn_w_down"].T,
    }
    nc = _bacc.Bacc("TRN2", target_bir_lowering=False, num_devices=1)
    arrays, args = {}, []
    for name, a in laid.items():
        a = _np.ascontiguousarray(a)
        arrays[f"in_{name}_dram"] = a
        args.append(nc.dram_tensor(f"in_{name}_dram", a.shape, _mybir.dt.from_np(a.dtype), kind="ExternalInput").ap())
    shape, dtype = v["x"].shape, v["x"].dtype
    args.append(nc.dram_tensor("out_0_dram", shape, _mybir.dt.from_np(dtype), kind="ExternalOutput").ap())
    bass_xattn_moe_additive_attn_bitlinear_ffn_kernel(nc, *args)
    r = _run(nc, [arrays], core_ids=[0])
    return r.results[0]["out_0_dram"]
```

```python
import concourse.bass as bass
from concourse import mybir
from contextlib import ExitStack


def bass_xattn_moe_additive_attn_bitlinear_ffn_kernel(
    nc, x_in, ctx_t, mask_in, wq_in, wkv_in, wout_in, bout_in, wr_in, ebias_in,
    wg_in, wu_in, wd_in, ws_in, w_in, wvec_in, b_in, wcw_in, bcw_in, wcb_in, bcb_in,
    fg_in, fu_in, fd_in, out,
):
    fp32 = mybir.dt.float32
    bf16 = mybir.dt.bfloat16
    f32r = mybir.dt.float32r
    i32 = mybir.dt.int32
    ALU = mybir.AluOpType
    ACT = mybir.ActivationFunctionType
    AX = mybir.AxisListType
    ds = bass.ds

    B, S, D = x_in.shape
    C = ctx_t.shape[2]
    P = 128
    KD = D // P
    INNER = wq_in.shape[1]
    DH = 64
    H = INNER // DH
    HC = INNER // P
    NJ = (C + S - 1) // S
    JR = [min(S, C - j * S) for j in range(NJ)]
    JF = C // S
    E = wr_in.shape[1]
    F = wg_in.shape[1] // (E + 1)
    FT = F * (E + 1)
    FC = (FT + P - 1) // P
    TB = 4
    N4 = TB * S
    NT = B // TB
    G = 512
    FI = fg_in.shape[1]
    FIC = FI // P
    HALF = 4
    HALVES = 4
    UNIT = HALVES * HALF
    NU = (C + UNIT - 1) // UNIT
    CP = NU * UNIT
    PAD = CP - C
    NEG = -1e30
    ROUND = 12582912.0
    EPS = 1e-5
    NP = B // 2
    NL = 4
    NB = 4
    BC = (C + NB - 1) // NB
    CE = NB * BC
    PC = CE - C
    assert CE % 2 == 0 and PC <= PAD
    assert F == 3 * P // 2
    WK = KD * INNER
    XT = KD * B * S

    ctx = ExitStack()
    with ctx:
        def sb(name, shape, dt=fp32):
            return ctx.enter_context(nc.sbuf_tensor(name, shape, dt))

        def sem(name):
            return ctx.enter_context(nc.semaphore(name))

        regions = (("lnT", XT),
                   ("ctxb", 2 * KD * CE),
                   ("spare", 7872),
                   ("att_w", 3 * WK),
                   ("big", HC * B * S),
                   ("work", 5600))
        with ExitStack() as first:
            plain = {n: first.enter_context(nc.sbuf_tensor(n, [P, z], fp32)) for n, z in regions}
        rounded = {n: ctx.enter_context(nc.sbuf_tensor(n + "_r", [P, z], f32r)) for n, z in regions}
        spare, att_w, big, work = [plain[n] for n in ("spare", "att_w", "big", "work")]
        spare_r, att_w_r, big_r, work_r = [rounded[n] for n in ("spare", "att_w", "big", "work")]
        lnT, lnT_hi = [m["lnT"][:, :].rearrange("p (k n) -> p k n", k=KD) for m in (plain, rounded)]
        ctxb, ctx_lo = [m["ctxb"][:, :].rearrange("p (a k c) -> p a k c", a=2, k=KD) for m in (plain, rounded)]

        x = sb("x", [S, B, D])
        ident = sb("ident", [P, P])
        ones = sb("ones", [P, P])
        unround = sb("unround", [P, 1])
        toround = sb("toround", [P, 1])
        headsel = sb("headsel", [P, 2, 4])
        simT = sb("simT", [P, C])
        half = sb("half", [S, B])
        stats = sb("stats", [S, B, 6])
        meanvar = sb("meanvar", [S, B, 2])
        vareps = sb("vareps", [S, B])
        rstd = sb("rstd", [S, B])
        shift = sb("shift", [S, B])
        lnN = sb("lnN", [S, NL, D])
        wk_hi = spare_r[:, 0:WK].rearrange("p (k n) -> p k n", k=KD)
        wv_hi = spare_r[:, WK:2 * WK].rearrange("p (k n) -> p k n", k=KD)
        ctx_hi = spare_r[:, 2 * WK:2 * WK + 2 * KD * CE].rearrange("p (a k c) -> p a k c", a=2, k=KD)
        moe_hi = [spare_r[:, KD * FT * m:KD * FT * (m + 1)].rearrange("p (k n) -> p k n", k=KD) for m in range(2)]
        featT = spare[:, 0:XT].rearrange("p (k n) -> p k n", k=KD)
        xq = spare[:, XT:XT + XT // 2].bitcast(bf16).rearrange("p (k n) -> p k n", k=KD)
        o = XT + XT // 2
        fq = spare[:, o:o + 3 * KD * FI // 2].bitcast(bf16).rearrange("p (m n) -> p m n", m=3)
        wq = att_w[:, 0:WK].rearrange("p (k n) -> p k n", k=KD)
        wkv = att_w[:, WK:3 * WK].rearrange("p (k n) -> p k n", k=KD)
        wq_lo = att_w_r[:, 0:WK].rearrange("p (k n) -> p k n", k=KD)
        wkv_lo = att_w_r[:, WK:3 * WK].rearrange("p (k n) -> p k n", k=KD)
        fw = [att_w[:, KD * FI * m:KD * FI * (m + 1)] for m in range(3)]
        wout = sb("wout", [P, HC, D])
        bout = sb("bout", [S, D])
        qT = big[:, :].rearrange("p (c n) -> p c n", c=HC)
        wg = big[:, 0:KD * FT].rearrange("p (k n) -> p k n", k=KD)
        wu = big[:, KD * FT:2 * KD * FT].rearrange("p (k n) -> p k n", k=KD)
        moe_lo = [big_r[:, KD * FT * m:KD * FT * (m + 1)].rearrange("p (k n) -> p k n", k=KD) for m in range(2)]
        wd = big[:, 2 * KD * FT:2 * KD * FT + FC * D].rearrange("p (c n) -> p c n", c=FC)
        HW = KD * HALF * S
        zt = [big[:, HW * m:HW * (m + 1)].rearrange("p (k t f) -> p k t f", k=KD, t=HALF) for m in range(HALVES)]
        ht = [big[:, HW * m:HW * (m + 1)].rearrange("p (k t f) -> p k t f", k=KD, t=HALF)
              for m in range(HALVES, 2 * HALVES)]
        o = 2 * HALVES * HW
        txtT = [big[:, o + KD * CP * m:o + KD * CP * (m + 1)].rearrange("p (k t) -> p k t", k=KD) for m in range(2)]
        o += 2 * KD * CP
        cwb = [big[0:S, o + 2 * CE * m:o + 2 * CE * (m + 1)].rearrange("p (w t) -> p w t", w=2) for m in range(2)]
        assert o + 4 * CE <= HC * B * S
        hT = work[:, :].rearrange("p (c n) -> p c n", c=FC)
        wq_hi = work_r[:, 0:WK].rearrange("p (k n) -> p k n", k=KD)
        lnT_lo = [work_r[:, WK:WK + XT].rearrange("p (k n) -> p k n", k=KD),
                  att_w_r[:, 0:XT].rearrange("p (k n) -> p k n", k=KD)]
        prod = [work[:, 2 * C * m:2 * C * (m + 1)].rearrange("p (c n) -> p c n", c=2) for m in range(2)]
        pacc = [work[0:S, INNER * m:INNER * (m + 1)] for m in range(2)]
        ptmp = [work[0:S, INNER * (m + 2):INNER * (m + 3)] for m in range(2)]
        oT = work[:, 4 * INNER:4 * INNER + HC * S].rearrange("p (c n) -> p c n", c=HC)
        g2 = [work[0:S, FI * m:FI * (m + 1)] for m in range(2)]
        h2 = [work[0:S, FI * (m + 2):FI * (m + 3)] for m in range(2)]
        hqT = work[:, 4608:4608 + FIC * S // 2].bitcast(bf16).rearrange("p (c n) -> p c n", c=FIC)
        rho = work[0:S, 0:3 * C].rearrange("p (a t) -> p a t", a=3)
        ee = work[0:S, 3 * C:4 * C]
        lrow = work[:, 4 * C:4 * C + HALF * S]
        sim = sb("sim", [S, B, NJ, H])
        smax = sb("smax", [S, B, H])
        ssum = sb("ssum", [S, B, H])
        wr = sb("wr", [P, KD, E])
        ebias = sb("ebias", [S, E])
        down8 = sb("down8", [S, E])
        down8i = sb("down8i", [S, E], i32)
        rt = sb("rt", [S, 6, B, E])
        rsm = sb("rsm", [S, 3, B])
        gate_w = sb("gate_w", [S, B, E])
        sg = sb("sg", [P, 2, N4])
        wsx = sb("wsx", [P, KD, D])
        wx = sb("wx", [P, KD, D])
        bcol = sb("bcol", [P, KD])
        wvec = sb("wvec", [P, KD])
        wpair = sb("wpair", [P, KD, 3])
        rowsel = sb("rowsel", [P, HALVES])
        wc = sb("wc", [P, 2, KD])
        wcrep = sb("wcrep", [P, 2, KD, S])
        bc = sb("bc", [S, 2])
        mrow = sb("mrow", [B, CP], i32)
        mnz = sb("mnz", [B, CP])
        kflag = sb("kflag", [B, NU])
        kdown = sb("kdown", [B, NU])
        kdowni = sb("kdowni", [B, NU], i32)
        kcount = sb("kcount", [B, 2])
        rowf = sb("rowf", [1, 6, B])
        table = sb("table", [1, 3, B], i32)
        maskb = sb("maskb", [S, 2, C], i32)
        sm = sb("sm", [S, 10])
        fsc = sb("fsc", [P, 4, 3])
        amax = sb("amax", [S, 4, B])
        alpha = sb("alpha", [S, 2, B])
        hm = sb("hm", [S, 2, 4])
        xl = att_w[0:S, 0:B * D].rearrange("p (b d) -> p b d", b=B)

        psum = ctx.enter_context(nc.psum_tensor("psum", [P, 8, G], fp32))
        bank = [psum[:, i, :] for i in range(8)]

        s = {}
        for name in (
            "ld_x0 ld_x1 ld_x2 ld_x3 ld_misc ld_wq ld_wkv ld_wout ld_gu ld_moe ld_ff ld_ctx0 ld_ctx1 ld_mrow "
            "ld_mask0 ld_mask1 st_out "
            "ident_rdy const p_chain pad_rdy act_set c_done wp_rdy d8 cnt_in cnt_mm tab_chain tab_rdy "
            "wq_hi wq_lo wkv_hi wkv_lo ctx_hi ctx_lo moe_hi moe_lo "
            "q_ready q_ev k_mm prod_rdy sim_zero sim_mm st_ev sim_tp sim_ev s_chain max_sub exp_done "
            "v_mm v_used pv_done tp_done tp_ev o_mm x1_rdy bo_rdy "
            "r_mm sig_done r_chain g_mm silu_done h_rdy d_mm d_used "
            "f_mm f_ev t_mm t_ev ctx_x cw_ev pz_chain rho_zero z_rdy t_done rho_mm row_ev rho_tp "
            "a_chain e_in e_done w_in w_done ab_done x3_rdy "
            "fw_mean fw_bc fw_chain fw_scale fw_rdy xs_rdy xr_done al_rdy fg_mm fu_mm fs_done h_used fh_chain "
            "hq_rdy hT_mm hT_ev fo_mm x4_rdy").split():
            s[name] = sem(name)
        lns = [{k: sem(f"ln{n}_{k}") for k in ("stat", "rstd", "x", "T", "ev", "lo", "ch", "pch")} for n in range(4)]

        block = ctx.enter_context(nc.Block())

        def sum_of(b, par, u, hf):
            return (zt[hf], featT[:, :, ds(b * S, S)].unsqueeze(2).broadcast_to([P, KD, HALF, S]),
                    txtT[par][:, :, ds(u * UNIT + hf * HALF, HALF)].unsqueeze(3).broadcast_to([P, KD, HALF, S]))

        def units_to(eng, b):
            return eng.value_load(table[0:1, 2, ds(b, 1)], min_val=1, max_val=B * NU)

        def units_of(eng, b):
            return eng.value_load(table[0:1, 0, ds(b, 1)], min_val=0, max_val=NU - 1), units_to(eng, b)

        def block_of(eng, b):
            return eng.value_load(table[0:1, 1, ds(b, 1)], min_val=0, max_val=NB - 1)

        def row(t, b):
            return t[:, ds(b, 1), :].rearrange("p a d -> p (a d)")

        def chain(eng, sm_, base=0):
            n = [0]

            def link(ins):
                n[0] += 1
                ins.then_inc(sm_, 1)
                eng.wait_ge(sm_, base + n[0])
            return link

        def f32(ap):
            return ap.bitcast(fp32)

        def by_parts(pe, dst, a, b):
            pairs = [(0, 0), (0, 1), (1, 0)]
            for n, (i, j) in enumerate(pairs):
                for k in range(KD):
                    last = pe.matmul(dst, a[i][k], b[j][k], start=(n == 0 and k == 0),
                                     stop=(n == len(pairs) - 1 and k == KD - 1))
            return last

        def ln_stats(dve, n, b):
            dve.bn_stats(row(stats, b), row(x, b)).then_inc(lns[n]["ch"], 1)

        def ln_vector(dve, n):
            q = lns[n]
            if n == 0:
                for b in range(B):
                    if b % 4 == 0:
                        dve.wait_ge(s[f"ld_x{b // 4}"], 16)
                    ln_stats(dve, n, b)
            for b in range(B):
                dve.wait_ge(q["ch"], b + 1)
                dve.bn_aggr(meanvar[:, b, :], stats[:, b, :]).then_inc(q["stat"], 1)
            dve.wait_ge(q["stat"], B)
            dve.wait_ge(q["rstd"], 1)
            if n == 3:
                with dve.Fori(0, B) as b:
                    dve.tensor_scalar(row(xl, b), row(x, b),
                                      meanvar[:, ds(b, 1), 0:1].rearrange("p a s -> p (a s)"), rstd[:, ds(b, 1)],
                                      ALU.subtract, ALU.mult).then_inc(q["ch"], 1)
                dve.wait_ge(q["ch"], 2 * B)
                link = chain(dve, q["ch"], 2 * B)
                link(dve.tensor_reduce(amax[:, 0, :], xl[:, :, :], AX.X, ALU.max, apply_absolute_value=True))
                link(dve.tensor_scalar(amax[:, 1, :], amax[:, 0, :], 1e-5, None, ALU.max))
                link(dve.reciprocal(amax[:, 2, :], amax[:, 1, :]))
                link(dve.tensor_scalar(amax[:, 2, :], amax[:, 2, :], 127.0, None, ALU.mult))
                link(dve.tensor_scalar(amax[:, 1, :], amax[:, 1, :], 1.0 / 127.0, None, ALU.mult))
                dve.sem_inc(s["xs_rdy"], 1)
                with dve.Fori(0, B // NL) as i:
                    for par in range(NL):
                        b = NL * i + par
                        dve.wait_ge(s["xr_done"], b + 1)
                        dve.wait_ge(q["T"], b + 1)
                        dve.tensor_scalar(lnN[:, par, :], row(xl, b), ROUND + 127.0, ROUND - 128.0, ALU.min, ALU.max
                                          ).then_inc(q["x"], 1)
            else:
                def normalise(b, par):
                    dve.wait_ge(q["T"], b + 1)
                    dve.tensor_scalar(lnN[:, par, :], row(x, b),
                                      meanvar[:, ds(b, 1), 0:1].rearrange("p a s -> p (a s)"), rstd[:, ds(b, 1)],
                                      ALU.subtract, ALU.mult).then_inc(q["x"], 1)

                def low_part(b, par):
                    if n == 2:
                        return
                    dve.wait_ge(q["ev"], b + NL + 1)
                    dve.tensor_tensor(lnT_lo[n][:, :, ds(b * S, S)],
                                      bank[4 + par][:, 0:KD * S].rearrange("p (k s) -> p k s", k=KD),
                                      f32(lnT_hi[:, :, ds(b * S, S)]), ALU.subtract).then_inc(q["lo"], 1)

                if n < 2:
                    dve.sem_inc(q["lo"], NL)
                for par in range(NL):
                    normalise(par, par)
                with dve.Fori(0, B // NL - 1) as i:
                    for par in range(NL):
                        low_part(NL * i + par, par)
                        normalise(NL * i + NL + par, par)
                for par in range(NL):
                    low_part(B - NL + par, par)

        def ln_gpsimd(pool, n):
            q = lns[n]
            pool.wait_ge(q["stat"], B)
            pool.tensor_scalar(vareps[:, :], meanvar[:, :, 1], EPS, None, ALU.add).then_inc(q["pch"], 1)
            pool.wait_ge(q["pch"], 1)
            pool.tensor_tensor(rstd[:, :], vareps[:, :], half[:, :], ALU.pow).then_inc(q["rstd"], 1)

        def ln_tensor(pe, n):
            q = lns[n]
            pe.sem_inc(q["T"], NL)
            with pe.Fori(0, B // NL) as i:
                for par in range(NL):
                    b = NL * i + par
                    pe.wait_ge(q["x"], b + 1)
                    pe.wait_ge(q["lo" if n < 2 else "ev"], b + 1)
                    for k in range(KD):
                        last = pe.transpose(bank[4 + par][:, k * S:(k + 1) * S],
                                            lnN[:, par, k * P:(k + 1) * P], ident[0:S, 0:S])
                    last.then_inc(q["T"], 1)

        def ln_scalar(act, n):
            q = lns[n]
            dst = xq if n == 3 else lnT if n == 2 else lnT_hi
            act.sem_inc(q["ev"], NL)

            def scale_and_round(b):
                act.activation(row(xl, b), row(xl, b), ACT.Identity, scale=amax[:, 2, ds(b, 1)], bias=toround[0:S, 0:1]
                               ).then_inc(s["xr_done"], 1)

            def copy(b, par):
                act.wait_ge(q["T"], b + NL + 1)
                to, turned = dst[:, :, ds(b * S, S)], bank[4 + par][:, 0:KD * S].rearrange("p (k s) -> p k s", k=KD)
                if n == 3:
                    last = act.activation(to, turned, ACT.Identity, bias=unround[:, 0:1])
                else:
                    last = act.activation(to, turned, ACT.Copy)
                last.then_inc(q["ev"], 1)

            if n == 3:
                act.wait_ge(s["xs_rdy"], 1)
                for par in range(NL):
                    scale_and_round(par)
                with act.Fori(0, B // NL - 1) as i:
                    for par in range(NL):
                        copy(NL * i + par, par)
                        scale_and_round(NL * i + NL + par)
                for par in range(NL):
                    copy(B - NL + par, par)
            else:
                with act.Fori(0, B // NL) as i:
                    for par in range(NL):
                        copy(NL * i + par, par)

        def ln_done(eng, n):
            eng.wait_ge(lns[n]["lo" if n < 2 else "ev"], B + NL)

        @block.sync
        def _(sp):
            for g in range(0, B, 4):
                sp.dma_start(x[:, g:g + 4, :], x_in[g:g + 4].rearrange("b s d -> s b d")).then_inc(s[f"ld_x{g // 4}"], 16)
            sp.dma_start(wq, wq_in.rearrange("(k p) n -> p k n", p=P)).then_inc(s["ld_wq"], 16)
            sp.dma_start(wkv, wkv_in.rearrange("(k p) n -> p k n", p=P)).then_inc(s["ld_wkv"], 16)

            def load_ctx(b, par, used, count):
                if used is not None:
                    sp.wait_ge(used, count)
                sp.dma_start(ctxb[:, par, :, PC:CE], ctx_t[ds(b, 1), :, :].rearrange("a (k p) c -> p (a k) c", p=P)
                             ).then_inc(s[f"ld_ctx{par}"], 16)
            load_ctx(0, 0, None, 0)
            load_ctx(1, 1, None, 0)
            sp.dma_start(wout[:, :, :], wout_in.rearrange("(c p) n -> p c n", p=P)).then_inc(s["ld_wout"], 16)
            with sp.Fori(1, NP) as i:
                for par in range(2):
                    load_ctx(2 * i + par, par, s["k_mm"], HC // 2 * (2 * i + par - 1))
            load_ctx(0, 0, s["k_mm"], HC // 2 * (B - 1))
            load_ctx(1, 1, s["k_mm"], HC // 2 * B)
            sp.wait_ge(s["prod_rdy"], B * (HC // 2) + 2)
            sp.dma_start(wg, wg_in.rearrange("(k p) n -> p k n", p=P)).then_inc(s["ld_gu"], 16)
            sp.dma_start(wu, wu_in.rearrange("(k p) n -> p k n", p=P)).then_inc(s["ld_gu"], 16)
            with sp.Fori(1, NP) as i:
                for par in range(2):
                    load_ctx(2 * i + par, par, s["v_mm"], NJ * (2 * i + par - 1))
            full = FT // P
            sp.dma_start(wd[:, 0:full, :], wd_in[0:full * P].rearrange("(c p) n -> p c n", p=P)).then_inc(s["ld_moe"], 16)
            sp.dma_start(wd[0:FT - full * P, full, :], wd_in[full * P:FT, :]).then_inc(s["ld_moe"], 16)
            sp.wait_ge(s["v_mm"], NJ * B)

            def load_mask(b, par):
                sp.dma_start(maskb[:, par, :], mask_in[ds(b, 1), :].broadcast_to([S, C])
                             ).then_inc(s[f"ld_mask{par}"], 16)
            for par in range(2):
                load_ctx(par, par, None, 0)
                load_mask(par, par)
            sp.wait_ge(s["g_mm"], NT * FC)
            sp.dma_start(fw[0].rearrange("p (k n) -> p k n", k=KD), fg_in.rearrange("(k p) n -> p k n", p=P)
                         ).then_inc(s["ld_ff"], 16)
            sp.dma_start(fw[1].rearrange("p (k n) -> p k n", k=KD), fu_in.rearrange("(k p) n -> p k n", p=P)
                         ).then_inc(s["ld_ff"], 16)
            sp.dma_start(fw[2].rearrange("p (k n) -> p k n", k=FIC), fd_in.rearrange("(k p) n -> p k n", p=P)
                         ).then_inc(s["ld_ff"], 16)
            with sp.Fori(1, NP) as i:
                for par in range(2):
                    b = 2 * i + par
                    load_ctx(b, par, s["ctx_x"], b - 1)
                    sp.wait_ge(s["e_in"], b + 1)
                    load_mask(b, par)
            with sp.Fori(0, NP) as i:
                sp.wait_ge(s["x4_rdy"], 2 * i + 4)
                sp.dma_start(out[ds(2 * i, 2)].rearrange("b s d -> s b d"), x[:, ds(2 * i, 2), :]
                             ).then_inc(s["st_out"], 16)
            sp.wait_ge(s["st_out"], 16 * NP)

        @block.gpsimd
        def _(pool):
            link = chain(pool, s["p_chain"])
            link(pool.memset(ident[:, :], 0.0))
            pool.affine_select(out=ident[:, :], in_=ident[:, :], compare_op=ALU.not_equal, fill=1.0,
                               base=0, pattern=[[-1, P]], channel_multiplier=1).then_inc(s["ident_rdy"], 1)
            pool.wait_ge(s["ident_rdy"], 1)
            link(pool.memset(half[:, :], -0.5))
            link(pool.memset(ones[:, :], 1.0))
            link(pool.memset(unround[:, :], -ROUND))
            link(pool.memset(toround[:, :], ROUND))
            link(pool.memset(rowsel[:, :], 0.0))
            for n in range(4):
                link(pool.affine_select(out=rowsel[32 * n:32 * n + 2, n // 2::2], in_=rowsel[32 * n:32 * n + 2, n // 2::2],
                                        compare_op=ALU.not_equal, fill=1.0, base=0, pattern=[[-1, 2]],
                                        channel_multiplier=1))
            link(pool.memset(headsel[:, :, :], 0.0))
            link(pool.memset(headsel[0:DH, 0, 0:1], 1.0))
            link(pool.memset(headsel[0:DH, 1, 2:3], 1.0))
            link(pool.memset(headsel[DH:P, 1, 3:4], 1.0))
            link(pool.memset(mrow[:, 0:PAD], 0))
            link(pool.iota(kdowni[:, :], pattern=[[-1, NU]], base=NU, channel_multiplier=0))
            link(pool.iota(down8i[:, :], pattern=[[-1, E]], base=E, channel_multiplier=0))
            pool.memset(headsel[DH:P, 0, 1:2], 1.0).then_inc(s["const"], 1)
            pool.dma_start(mrow[:, PAD:CP], mask_in).then_inc(s["ld_mrow"], 16)
            small = [(wr[:, :, :], wr_in.rearrange("(k p) n -> p k n", p=P)),
                     (ebias[:, :], ebias_in.rearrange("(a n) -> a n", a=1).broadcast_to([S, E])),
                     (bout[:, :], bout_in.rearrange("(a n) -> a n", a=1).broadcast_to([S, D])),
                     (wsx[:, :, :], ws_in.rearrange("(k p) n -> p k n", p=P)),
                     (wx[:, :, :], w_in.rearrange("(k p) n -> p k n", p=P)),
                     (bc[:, 0:1], bcw_in.rearrange("(a n) -> a n", a=1).broadcast_to([S, 1])),
                     (bc[:, 1:2], bcb_in.rearrange("(a n) -> a n", a=1).broadcast_to([S, 1]))]
            pool.wait_ge(s["const"], 1)
            for par in range(2):
                link(pool.memset(f32(ctx_lo[:, par, :, 0:PC]), 0.0))
                pool.memset(f32(ctx_hi[:, par, :, 0:PC]), 0.0).then_inc(s["pad_rdy"], 1)
            pool.wait_ge(s["pad_rdy"], 2)
            ln_gpsimd(pool, 0)
            pool.wait_ge(s["wq_hi"], 1)
            pool.tensor_tensor(wq_lo, wq, f32(wq_hi), ALU.subtract).then_inc(s["wq_lo"], 1)
            pool.wait_ge(s["wkv_hi"], 1)
            pool.tensor_tensor(wkv_lo[:, :, 0:INNER], wkv[:, :, 0:INNER], f32(wk_hi), ALU.subtract).then_inc(s["wkv_lo"], 1)
            pool.wait_ge(s["wkv_hi"], 2)

            def ctx_low(n, par):
                pool.wait_ge(s["ctx_hi"], n + 1)
                pool.tensor_tensor(ctx_lo[:, par, :, PC:CE], ctxb[:, par, :, PC:CE], f32(ctx_hi[:, par, :, PC:CE]),
                                   ALU.subtract).then_inc(s["ctx_lo"], 1)
            ctx_low(0, 0)
            for dst, src in small:
                pool.dma_start(dst, src).then_inc(s["ld_misc"], 16)
            with nc.allow_non_contiguous_dma(reason="256 values each, once"):
                for dst, src in ((bcol[:, :], b_in.rearrange("a (k p) -> p (a k)", p=P)),
                                 (wvec[:, :], wvec_in.rearrange("(k p) a -> p (k a)", p=P)),
                                 (wc[:, 0, :], wcw_in.rearrange("a (k p) -> p (a k)", p=P)),
                                 (wc[:, 1, :], wcb_in.rearrange("a (k p) -> p (a k)", p=P))):
                    pool.dma_start(dst, src).then_inc(s["ld_misc"], 16)
            pool.tensor_tensor(wkv_lo[:, :, INNER:], wkv[:, :, INNER:], f32(wv_hi), ALU.subtract).then_inc(s["wkv_lo"], 1)
            ctx_low(1, 1)
            pool.wait_ge(s["ld_misc"], 16 * 11)
            pool.wait_ge(lns[0]["x"], B)
            pool.tensor_tensor(x[:, :, :], x[:, :, :], bout[:, :].unsqueeze(1).broadcast_to([S, B, D]), ALU.add
                               ).then_inc(s["bo_rdy"], 1)
            with pool.Fori(1, NP) as i:
                for par in range(2):
                    ctx_low(2 * i + par, par)
            ctx_low(B, 0)
            ctx_low(B + 1, 1)
            pool.sem_inc(s["pv_done"], 2)

            def sum_keys(b, par):
                for j in range(1, NJ):
                    n = JR[j]
                    pool.wait_ge(s["v_used"], NJ * b + j + 3)
                    if j > 1:
                        pool.wait_ge(s["pv_done"], (NJ - 1) * b + j + 1)
                    pool.tensor_tensor(pacc[par][0:n, :], pacc[par][0:n, :], ptmp[(par * (NJ - 1) + j - 1) % 2][0:n, :],
                                       ALU.add).then_inc(s["pv_done"], 1)

            with pool.Fori(0, NP - 1) as i:
                for par in range(2):
                    sum_keys(2 * i + par, par)
                    ctx_low(B + 2 * i + par + 2, par)
            sum_keys(B - 2, 0)
            sum_keys(B - 1, 1)
            ln_gpsimd(pool, 1)
            for m, wgt in enumerate((wg, wu)):
                pool.wait_ge(s["moe_hi"], m + 1)
                pool.tensor_tensor(moe_lo[m], wgt, f32(moe_hi[m]), ALU.subtract).then_inc(s["moe_lo"], 1)
            ln_gpsimd(pool, 2)
            zlink = chain(pool, s["pz_chain"])
            for par in range(2):
                zlink(pool.memset(ctxb[:, par, :, 0:PC], 0.0))
                zlink(pool.memset(txtT[par][:, :, 0:PAD], 0.0))
                zlink(pool.memset(cwb[par], 0.0))
            pool.sem_inc(s["rho_zero"], 1)
            pool.wait_ge(s["fw_scale"], 1)
            qlink = chain(pool, s["fw_rdy"])
            for m in range(3):
                qlink(pool.tensor_scalar(fw[m], fw[m], fsc[:, 2, m:m + 1], 1.0, ALU.mult, ALU.min))
                qlink(pool.tensor_scalar(fw[m], fw[m], -1.0, ROUND, ALU.max, ALU.add))
                qlink(pool.tensor_scalar(fq[:, m, :], fw[m], ROUND, None, ALU.subtract))
            ln_gpsimd(pool, 3)

        @block.tensor
        def _(pe):
            pe.wait_ge(s["ident_rdy"], 1)
            ln_tensor(pe, 0)
            ln_done(pe, 0)
            pe.wait_ge(s["wq_lo"], 1)
            with pe.Fori(0, NT) as t:
                for c in range(HC):
                    pe.wait_ge(s["q_ev"], t * HC + c + 1)
                    by_parts(pe, bank[c % 2][:, 0:N4],
                             [[w_[:, k, c * P:(c + 1) * P] for k in range(KD)] for w_ in (wq_hi, wq_lo)],
                             [[l_[:, k, ds(t * N4, N4)] for k in range(KD)] for l_ in (lnT_hi, lnT_lo[0])]
                             ).then_inc(s["q_ready"], 1)
            pe.wait_ge(s["cnt_in"], 1)
            for n in range(2):
                last = pe.transpose(bank[7][0:1, n * B:(n + 1) * B], kcount[:, n:n + 1], ident[0:B, 0:B])
            last.then_inc(s["cnt_mm"], 1)
            pe.wait_ge(s["wkv_lo"], 1)
            pe.wait_ge(s["const"], 1)
            pe.wait_ge(s["q_ev"], NT * HC + 2)

            def sims(b, par, m, turn):
                pe.wait_ge(s["prod_rdy"], (HC // 2) * b + m + 3)
                if m == 0:
                    pe.wait_ge(s["st_ev"], b + 1)
                for u in range(2):
                    c = 2 * m + u
                    n = 32 * (c % 4)
                    last = pe.matmul(bank[4 + par][n:n + 4, 0:C], headsel[:, c // 4, :], prod[m % 2][:, u, :],
                                     start=(c < 4), stop=(c >= 4), skip_group_check=True)
                last.then_inc(s["sim_mm"], 1)
                if m == 1 and turn:
                    turn_sims(b - 1)

            def turn_sims(b):
                pe.wait_ge(s["st_ev"], b + 3)
                pe.wait_ge(s["sim_ev"], b + 1)
                for j in range(NJ):
                    last = pe.transpose(bank[6][0:JR[j], j * P:(j + 1) * P], simT[:, j * S:j * S + JR[j]], ident[:, :])
                last.then_inc(s["sim_tp"], 1)

            pe.wait_ge(s["sim_zero"], 2)
            pe.sem_inc(s["sim_mm"], 2)

            def keys(b, par, m):
                if m == 0:
                    pe.wait_ge(s["ctx_lo"], b + 1)
                pe.wait_ge(s["prod_rdy"], (HC // 2) * b + m + 1)
                for u in range(2):
                    c = 2 * m + u
                    last = by_parts(pe, bank[2 * (m % 2) + u][:, 0:CE],
                                    [[w_[:, k, c * P:(c + 1) * P] for k in range(KD)] for w_ in (wk_hi, wkv_lo)],
                                    [[c_[:, par, k, :] for k in range(KD)] for c_ in (ctx_hi, ctx_lo)])
                last.then_inc(s["k_mm"], 1)

            def keys_and_sims(b, par, more=True, turn=True):
                for m in range(HC // 2):
                    if m < HC // 2 - 1:
                        keys(b, par, m + 1)
                    elif more:
                        keys(b + 1, 1 - par, 0)
                    sims(b, par, m, turn)

            keys(0, 0, 0)
            keys_and_sims(0, 0, turn=False)
            with pe.Fori(0, NP - 1) as i:
                keys_and_sims(2 * i + 1, 1)
                keys_and_sims(2 * i + 2, 0)
            keys_and_sims(B - 1, 1, more=False)
            turn_sims(B - 1)
            def values(b, par):
                pe.wait_ge(s["ctx_lo"], B + b + 1)
                for j in range(NJ):
                    pe.wait_ge(s["v_used"], NJ * b + j + 1)
                    for n in range(2):
                        last = by_parts(pe, bank[2 * (j % 2) + n][0:JR[j], :],
                                        [[c_[:, par, k, PC + j * S:PC + j * S + JR[j]] for k in range(KD)] for c_ in (ctx_hi, ctx_lo)],
                                        [[wv_hi[:, k, n * G:(n + 1) * G] for k in range(KD)],
                                         [wkv_lo[:, k, INNER + n * G:INNER + (n + 1) * G] for k in range(KD)]])
                    last.then_inc(s["v_mm"], 1)

            def project(b, par):
                pe.wait_ge(s["pv_done"], (NJ - 1) * (b + 1) + 2)
                for c in range(HC):
                    if c % 4 == 0:
                        pe.wait_ge(s["tp_ev"], 2 * b + c // 4 + 1)
                    last = pe.transpose(bank[4 + c // 4][:, (c % 4) * S:(c % 4 + 1) * S],
                                        pacc[par][:, c * P:(c + 1) * P], ident[0:S, 0:S])
                    if c % 4 == 3:
                        last.then_inc(s["tp_done"], 1)
                pe.wait_ge(s["tp_ev"], 2 * b + 4)
                pe.wait_ge(s["x1_rdy"], b + 1)
                for c in range(HC):
                    last = pe.matmul(bank[6 + par][0:S, 0:D], oT[:, c, :], wout[:, c, :],
                                     start=(c == 0), stop=(c == HC - 1))
                last.then_inc(s["o_mm"], 1)

            pe.wait_ge(s["ld_wout"], 16)
            pe.sem_inc(s["tp_done"], 4)
            pe.sem_inc(s["o_mm"], 1)
            pe.wait_ge(s["wkv_lo"], 2)
            values(0, 0)
            with pe.Fori(0, NP - 1) as i:
                for par in range(2):
                    b = 2 * i + par
                    values(b + 1, 1 - par)
                    project(b, par)
            values(B - 1, 1)
            project(B - 2, 0)
            project(B - 1, 1)

            pe.wait_ge(s["x1_rdy"], B + 2)
            ln_tensor(pe, 1)
            ln_done(pe, 1)
            for b in range(B):
                for n, l_ in enumerate((f32(lnT_hi), f32(lnT_lo[1]))):
                    for k in range(KD):
                        last = pe.matmul(bank[7][0:S, b * E:(b + 1) * E], l_[:, k, b * S:(b + 1) * S], wr[:, k, :],
                                         start=(n == 0 and k == 0), stop=(n == 1 and k == KD - 1))
            last.then_inc(s["r_mm"], 1)
            pe.wait_ge(s["moe_lo"], 2)
            with pe.Fori(0, NT) as t:
                for c in range(FC):
                    w = min(P, FT - c * P)
                    before = pe.to_reg(t * FC + c + 1)
                    if w < P:
                        pe.wait_ge(s["ld_moe"], 32)
                    pe.wait_ge(s["h_rdy"], before)
                    for bk, hi, lo in ((0, moe_hi[0], moe_lo[0]), (2, moe_hi[1], moe_lo[1])):
                        last = by_parts(pe, bank[bk + c % 2][0:w, 0:N4],
                                        [[w_[:, k, c * P:c * P + w] for k in range(KD)] for w_ in (hi, lo)],
                                        [[l_[:, k, ds(t * N4, N4)] for k in range(KD)] for l_ in (lnT_hi, lnT_lo[1])])
                    last.then_inc(s["g_mm"], 1)
                pe.wait_ge(s["h_rdy"], t * FC + FC + 2)
                for lb in range(TB):
                    for n, e in enumerate([E] + list(range(E))):
                        parts = [(3 * (e // 2), 0, P), (3 * (e // 2) + 1, 0, P // 2)] if e % 2 == 0 else \
                                [(3 * (e // 2) + 1, P // 2, P), (3 * (e // 2) + 2, 0, P)]
                        slot = (lb * (E + 1) + n) % 4
                        pe.wait_ge(s["d_used"], t * TB * (E + 1) + lb * (E + 1) + n + 1)
                        for q, (c, lo, hi) in enumerate(parts):
                            last = pe.matmul(bank[4 + slot][0:S, 0:D], hT[lo:hi, c, lb * S:(lb + 1) * S],
                                             wd[lo:hi, c, :], start=(q == 0), stop=(q == 1))
                        last.then_inc(s["d_mm"], 1)

            pe.wait_ge(s["d_used"], NT * TB * (E + 1) + 4)
            ln_tensor(pe, 2)
            ln_done(pe, 2)
            pe.wait_ge(s["fw_mean"], 3)
            pe.matmul(bank[7][:, 0:3], ones[:, :], fsc[:, 0, :], start=True, stop=True).then_inc(s["fw_bc"], 1)
            with pe.Fori(0, NT) as t:
                for m in range(KD):
                    pe.wait_ge(s["f_ev"], t * KD + m + 1)
                    for k in range(KD):
                        last = pe.matmul(bank[m][:, 0:N4], wx[:, k, m * P:(m + 1) * P], lnT[:, k, ds(t * N4, N4)],
                                         start=(k == 0), stop=(k == KD - 1))
                    last.then_inc(s["f_mm"], 1)
            pe.wait_ge(s["f_ev"], NT * KD + 2)

            def project(b, par, i, block, outs, weights, free, done):
                this = pe.to_reg(b + 1)
                pe.wait_ge(s["tab_rdy"], 1)
                pe.wait_ge(s[free], this)
                pe.wait_ge(s[f"ld_ctx{par}"], 2 * 16 * NP + 16 * i + 16)

                def columns(outs, weights, j):
                    for dst, w_ in zip(outs, weights):
                        for k in range(KD):
                            last = pe.matmul(dst[:, ds(j * BC, BC)], w_(k), ctxb[:, par, k, ds(j * BC, BC)],
                                             start=(k == 0), stop=(k == KD - 1))
                    return last

                with pe.If_lt(pe.to_reg(block), NB - 1):
                    with pe.Fori(block, NB - 1) as j:
                        columns(outs, weights, j)
                columns(outs, weights, NB - 1).then_inc(s[done], 1)

            def project_txt(b, par, i, block):
                project(b, par, i, block, [bank[m] for m in range(KD)],
                        [lambda k, m=m: wsx[:, k, m * P:(m + 1) * P] for m in range(KD)], "t_ev", "t_mm")

            def project_cw(b, par, i, block):
                project(b, par, i, block, [bank[2 + m][0:S, :] for m in range(2)],
                        [lambda k, m=m: wcrep[:, m, k, :] for m in range(2)], "cw_ev", "ctx_x")

            def logits(unit, h):
                pe.wait_ge(s["t_done"], HALVES * unit + h + HALVES + 1)
                if h == 0:
                    pe.wait_ge(s["row_ev"], unit + 1)
                for k in range(KD):
                    n = 32 * (KD * (h % 2) + k)
                    last = pe.matmul(bank[4][n:n + 2, 0:HALF * S], wpair[:, k, 1 - h // 2:3 - h // 2],
                                     ht[h][:, k, :, :], start=(h < 2), stop=(h >= 2), skip_group_check=True)
                last.then_inc(s["rho_mm"], 1)

            def turn_logits(unit, u, par):
                pe.wait_ge(s["row_ev"], unit + 2)
                turned = bank[6 + par][0:S, 0:CP].rearrange("p (u h t) -> p u t h", h=HALVES, t=HALF)
                for t in range(HALF):
                    last = pe.matmul(turned[:, ds(u, 1), t, :].rearrange("p a h -> p (a h)"),
                                     lrow[:, t * S:(t + 1) * S], rowsel[:, :], start=True, stop=True)
                last.then_inc(s["rho_tp"], 1)

            def all_logits(b, par, between=None):
                first, ends = units_of(pe, b)
                this = pe.to_reg(b + 1)
                pe.wait_ge(s["tab_rdy"], 1)
                pe.wait_ge(s["e_in"], this)

                def one_unit(u, between=None):
                    for h in range(1, HALVES):
                        logits(ends + u, h)
                    if between is not None:
                        between()
                    turn_logits(ends + u, u, par)
                    logits(ends + u + 1, 0)

                one_unit(first, between)
                with pe.If_lt(pe.to_reg(first), NU - 1):
                    with pe.Fori(first + 1, NU) as u:
                        one_unit(u)

            pe.wait_ge(s["tab_rdy"], 1)
            pe.wait_ge(s["rho_zero"], 4)
            pe.wait_ge(s["c_done"], 1)
            pe.wait_ge(s["wp_rdy"], 2)
            pe.sem_inc(s["rho_tp"], NU + 1)
            pe.sem_inc(s["rho_mm"], HALVES * (NU + 1))
            block = block_of(pe, 0)
            project_txt(0, 0, 0, block)
            project_cw(0, 0, 0, block)
            logits(NU, 0)
            with pe.Fori(0, NP - 1) as i:
                for par in range(2):
                    b = 2 * i + par
                    block = block_of(pe, b + 1)
                    project_txt(b + 1, 1 - par, i + par, block)
                    all_logits(b, par, lambda: project_cw(b + 1, 1 - par, i + par, block))
            block = block_of(pe, B - 1)
            project_txt(B - 1, 1, NP - 1, block)
            all_logits(B - 2, 0, lambda: project_cw(B - 1, 1, NP - 1, block))
            all_logits(B - 1, 1)

            pe.wait_ge(s["x3_rdy"], B + 2)
            ln_tensor(pe, 3)
            ln_done(pe, 3)
            pe.wait_ge(s["fw_rdy"], 9)
            pe.sem_inc(s["hT_mm"], 2)
            pe.sem_inc(s["fo_mm"], 1)

            def up(b):
                for hf in range(2):
                    for m, (bk, used) in enumerate(((0, "fs_done"), (2, "h_used"))):
                        pe.wait_ge(s[used], 2 * b + hf + 1)
                        for k in range(KD):
                            last = pe.matmul(bank[bk + hf][0:S, :], xq[:, k, ds(b * S, S)],
                                             fq[:, m, k * FI + hf * G:k * FI + (hf + 1) * G],
                                             start=(k == 0), stop=(k == KD - 1))
                        last.then_inc(s["fg_mm" if m == 0 else "fu_mm"], 1)

            def down(b, par):
                pe.wait_ge(s["hq_rdy"], b + 1)
                pe.wait_ge(s["hT_ev"], b + 1)
                for c in range(FIC):
                    last = pe.transpose(bank[4 + c // 4][:, c % 4 * S:(c % 4 + 1) * S],
                                        h2[par][:, c * P:(c + 1) * P], ident[0:S, 0:S])
                last.then_inc(s["hT_mm"], 1)
                pe.wait_ge(s["hT_ev"], b + 2)
                pe.wait_ge(s["x4_rdy"], b + 1)
                for c in range(FIC):
                    last = pe.matmul(bank[6 + par][0:S, 0:D], hqT[:, c, :], fq[:, 2, c * D:(c + 1) * D],
                                     start=(c == 0), stop=(c == FIC - 1))
                last.then_inc(s["fo_mm"], 1)

            up(0)
            with pe.Fori(0, NP - 1) as i:
                for par in range(2):
                    up(2 * i + par + 1)
                    down(2 * i + par, par)
            up(B - 1)
            down(B - 2, 0)
            down(B - 1, 1)

        @block.scalar
        def _(act):
            act.wait_ge(s["const"], 1)
            act.activation(sm[:, 9:10], half[:, 0:1], ACT.Copy).then_inc(s["act_set"], 1)
            act.wait_ge(s["act_set"], 1)
            act.wait_ge(s["ld_wq"], 16)
            act.activation(wq_hi, wq, ACT.Copy).then_inc(s["wq_hi"], 1)
            ln_scalar(act, 0)
            act.sem_inc(s["q_ev"], 2)
            with act.Fori(0, NT) as t:
                for c in range(HC):
                    act.wait_ge(s["q_ready"], t * HC + c + 1)
                    act.activation(qT[:, c, ds(t * N4, N4)], bank[c % 2][:, 0:N4], ACT.Copy, scale=DH ** -0.5
                                   ).then_inc(s["q_ev"], 1)
            act.sem_inc(s["st_ev"], 2)

            def ctx_high(i, par):
                act.wait_ge(s[f"ld_ctx{par}"], 16 * i + 16)
                act.activation(ctx_hi[:, par, :, PC:CE], ctxb[:, par, :, PC:CE], ACT.Copy).then_inc(s["ctx_hi"], 1)

            def sims_rows(b, par):
                act.wait_ge(s["sim_mm"], (HC // 2) * (b + 1) + 2)
                act.wait_ge(s["sim_ev"], b + 1)
                act.activation(simT[:, :], bank[4 + par][:, 0:C], ACT.Copy).then_inc(s["st_ev"], 1)

            with act.Fori(0, NP - 1) as i:
                for par in range(2):
                    sims_rows(2 * i + par, par)
                    ctx_high(i + 1, par)
            sims_rows(B - 2, 0)
            ctx_high(NP, 0)
            sims_rows(B - 1, 1)
            ctx_high(NP, 1)
            act.wait_ge(s["max_sub"], 1)
            act.activation(sim[:, :, :, :], sim[:, :, :, :], ACT.Exp).then_inc(s["exp_done"], 1)
            act.sem_inc(s["tp_ev"], 2)

            def copy_heads(b):
                act.wait_ge(s["o_mm"], b + 1)
                for hf in range(2):
                    act.wait_ge(s["tp_done"], 2 * b + hf + 5)
                    act.activation(oT[:, 4 * hf:4 * hf + 4, :],
                                   bank[4 + hf][:, 0:4 * S].rearrange("p (c n) -> p c n", c=4), ACT.Copy
                                   ).then_inc(s["tp_ev"], 1)

            with act.Fori(0, NP - 1) as i:
                for par in range(2):
                    ctx_high(NP + i + 1, par)
                    copy_heads(2 * i + par)
            copy_heads(B - 2)
            copy_heads(B - 1)
            act.wait_ge(s["v_mm"], NJ * B)
            act.wait_ge(s["ld_gu"], 32)
            for m, wgt in enumerate((wg, wu)):
                act.activation(moe_hi[m], wgt, ACT.Copy).then_inc(s["moe_hi"], 1)
            ln_scalar(act, 1)
            act.wait_ge(s["r_mm"], 1)
            act.activation(rt[:, 0, :, :], bank[7][0:S, 0:B * E].rearrange("p (b e) -> p b e", b=B), ACT.Sigmoid
                           ).then_inc(s["sig_done"], 1)
            act.activation(sm[:, 9:10], half[:, 0:1], ACT.Silu).then_inc(s["act_set"], 1)
            act.wait_ge(s["act_set"], 2)
            with act.Fori(0, NT) as t:
                for c in range(FC):
                    w = min(P, FT - c * P)
                    act.wait_ge(s["g_mm"], t * FC + c + 1)
                    act.wait_ge(s["h_rdy"], t * FC + c + 1)
                    act.activation(sg[0:w, c % 2, :], bank[c % 2][0:w, 0:N4], ACT.Silu).then_inc(s["silu_done"], 1)
            act.wait_ge(s["ld_ff"], 48)
            for m in range(3):
                act.activation(fq[:, m, :], fw[m], ACT.Abs, accum_out=fsc[:, 0, m:m + 1]).then_inc(s["fw_mean"], 1)
            ln_scalar(act, 2)
            act.sem_inc(s["f_ev"], 2)
            act.sem_inc(s["x3_rdy"], 2)
            act.sem_inc(s["t_ev"], 1)
            act.sem_inc(s["cw_ev"], 1)
            act.sem_inc(s["row_ev"], NU)
            act.sem_inc(s["t_done"], HALVES * (NU + 1))
            act.wait_ge(s["ld_misc"], 16 * 11)
            with act.Fori(0, NT) as t:
                for m in range(KD):
                    act.wait_ge(s["f_mm"], t * KD + m + 1)
                    act.activation(featT[:, m, ds(t * N4, N4)], bank[m][:, 0:N4], ACT.Identity, bias=bcol[:, m:m + 1]
                                   ).then_inc(s["f_ev"], 1)

            def copy_blocks(block, copy, done):
                with act.If_lt(act.to_reg(block), NB - 1):
                    with act.Fori(block, NB - 1) as j:
                        copy(j)
                copy(NB - 1).then_inc(s[done], 1)

            def copy_txt(b, par, block):
                this = act.to_reg(b + 1)
                act.wait_ge(s["tab_rdy"], 1)
                act.wait_ge(s["t_mm"], this)
                copy_blocks(block, lambda j: act.activation(txtT[par][:, :, ds(j * BC + PAD - PC, BC)],
                                                            psum[:, 0:KD, ds(j * BC, BC)], ACT.Copy), "t_ev")

            def copy_cw(b, par, block):
                this = act.to_reg(b + 1)
                act.wait_ge(s["tab_rdy"], 1)
                act.wait_ge(s["ctx_x"], this)
                copy_blocks(block, lambda j: act.activation(cwb[par][:, :, ds(j * BC, BC)],
                                                            psum[0:S, 2:4, ds(j * BC, BC)], ACT.Copy), "cw_ev")

            def copy_rows(unit):
                act.wait_ge(s["rho_mm"], HALVES * unit + 2 * HALVES)
                act.wait_ge(s["rho_tp"], unit + 1)
                act.activation(lrow, bank[4][:, 0:HALF * S], ACT.Copy).then_inc(s["row_ev"], 1)

            def tanhs(first, ends):
                with act.Fori(first, NU) as u:
                    for h in range(HALVES):
                        q = HALVES * (ends + u) + h
                        act.wait_ge(s["z_rdy"], q + HALVES + 1)
                        act.wait_ge(s["rho_mm"], q + 1)
                        act.activation(ht[h], zt[h], ACT.Tanh).then_inc(s["t_done"], 1)
                        if h == 0:
                            copy_rows(ends + u - 1)

            def exps(b):
                act.wait_ge(s["e_in"], b + 3)
                act.activation(ee[:, :], rho[:, 1, :], ACT.Exp, bias=sm[:, 0:1], accum_out=sm[:, 1:2]
                               ).then_inc(s["e_done"], 1)

            def weights(b):
                act.wait_ge(s["w_in"], b + 1)
                for m in range(2):
                    last = act.activation(sm[:, 5 + m:6 + m], sm[:, 2 + m:3 + m], ACT.Tanh,
                                          bias=bc[:, m:m + 1], scale=sm[:, 4:5])
                last.then_inc(s["w_done"], 1)
                ready = act.to_reg(b + 1)
                act.wait_ge(s["tab_rdy"], 1)
                act.wait_ge(s["w_done"], ready)
                act.activation(sm[:, 7:8], rstd[:, ds(b, 1)], ACT.Identity, scale=sm[:, 5:6], bias=ones[0:S, 0:1])
                act.activation(sm[:, 8:9], shift[:, ds(b, 1)], ACT.Identity, scale=sm[:, 5:6], bias=sm[:, 6:7]
                               ).then_inc(s["ab_done"], 1)
                act.wait_ge(s["tab_rdy"], 1)
                act.wait_ge(s["ab_done"], ready)
                act.activation(row(x, b), row(x, b), ACT.Identity, scale=sm[:, 7:8], bias=sm[:, 8:9]
                               ).then_inc(s["x3_rdy"], 1)

            act.activation(sm[:, 9:10], half[:, 0:1], ACT.Exp).then_inc(s["act_set"], 1)
            act.wait_ge(s["rho_zero"], 4)
            for b in range(2):
                block = block_of(act, b)
                units = units_of(act, b)
                copy_txt(b, b, block)
                copy_cw(b, b, block)
                tanhs(*units)
            with act.Fori(0, NP - 1) as i:
                for par in range(2):
                    b = 2 * i + par
                    block = block_of(act, b + 2)
                    units = units_of(act, b + 2)
                    exps(b)
                    copy_txt(b + 2, par, block)
                    weights(b)
                    copy_cw(b + 2, par, block)
                    tanhs(*units)
            copy_rows(units_to(act, B - 1) + NU - 1)
            act.sem_inc(s["t_done"], 1)
            for b in (B - 2, B - 1):
                exps(b)
                weights(b)
            ln_scalar(act, 3)
            act.wait_ge(s["al_rdy"], 2)
            act.sem_inc(s["fs_done"], 2)
            act.sem_inc(s["hT_ev"], 1)

            def gate(b, par):
                for hf in range(2):
                    this = act.to_reg(2 * b + hf + 1)
                    act.wait_ge(s["al_rdy"], 2)
                    act.wait_ge(s["fg_mm"], this)
                    act.wait_ge(s["h_used"], this)
                    act.activation(g2[par][:, hf * G:(hf + 1) * G], bank[hf][0:S, :], ACT.Silu,
                                   scale=alpha[:, 0, ds(b, 1)]).then_inc(s["fs_done"], 1)

            def copy_h(b):
                act.wait_ge(s["hT_mm"], b + 3)
                act.wait_ge(s["fo_mm"], b + 1)
                act.activation(hqT.rearrange("p (a c) n -> p a (c n)", a=2), psum[:, 4:6, 0:FIC // 2 * S], ACT.Identity,
                               bias=unround[:, 0:1]).then_inc(s["hT_ev"], 1)

            gate(0, 0)
            with act.Fori(0, NP - 1) as i:
                for par in range(2):
                    gate(2 * i + par + 1, 1 - par)
                    copy_h(2 * i + par)
            gate(B - 1, 1)
            copy_h(B - 2)
            copy_h(B - 1)

        @block.vector
        def _(dve):
            ln_vector(dve, 0)
            link = chain(dve, s["tab_chain"])
            dve.wait_ge(s["ld_mrow"], 16)
            dve.wait_ge(s["const"], 1)
            link(dve.tensor_copy(kdown[:, :], kdowni[:, :]))
            link(dve.tensor_scalar(mnz[:, :], mrow[:, :], 0.0, None, ALU.not_equal))
            link(dve.tensor_reduce(kflag[:, :], mnz[:, :].rearrange("p (u t) -> p u t", t=UNIT), AX.X, ALU.max))
            link(dve.tensor_tensor(kflag[:, :], kflag[:, :], kdown[:, :], ALU.mult))
            link(dve.tensor_reduce(kcount[:, 0:1], kflag[:, :], AX.X, ALU.max))
            link(dve.tensor_scalar(mnz[:, :], mrow[:, :], 0.0, None, ALU.is_gt))
            link(dve.tensor_reduce(kcount[:, 1:2], mnz[:, :], AX.X, ALU.max))
            dve.tensor_scalar(kcount[:, 0:1], kcount[:, 0:1], 1.0, None, ALU.max).then_inc(s["cnt_in"], 1)
            dve.tensor_copy(down8[:, :], down8i[:, :]).then_inc(s["d8"], 1)
            dve.wait_ge(s["ld_wkv"], 16)
            dve.tensor_copy(wk_hi, wkv[:, :, 0:INNER]).then_inc(s["wkv_hi"], 1)
            for n in range(2):
                dve.wait_ge(s[f"ld_ctx{n}"], 16)
                dve.tensor_copy(ctx_hi[:, n, :, PC:CE], ctxb[:, n, :, PC:CE]).then_inc(s["ctx_hi"], 1)
            dve.tensor_copy(wv_hi, wkv[:, :, INNER:]).then_inc(s["wkv_hi"], 1)
            dve.wait_ge(s["ld_misc"], 16 * 11)
            dve.tensor_copy(wcrep[:, :, :, :], wc[:, :, :].unsqueeze(3).broadcast_to([P, 2, KD, S])
                            ).then_inc(s["c_done"], 1)
            dve.memset(wpair[:, :, :], 0.0).then_inc(s["wp_rdy"], 1)
            dve.wait_ge(s["wp_rdy"], 1)
            dve.tensor_copy(wpair[:, :, 1], wvec[:, :]).then_inc(s["wp_rdy"], 1)
            dve.memset(sim[:, :, NJ - 1, :], NEG).then_inc(s["s_chain"], 1)
            dve.wait_ge(s["s_chain"], 1)
            for n in (4, 5):
                dve.memset(bank[n][:, 0:C], 0.0).then_inc(s["sim_zero"], 1)
            dve.wait_ge(s["cnt_mm"], 1)
            link(dve.tensor_copy(rowf[:, 0, :], bank[7][0:1, 0:B]))
            link(dve.tensor_copy(rowf[:, 3, :], bank[7][0:1, B:2 * B]))
            link(dve.tensor_scalar(rowf[:, 2, :], rowf[:, 0, :], -1.0, float(NU), ALU.mult, ALU.add))
            link(dve.tensor_copy(table[:, 0, :], rowf[:, 2, :]))
            for j in range(1, NB):
                link(dve.tensor_scalar(rowf[:, 4, :], rowf[:, 2, :], float(UNIT), float(j * BC + PAD - PC), ALU.mult, ALU.is_ge))
                link(dve.tensor_tensor(rowf[:, 4, :], rowf[:, 4, :], rowf[:, 3, :], ALU.mult))
                link(dve.tensor_copy(rowf[:, 5, :], rowf[:, 4, :]) if j == 1 else
                     dve.tensor_tensor(rowf[:, 5, :], rowf[:, 4, :], rowf[:, 5, :], ALU.add))
            link(dve.tensor_copy(table[:, 1, :], rowf[:, 5, :]))
            link(dve.tensor_tensor_scan(rowf[:, 1, :], ones[0:1, 0:B], rowf[:, 0, :], 0.0, ALU.mult, ALU.add))
            dve.tensor_copy(table[:, 2, :], rowf[:, 1, :]).then_inc(s["tab_rdy"], 1)
            dve.sem_inc(s["prod_rdy"], 2)
            dve.sem_inc(s["sim_ev"], 1)
            dve.wait_ge(s["q_ev"], NT * HC + 2)

            def products(b, m):
                g = (HC // 2) * b + m
                k2 = psum[:, 2 * (m % 2):2 * (m % 2) + 2, PC:CE]
                dve.wait_ge(s["k_mm"], g + 1)
                dve.wait_ge(s["sim_mm"], g + 1)
                q2 = qT[:, 2 * m:2 * m + 2, ds(b * S, S)]
                dve.tensor_tensor(prod[m % 2][:, :, 0:JF * S].rearrange("p u (j s) -> p u j s", s=S),
                                  k2[:, :, 0:JF * S].rearrange("p u (j s) -> p u j s", s=S),
                                  q2.unsqueeze(2).broadcast_to([P, 2, JF, S]), ALU.mult)
                dve.tensor_tensor(prod[m % 2][:, :, JF * S:C], k2[:, :, JF * S:C],
                                  qT[:, 2 * m:2 * m + 2, ds(b * S, C - JF * S)], ALU.mult).then_inc(s["prod_rdy"], 1)

            def copy_sims(b):
                dve.wait_ge(s["sim_tp"], b + 1)
                turned = bank[6].rearrange("p (j q r) -> p j q r", j=NJ, q=4)
                rows = row(sim.rearrange("p b j h -> p b (j h)"), b).rearrange("p (j h) -> p j h", j=NJ)
                for n, j0, j1 in ((S, 0, JF), (JR[-1], JF, NJ)):
                    for r in range(2):
                        last = dve.tensor_copy(rows[0:n, j0:j1, 8 * r:8 * r + 8].rearrange("p j (q h) -> p j q h", h=2),
                                               turned[0:n, j0:j1, :, 2 * r:2 * r + 2])
                last.then_inc(s["sim_ev"], 1)

            for m in range(HC // 2):
                products(0, m)
            with dve.Fori(1, B) as b:
                for m in range(HC // 2):
                    products(b, m)
                copy_sims(b - 1)
            copy_sims(B - 1)
            link = chain(dve, s["s_chain"], 1)
            dve.wait_ge(s["sim_ev"], B + 1)
            link(dve.tensor_reduce(smax[:, :, :], sim[:, :, :, :].rearrange("p b j h -> p b h j"), AX.X, ALU.max))
            dve.tensor_tensor(sim[:, :, :, :], sim[:, :, :, :], smax[:, :, :].unsqueeze(2).broadcast_to([S, B, NJ, H]),
                              ALU.subtract).then_inc(s["max_sub"], 1)
            dve.wait_ge(s["exp_done"], 1)
            link(dve.tensor_reduce(ssum[:, :, :], sim[:, :, :, :].rearrange("p b j h -> p b h j"), AX.X, ALU.add))
            link(dve.reciprocal(ssum[:, :, :], ssum[:, :, :]))
            link(dve.tensor_tensor(sim[:, :, :, :], sim[:, :, :, :], ssum[:, :, :].unsqueeze(2).broadcast_to([S, B, NJ, H]),
                                   ALU.mult))
            dve.sem_inc(s["v_used"], 2)
            dve.sem_inc(s["x1_rdy"], 2)

            def weigh_v(b, par):
                for j in range(NJ):
                    n = JR[j]
                    dve.wait_ge(s["v_mm"], NJ * b + j + 1)
                    if j == 0:
                        dve.wait_ge(s["tp_done"], 2 * b + 2)
                        dst = pacc[par]
                    else:
                        dve.wait_ge(s["pv_done"], (NJ - 1) * b + j)
                        dst = ptmp[(par * (NJ - 1) + j - 1) % 2]
                    v = psum[0:n, 2 * (j % 2):2 * (j % 2) + 2, :].rearrange("p w (h d) -> p (w h) d", d=DH)
                    p = sim[0:n, ds(b, 1), j, :].rearrange("p a h -> p (a h)").unsqueeze(2).broadcast_to([n, H, DH])
                    dve.tensor_tensor(dst[0:n, :].rearrange("p (h d) -> p h d", h=H), v, p, ALU.mult
                                      ).then_inc(s["v_used"], 1)

            def residual1(b, par):
                dve.wait_ge(s["o_mm"], b + 2)
                dve.tensor_tensor(row(x, b), bank[6 + par][0:S, 0:D], row(x, b), ALU.add).then_inc(s["x1_rdy"], 1)
                dve.wait_ge(s["x1_rdy"], b + 3)
                ln_stats(dve, 1, b)

            dve.wait_ge(s["bo_rdy"], 1)
            weigh_v(0, 0)
            with dve.Fori(0, NP - 1) as i:
                for par in range(2):
                    weigh_v(2 * i + par + 1, 1 - par)
                    residual1(2 * i + par, par)
            weigh_v(B - 1, 1)
            residual1(B - 2, 0)
            residual1(B - 1, 1)
            dve.wait_ge(s["x1_rdy"], B + 2)
            ln_vector(dve, 1)
            link = chain(dve, s["r_chain"])
            dve.wait_ge(s["sig_done"], 1)
            dve.wait_ge(s["d8"], 1)

            def each(t):
                return t.unsqueeze(2).broadcast_to([S, B, E])
            score, biased, hit, one, two, w = [rt[:, n, :, :] for n in range(6)]
            best, order, total = [rsm[:, n, :] for n in range(3)]
            link(dve.tensor_tensor(biased, score, ebias[:, :].unsqueeze(1).broadcast_to([S, B, E]), ALU.add))
            for n, pick in enumerate((one, two)):
                link(dve.tensor_reduce(best, biased, AX.X, ALU.max))
                link(dve.tensor_tensor(hit, biased, each(best), ALU.is_equal))
                link(dve.tensor_tensor(hit, hit, down8[:, :].unsqueeze(1).broadcast_to([S, B, E]), ALU.mult))
                link(dve.tensor_reduce(order, hit, AX.X, ALU.max))
                link(dve.tensor_tensor(pick, hit, each(order), ALU.is_equal))
                if n == 0:
                    link(dve.scalar_tensor_tensor(biased, pick, NEG, biased, ALU.mult, ALU.add))
            link(dve.tensor_tensor(w, one, two, ALU.add))
            link(dve.tensor_tensor(w, w, score, ALU.mult))
            link(dve.tensor_reduce(total, w, AX.X, ALU.add))
            link(dve.tensor_scalar(total, total, 1e-20, None, ALU.add))
            link(dve.reciprocal(total, total))
            link(dve.tensor_tensor(gate_w[:, :, :], w, each(total), ALU.mult))
            dve.sem_inc(s["h_rdy"], 2)
            dve.sem_inc(s["d_used"], 4)
            with dve.Fori(0, NT) as t:
                for c in range(FC):
                    w_ = min(P, FT - c * P)
                    dve.wait_ge(s["silu_done"], t * FC + c + 1)
                    dve.tensor_tensor(hT[0:w_, c, :], sg[0:w_, c % 2, :], bank[2 + c % 2][0:w_, 0:N4], ALU.mult
                                      ).then_inc(s["h_rdy"], 1)
                for lb in range(TB):
                    b = t * TB + lb
                    for n, e in enumerate([E] + list(range(E))):
                        d = t * TB * (E + 1) + lb * (E + 1) + n
                        dve.wait_ge(s["d_mm"], d + 1)
                        dve.wait_ge(s["d_used"], d + 4)
                        pd = bank[4 + (lb * (E + 1) + n) % 4][0:S, 0:D]
                        if e == E:
                            dve.tensor_tensor(row(x, b), pd, row(x, b), ALU.add).then_inc(s["d_used"], 1)
                        else:
                            dve.scalar_tensor_tensor(row(x, b), pd, gate_w[:, ds(b, 1), e], row(x, b),
                                                     ALU.mult, ALU.add).then_inc(s["d_used"], 1)
                    dve.wait_ge(s["d_used"], t * TB * (E + 1) + (lb + 1) * (E + 1) + 4)
                    ln_stats(dve, 2, b)
            dve.wait_ge(s["d_used"], NT * TB * (E + 1) + 4)
            ln_vector(dve, 2)
            link = chain(dve, s["fw_chain"])
            dve.wait_ge(s["fw_bc"], 1)
            link(dve.tensor_scalar(fsc[:, 1, :], bank[7][:, 0:3], 1.0 / (D * FI), 1e-5, ALU.mult, ALU.max))
            dve.reciprocal(fsc[:, 2, :], fsc[:, 1, :]).then_inc(s["fw_scale"], 1)
            ln_done(dve, 2)
            for par in range(2):
                dve.memset(bank[6 + par][:, 0:CP], 0.0).then_inc(s["rho_zero"], 1)
            link(dve.scalar_tensor_tensor(shift[:, :], meanvar[:, :, 0], -1.0, rstd[:, :], ALU.mult, ALU.mult))
            dve.memset(bank[4][:, 0:HALF * S], 0.0).then_inc(s["rho_zero"], 1)
            dve.sem_inc(s["e_in"], 2)
            dve.sem_inc(s["z_rdy"], HALVES * (NU + 1))

            def sums(b, par, first, ends):
                this = dve.to_reg(b + 2)
                dve.wait_ge(s["tab_rdy"], 1)
                dve.wait_ge(s["t_ev"], this)
                with dve.Fori(first, NU) as u:
                    for h in range(HALVES):
                        q = HALVES * (ends + u) + h
                        dve.wait_ge(s["t_done"], q + 1)
                        dve.tensor_tensor(*sum_of(b, par, u, h), ALU.add).then_inc(s["z_rdy"], 1)

            NS = 4

            def mask_logits(b, par, i, ahead=None):
                turned = dve.to_reg(units_to(dve, b) + NU + 1)
                link = chain(dve, s["a_chain"], NS * b)
                dve.wait_ge(s[f"ld_mask{par}"], 16 * i + 16)
                link(dve.tensor_scalar(rho[:, 0, :], maskb[:, par, :], -1.0, 1.0, ALU.mult, ALU.add))
                units = None if ahead is None else units_of(dve, ahead)
                dve.wait_ge(s["tab_rdy"], 1)
                dve.wait_ge(s["rho_tp"], turned)
                link(dve.scalar_tensor_tensor(rho[:, 1, :], rho[:, 0, :], NEG, bank[6 + par][0:S, PAD:CP],
                                              ALU.mult, ALU.add))
                dve.tensor_reduce(sm[:, 0:1], rho[:, 1, :], AX.X, ALU.max, negate=True).then_inc(s["e_in"], 1)
                return units

            def sum_ctx(b, par):
                link = chain(dve, s["a_chain"], NS * b + 2)
                dve.wait_ge(s["e_done"], b + 1)
                dve.wait_ge(s["cw_ev"], b + 2)
                link(dve.tensor_tensor_reduce(out=rho[:, 2, :], in0=ee[:, :], in1=cwb[par][:, 0, PC:CE], scale=1.0,
                                              scalar=0.0, op0=ALU.mult, op1=ALU.add, accum_out=sm[:, 2:3]))
                link(dve.tensor_tensor_reduce(out=rho[:, 2, :], in0=ee[:, :], in1=cwb[par][:, 1, PC:CE], scale=1.0,
                                              scalar=0.0, op0=ALU.mult, op1=ALU.add, accum_out=sm[:, 3:4]))
                dve.reciprocal(sm[:, 4:5], sm[:, 1:2]).then_inc(s["w_in"], 1)

            def last_stats(b):
                dve.wait_ge(s["x3_rdy"], b + 3)
                ln_stats(dve, 3, b)

            dve.wait_ge(s["rho_zero"], 4)
            dve.wait_ge(s["f_ev"], NT * KD + 2)
            sums(0, 0, *units_of(dve, 0))
            sums(1, 1, *units_of(dve, 1))
            units = mask_logits(0, 0, 0, 2)
            sum_ctx(0, 0)
            sums(2, 0, *units)
            with dve.Fori(0, NP - 2) as i:
                for d in (1, 2):
                    b = 2 * i + d
                    units = mask_logits(b, d % 2, i + d // 2, b + 2)
                    last_stats(b - 1)
                    sum_ctx(b, d % 2)
                    sums(b + 2, d % 2, *units)
            units = mask_logits(B - 3, 1, NP - 2, B - 1)
            last_stats(B - 4)
            sum_ctx(B - 3, 1)
            sums(B - 1, 1, *units)
            for b in (B - 2, B - 1):
                mask_logits(b, b % 2, NP - 1)
                last_stats(b - 1)
                sum_ctx(b, b % 2)
            last_stats(B - 1)
            dve.wait_ge(s["x3_rdy"], B + 2)
            ln_vector(dve, 3)
            for m in range(2):
                dve.tensor_scalar(alpha[:, m, :], amax[:, 1, :], fsc[0:S, 1, m:m + 1], None, ALU.mult).then_inc(s["al_rdy"], 1)
            dve.wait_ge(s["al_rdy"], 2)
            dve.sem_inc(s["h_used"], 2)
            dve.sem_inc(s["x4_rdy"], 2)
            NH = 5

            def hidden(b, par):
                link = chain(dve, s["fh_chain"], NH * b)
                m = hm[:, par, :]
                dve.wait_ge(s["hT_mm"], b + 1)
                for hf in range(2):
                    dve.wait_ge(s["fu_mm"], 2 * b + hf + 1)
                    dve.wait_ge(s["fs_done"], 2 * b + hf + 3)
                    dve.scalar_tensor_tensor(h2[par][:, hf * G:(hf + 1) * G], bank[2 + hf][0:S, :], alpha[:, 1, ds(b, 1)],
                                             g2[par][:, hf * G:(hf + 1) * G], ALU.mult, ALU.mult).then_inc(s["h_used"], 1)
                dve.wait_ge(s["h_used"], 2 * b + 4)
                link(dve.tensor_reduce(m[:, 0:1], h2[par], AX.X, ALU.max, apply_absolute_value=True))
                link(dve.tensor_scalar(m[:, 0:1], m[:, 0:1], 1e-5, None, ALU.max))
                link(dve.reciprocal(m[:, 1:2], m[:, 0:1]))
                dve.tensor_scalar(m[:, 2:3], m[:, 0:1], 1.0 / 127.0, fsc[0:S, 1, 2:3], ALU.mult, ALU.mult)
                link(dve.tensor_scalar(m[:, 1:2], m[:, 1:2], 127.0, None, ALU.mult))
                link(dve.tensor_scalar(h2[par], h2[par], m[:, 1:2], 127.0, ALU.mult, ALU.min))
                dve.tensor_scalar(h2[par], h2[par], -128.0, ROUND, ALU.max, ALU.add).then_inc(s["hq_rdy"], 1)

            def residual4(b, par):
                dve.wait_ge(s["fo_mm"], b + 2)
                dve.scalar_tensor_tensor(row(x, b), bank[6 + par][0:S, 0:D], hm[:, par, 2:3], row(x, b),
                                         ALU.mult, ALU.add).then_inc(s["x4_rdy"], 1)

            hidden(0, 0)
            with dve.Fori(0, NP - 1) as i:
                for par in range(2):
                    hidden(2 * i + par + 1, 1 - par)
                    residual4(2 * i + par, par)
            hidden(B - 1, 1)
            residual4(B - 2, 0)
            residual4(B - 1, 1)


def kernel(**inputs):
    import numpy as _np
    import concourse.bacc as _bacc
    from concourse import mybir as _mybir
    from concourse.bass_utils import run_bass_kernel_spmd as _run

    v = {n: _np.asarray(a) for n, a in inputs.items()}

    def experts(routed, shared):
        e, d, f = routed.shape
        return _np.concatenate([routed.transpose(1, 0, 2).reshape(d, e * f), shared], axis=1)

    laid = {
        "x": v["x"],
        "ctx_t": v["ctx_1024"].transpose(0, 2, 1),
        "mask": v["mask_BxS2_ik0"],
        "wq": v["L0_xattn_Wq"], "wkv": v["L0_xattn_Wkv"], "wout": v["L0_xattn_Wout"], "bout": v["L0_xattn_bout"],
        "wr": v["L0_ffn_W_gate_router"], "ebias": v["L0_ffn_expert_bias"],
        "wg": experts(v["L0_ffn_Wg"], v["L0_ffn_Wg_s"]),
        "wu": experts(v["L0_ffn_Wu"], v["L0_ffn_Wu_s"]),
        "wd": _np.concatenate([v["L0_ffn_Wd"].reshape(-1, v["L0_ffn_Wd"].shape[2]), v["L0_ffn_Wd_s"]], axis=0),
        "ws": v["L1_xattn_Ws"], "w": v["L1_xattn_W"], "wvec": v["L1_xattn_w"], "b": v["L1_xattn_b"],
        "wcw": v["L1_xattn_Wcw"], "bcw": v["L1_xattn_bcw"], "wcb": v["L1_xattn_Wcb"], "bcb": v["L1_xattn_bcb"],
        "fg": v["L1_ffn_w_gate"].T, "fu": v["L1_ffn_w_up"].T, "fd": v["L1_ffn_w_down"].T,
    }
    nc = _bacc.Bacc("TRN2", target_bir_lowering=False, num_devices=1)
    arrays, args = {}, []
    for name, a in laid.items():
        a = _np.ascontiguousarray(a)
        arrays[f"in_{name}_dram"] = a
        args.append(nc.dram_tensor(f"in_{name}_dram", a.shape, _mybir.dt.from_np(a.dtype), kind="ExternalInput").ap())
    shape, dtype = v["x"].shape, v["x"].dtype
    args.append(nc.dram_tensor("out_0_dram", shape, _mybir.dt.from_np(dtype), kind="ExternalOutput").ap())
    bass_xattn_moe_additive_attn_bitlinear_ffn_kernel(nc, *args)
    r = _run(nc, [arrays], core_ids=[0])
    return r.results[0]["out_0_dram"]
```
